# Optimizing a Trainium2 kernel written in Bass

```python
import numpy as np
import jax
import jax.numpy as jnp

def _softmax(x, axis=-1):
    return jax.nn.softmax(x, axis=axis)

def _gelu(x):
    return jax.nn.gelu(x, approximate=True)

def _silu(x):
    return jax.nn.silu(x)

def _sigmoid(x):
    return jax.nn.sigmoid(x)

def _layernorm(x, axis=-1, eps=1e-05):
    m = jnp.mean(x, axis=axis, keepdims=True)
    v = jnp.var(x, axis=axis, keepdims=True)
    return (x - m) / jnp.sqrt(v + eps)

def _scatter_add(tgt, idx, src, axis=0):
    return tgt.at[idx].add(src)

def _segment_sum(src, seg, n):
    return jax.ops.segment_sum(src, seg, n)
kernel_name = 'mk_seq_postln_d2_jaxref_r8_47194b'

def setup_inputs(seed: int=0):
    np.random.seed(seed)
    _w = jnp.asarray

    def _L0_attn_setup():
        import jax, jax.numpy as jnp
        import numpy as np
        B, S, HID = (2, 256, 256)
        H = 16
        NOPE, ROPE, V_DIM, KV_RANK = (128, 64, 128, 64)
        Q_DIM = NOPE + ROPE
        EPS = 1e-06
        NEG = -1000000000.0

        def _rmsnorm(x, w):
            xf = x.astype(jnp.float32)
            var = jnp.mean(xf * xf, axis=-1, keepdims=True)
            return w * (xf * jax.lax.rsqrt(var + EPS)).astype(x.dtype)
        key = jax.random.key(seed)
        ks = jax.random.split(key, 5)
        return {'hidden_states': jax.random.normal(ks[0], (B, S, HID), jnp.float32), 'q_proj_w': jax.random.normal(ks[1], (H * Q_DIM, HID), jnp.float32) * HID ** (-0.5), 'kv_a_proj_w': jax.random.normal(ks[2], (KV_RANK + ROPE, HID), jnp.float32) * HID ** (-0.5), 'kv_a_ln_w': jnp.ones((KV_RANK,), jnp.float32), 'kv_b_proj_w': jax.random.normal(ks[3], (H * (NOPE + V_DIM), KV_RANK), jnp.float32) * KV_RANK ** (-0.5), 'o_proj_w': jax.random.normal(ks[4], (HID, H * V_DIM), jnp.float32) * (H * V_DIM) ** (-0.5)}
    _L0_attn_in = _L0_attn_setup()

    def _L0_ffn_setup():
        import jax, jax.numpy as jnp
        import numpy as np
        TOP_K = 8
        CAPACITY = 128
        key = jax.random.key(seed)
        k1, k2, k3, k4 = jax.random.split(key, 4)
        B, S, H, E, I = (2, 128, 256, 64, 96)
        hidden_states = jax.random.normal(k1, (B, S, H), dtype=jnp.float32)
        router_weight = jax.random.normal(k2, (E, H), dtype=jnp.float32) * 0.02
        gate_up_proj = jax.random.normal(k3, (E, H, 2 * I), dtype=jnp.float32) * 0.02
        down_proj = jax.random.normal(k4, (E, I, H), dtype=jnp.float32) * 0.02
        return {'hidden_states': hidden_states, 'router_weight': router_weight, 'gate_up_proj': gate_up_proj, 'down_proj': down_proj}
    _L0_ffn_in = _L0_ffn_setup()

    def _L1_attn_setup():
        import jax, jax.numpy as jnp
        import numpy as np
        B, S, H, R, L = (4, 256, 256, 256, 256)
        W_SCALE = 0.02

        def _reference_tuple_inner(x, w_f, w_i, w_v, w_q, w_ro, w_aux, w_up, w_gate, w_down, init_state):
            b, s, _ = x.shape
            f = jnp.tanh(jnp.einsum('bsh,hr->bsr', x, w_f))
            g = jax.nn.sigmoid(jnp.einsum('bsh,hr->bsr', x, w_i)) * jax.nn.silu(jnp.einsum('bsh,hr->bsr', x, w_v))

            def step(state, fg):
                ft, gt = fg
                state = ft * state + gt
                return (state, state)
            s0 = jnp.broadcast_to(init_state, (b, init_state.shape[0]))
            _, states = jax.lax.scan(step, s0, (jnp.swapaxes(f, 0, 1), jnp.swapaxes(g, 0, 1)))
            states = jnp.swapaxes(states, 0, 1)
            q = jnp.einsum('bsh,hr->bsr', x, w_q)
            readout = jax.nn.silu(q * states)
            local = jnp.einsum('bsl,lh->bsh', jnp.einsum('bsh,hl->bsl', x, w_up) * jax.nn.silu(jnp.einsum('bsh,hl->bsl', x, w_gate)), w_down)
            out = jnp.einsum('bsr,rh->bsh', readout, w_ro) + local
            aux_pred = jnp.einsum('bsr,rh->bsh', jax.nn.silu(states[:, :-1]), w_aux)
            aux_target = jax.lax.stop_gradient(x[:, 1:])
            aux_loss = jnp.mean((aux_pred - aux_target) ** 2)
            return (out, aux_loss)
        key = jax.random.key(seed)
        ks = jax.random.split(key, 11)
        w = lambda k, shp: jax.random.normal(k, shp, jnp.float32) * W_SCALE
        return {'x': jax.random.normal(ks[0], (B, S, H), jnp.float32), 'w_f': w(ks[1], (H, R)), 'w_i': w(ks[2], (H, R)), 'w_v': w(ks[3], (H, R)), 'w_q': w(ks[4], (H, R)), 'w_ro': w(ks[5], (R, H)), 'w_aux': w(ks[6], (R, H)), 'w_up': w(ks[7], (H, L)), 'w_gate': w(ks[8], (H, L)), 'w_down': w(ks[9], (L, H)), 'init_state': jnp.zeros((R,), jnp.float32)}
    _L1_attn_in = _L1_attn_setup()

    def _L1_ffn_setup():
        import jax, jax.numpy as jnp
        import numpy as np
        B, S, H = (4, 256, 256)
        INTER = 512
        E = 8
        TOPK = 2
        SHARED_I = INTER * 2

        def moe_forward(hidden_states, router_w, w1, w2, w_gate, w_up, w_down):
            b, s, h = hidden_states.shape
            x = hidden_states.reshape(-1, h)
            T = x.shape[0]
            logits = x @ router_w
            top_logits, top_indices = jax.lax.top_k(logits, TOPK)
            scores = jax.nn.softmax(top_logits, axis=-1)
            flat_idx = top_indices.reshape(-1)
            sorted_pos = jnp.argsort(flat_idx, stable=True)
            permuted = x[sorted_pos // TOPK]
            expert_ids = flat_idx[sorted_pos]
            out = jnp.zeros((T * TOPK, h), x.dtype)
            for e in range(E):
                mask = (expert_ids == e)[:, None]
                f1 = permuted * mask @ w1[e]
                g, u = jnp.split(f1, 2, axis=-1)
                act = jax.nn.silu(g) * u
                out = out + jnp.where(mask, act @ w2[e], 0.0)
            unperm = jnp.zeros_like(out).at[sorted_pos].set(out)
            combined = (unperm.reshape(T, TOPK, h) * scores[..., None]).sum(axis=1)
            shared = jax.nn.silu(x @ w_gate) * (x @ w_up) @ w_down
            return (combined + shared).reshape(b, s, h)
        key = jax.random.key(seed)
        ks = jax.random.split(key, 7)
        s = 0.02
        return {'hidden_states': jax.random.normal(ks[0], (B, S, H), jnp.float32), 'router_w': jax.random.normal(ks[1], (H, E), jnp.float32) * s, 'w1': jax.random.normal(ks[2], (E, H, 2 * INTER), jnp.float32) * s, 'w2': jax.random.normal(ks[3], (E, INTER, H), jnp.float32) * s, 'w_gate': jax.random.normal(ks[4], (H, SHARED_I), jnp.float32) * s, 'w_up': jax.random.normal(ks[5], (H, SHARED_I), jnp.float32) * s, 'w_down': jax.random.normal(ks[6], (SHARED_I, H), jnp.float32) * s}
    _L1_ffn_in = _L1_ffn_setup()
    _d = {'L0_attn_hidden_states': _L0_attn_in['hidden_states'], 'L0_attn_q_proj_w': _L0_attn_in['q_proj_w'], 'L0_attn_kv_a_proj_w': _L0_attn_in['kv_a_proj_w'], 'L0_attn_kv_a_ln_w': _L0_attn_in['kv_a_ln_w'], 'L0_attn_kv_b_proj_w': _L0_attn_in['kv_b_proj_w'], 'L0_attn_o_proj_w': _L0_attn_in['o_proj_w'], 'L0_ffn_router_weight': _L0_ffn_in['router_weight'], 'L0_ffn_gate_up_proj': _L0_ffn_in['gate_up_proj'], 'L0_ffn_down_proj': _L0_ffn_in['down_proj'], 'L1_attn_w_f': _L1_attn_in['w_f'], 'L1_attn_w_i': _L1_attn_in['w_i'], 'L1_attn_w_v': _L1_attn_in['w_v'], 'L1_attn_w_q': _L1_attn_in['w_q'], 'L1_attn_w_ro': _L1_attn_in['w_ro'], 'L1_attn_w_aux': _L1_attn_in['w_aux'], 'L1_attn_w_up': _L1_attn_in['w_up'], 'L1_attn_w_gate': _L1_attn_in['w_gate'], 'L1_attn_w_down': _L1_attn_in['w_down'], 'L1_attn_init_state': _L1_attn_in['init_state'], 'L1_ffn_router_w': _L1_ffn_in['router_w'], 'L1_ffn_w1': _L1_ffn_in['w1'], 'L1_ffn_w2': _L1_ffn_in['w2'], 'L1_ffn_w_gate': _L1_ffn_in['w_gate'], 'L1_ffn_w_up': _L1_ffn_in['w_up'], 'L1_ffn_w_down': _L1_ffn_in['w_down']}
    _x0 = _d['L0_attn_hidden_states']
    _d['L0_attn_hidden_states'] = jax.random.normal(jax.random.fold_in(jax.random.key(seed), 1), (1, 1024, 256), dtype=_x0.dtype)
    del _x0
    return _d

def reference(L0_attn_hidden_states, L0_attn_q_proj_w, L0_attn_kv_a_proj_w, L0_attn_kv_a_ln_w, L0_attn_kv_b_proj_w, L0_attn_o_proj_w, L0_ffn_router_weight, L0_ffn_gate_up_proj, L0_ffn_down_proj, L1_attn_w_f, L1_attn_w_i, L1_attn_w_v, L1_attn_w_q, L1_attn_w_ro, L1_attn_w_aux, L1_attn_w_up, L1_attn_w_gate, L1_attn_w_down, L1_attn_init_state, L1_ffn_router_w, L1_ffn_w1, L1_ffn_w2, L1_ffn_w_gate, L1_ffn_w_up, L1_ffn_w_down):

    def _L0_attn_ref(hidden_states, q_proj_w, kv_a_proj_w, kv_a_ln_w, kv_b_proj_w, o_proj_w):
        import jax, jax.numpy as jnp
        import numpy as np
        B, S, HID = (2, 256, 256)
        H = 16
        NOPE, ROPE, V_DIM, KV_RANK = (128, 64, 128, 64)
        Q_DIM = NOPE + ROPE
        EPS = 1e-06
        NEG = -1000000000.0

        def _rmsnorm(x, w):
            xf = x.astype(jnp.float32)
            var = jnp.mean(xf * xf, axis=-1, keepdims=True)
            return w * (xf * jax.lax.rsqrt(var + EPS)).astype(x.dtype)
        b, s, _ = hidden_states.shape
        scaling = Q_DIM ** (-0.5)
        q = (hidden_states @ q_proj_w.T).reshape(b, s, H, Q_DIM).transpose(0, 2, 1, 3)
        compressed = hidden_states @ kv_a_proj_w.T
        k_pass_lat = compressed[..., :KV_RANK]
        k_rot = compressed[..., KV_RANK:]
        kv = _rmsnorm(k_pass_lat, kv_a_ln_w) @ kv_b_proj_w.T
        kv = kv.reshape(b, s, H, NOPE + V_DIM).transpose(0, 2, 1, 3)
        k_pass = kv[..., :NOPE]
        v = kv[..., NOPE:]
        k_rot = jnp.broadcast_to(k_rot[:, None, :, :], (b, H, s, ROPE))
        k = jnp.concatenate([k_pass, k_rot], axis=-1)
        scores = jnp.einsum('bhqd,bhkd->bhqk', q, k) * scaling
        causal = jnp.tril(jnp.ones((s, s), bool))
        scores = jnp.where(causal[None, None], scores, NEG)
        probs = jax.nn.softmax(scores.astype(jnp.float32), axis=-1).astype(q.dtype)
        out = jnp.einsum('bhqk,bhkd->bhqd', probs, v)
        out = out.transpose(0, 2, 1, 3).reshape(b, s, H * V_DIM)
        return out @ o_proj_w.T

    def _L0_ffn_ref(hidden_states, router_weight, gate_up_proj, down_proj):
        import jax, jax.numpy as jnp
        import numpy as np
        TOP_K = 8
        CAPACITY = 128
        B, S, H = hidden_states.shape
        E = router_weight.shape[0]
        K, C = (TOP_K, CAPACITY)
        x = hidden_states.reshape(-1, H)
        logits = x @ router_weight.T
        probs = jax.nn.softmax(logits, axis=-1)
        topw, topi = jax.lax.top_k(probs, K)
        topw = topw / jnp.sum(topw, axis=-1, keepdims=True)
        flat_e = topi.reshape(-1)
        oh = jax.nn.one_hot(flat_e, E, dtype=jnp.int32)
        pos = jnp.take_along_axis(jnp.cumsum(oh, axis=0), flat_e[:, None], axis=1)[:, 0] - 1
        x_rep = jnp.repeat(x, K, axis=0)
        xe = jnp.zeros((E, C, H), x.dtype).at[flat_e, pos].set(x_rep, mode='drop')
        gu = jnp.einsum('ech,ehf->ecf', xe, gate_up_proj)
        g, u = jnp.split(gu, 2, axis=-1)
        h = jax.nn.silu(g) * u
        ye = jnp.einsum('eci,eih->ech', h, down_proj)
        valid = pos < C
        y_flat = jnp.where(valid[:, None], ye[flat_e, jnp.minimum(pos, C - 1)], 0.0)
        y = jnp.sum(y_flat.reshape(-1, K, H) * topw.reshape(-1, K)[..., None], axis=1)
        return y.reshape(B, S, H)

    def _L1_attn_ref(x, w_f, w_i, w_v, w_q, w_ro, w_aux, w_up, w_gate, w_down, init_state):
        import jax, jax.numpy as jnp
        import numpy as np
        B, S, H, R, L = (4, 256, 256, 256, 256)
        W_SCALE = 0.02

        def _reference_tuple_inner(x, w_f, w_i, w_v, w_q, w_ro, w_aux, w_up, w_gate, w_down, init_state):
            b, s, _ = x.shape
            f = jnp.tanh(jnp.einsum('bsh,hr->bsr', x, w_f))
            g = jax.nn.sigmoid(jnp.einsum('bsh,hr->bsr', x, w_i)) * jax.nn.silu(jnp.einsum('bsh,hr->bsr', x, w_v))

            def step(state, fg):
                ft, gt = fg
                state = ft * state + gt
                return (state, state)
            s0 = jnp.broadcast_to(init_state, (b, init_state.shape[0]))
            _, states = jax.lax.scan(step, s0, (jnp.swapaxes(f, 0, 1), jnp.swapaxes(g, 0, 1)))
            states = jnp.swapaxes(states, 0, 1)
            q = jnp.einsum('bsh,hr->bsr', x, w_q)
            readout = jax.nn.silu(q * states)
            local = jnp.einsum('bsl,lh->bsh', jnp.einsum('bsh,hl->bsl', x, w_up) * jax.nn.silu(jnp.einsum('bsh,hl->bsl', x, w_gate)), w_down)
            out = jnp.einsum('bsr,rh->bsh', readout, w_ro) + local
            aux_pred = jnp.einsum('bsr,rh->bsh', jax.nn.silu(states[:, :-1]), w_aux)
            aux_target = jax.lax.stop_gradient(x[:, 1:])
            aux_loss = jnp.mean((aux_pred - aux_target) ** 2)
            return (out, aux_loss)
        return _reference_tuple_inner(x, w_f, w_i, w_v, w_q, w_ro, w_aux, w_up, w_gate, w_down, init_state)[0]

    def _L1_ffn_ref(hidden_states, router_w, w1, w2, w_gate, w_up, w_down):
        import jax, jax.numpy as jnp
        import numpy as np
        B, S, H = (4, 256, 256)
        INTER = 512
        E = 8
        TOPK = 2
        SHARED_I = INTER * 2

        def moe_forward(hidden_states, router_w, w1, w2, w_gate, w_up, w_down):
            b, s, h = hidden_states.shape
            x = hidden_states.reshape(-1, h)
            T = x.shape[0]
            logits = x @ router_w
            top_logits, top_indices = jax.lax.top_k(logits, TOPK)
            scores = jax.nn.softmax(top_logits, axis=-1)
            flat_idx = top_indices.reshape(-1)
            sorted_pos = jnp.argsort(flat_idx, stable=True)
            permuted = x[sorted_pos // TOPK]
            expert_ids = flat_idx[sorted_pos]
            out = jnp.zeros((T * TOPK, h), x.dtype)
            for e in range(E):
                mask = (expert_ids == e)[:, None]
                f1 = permuted * mask @ w1[e]
                g, u = jnp.split(f1, 2, axis=-1)
                act = jax.nn.silu(g) * u
                out = out + jnp.where(mask, act @ w2[e], 0.0)
            unperm = jnp.zeros_like(out).at[sorted_pos].set(out)
            combined = (unperm.reshape(T, TOPK, h) * scores[..., None]).sum(axis=1)
            shared = jax.nn.silu(x @ w_gate) * (x @ w_up) @ w_down
            return (combined + shared).reshape(b, s, h)
        return moe_forward(hidden_states, router_w, w1, w2, w_gate, w_up, w_down)
    x = L0_attn_hidden_states
    x = _layernorm(x + _L0_attn_ref(x, L0_attn_q_proj_w, L0_attn_kv_a_proj_w, L0_attn_kv_a_ln_w, L0_attn_kv_b_proj_w, L0_attn_o_proj_w), axis=-1)
    x = _layernorm(x + _L0_ffn_ref(x, L0_ffn_router_weight, L0_ffn_gate_up_proj, L0_ffn_down_proj), axis=-1)
    x = _layernorm(x + _L1_attn_ref(x, L1_attn_w_f, L1_attn_w_i, L1_attn_w_v, L1_attn_w_q, L1_attn_w_ro, L1_attn_w_aux, L1_attn_w_up, L1_attn_w_gate, L1_attn_w_down, L1_attn_init_state), axis=-1)
    x = _layernorm(x + _L1_ffn_ref(x, L1_ffn_router_w, L1_ffn_w1, L1_ffn_w2, L1_ffn_w_gate, L1_ffn_w_up, L1_ffn_w_down), axis=-1)
    return x

_drawn_inputs = setup_inputs


def setup_inputs(seed=0):
    import zlib

    import numpy as np

    out = dict(_drawn_inputs(seed))
    spreads = {'L0_attn_kv_a_ln_w': (1.0, 0.2), 'L1_attn_init_state': (0.0, 0.8)}
    factors = {'L0_ffn_router_weight': 8.0,
     'L0_ffn_gate_up_proj': 8.0,
     'L0_ffn_down_proj': 8.0,
     'L1_attn_w_f': 8.0,
     'L1_attn_w_i': 8.0,
     'L1_attn_w_v': 8.0,
     'L1_attn_w_q': 8.0,
     'L1_attn_w_ro': 8.0,
     'L1_attn_w_up': 3.362,
     'L1_attn_w_gate': 3.382,
     'L1_attn_w_down': 3.339,
     'L1_ffn_router_w': 3.875,
     'L1_ffn_w1': 3.326,
     'L1_ffn_w2': 3.33}
    for name, (base, spread) in spreads.items():
        noise = np.random.default_rng([zlib.crc32(name.encode()), seed]).standard_normal(out[name].shape)
        drawn = base * np.exp(spread * noise) if base else spread * noise
        out[name] = jnp.asarray(drawn.astype(out[name].dtype))
    for name, factor in factors.items():
        out[name] = (out[name] * factor).astype(out[name].dtype)
    return out
```

```python
import concourse.bass as bass
from concourse import mybir
from contextlib import ExitStack

P = 128
T, HID = 1024, 256
TILES = T // P
HC = HID // P
HEADS, NOPE, ROPE, VDIM, RANK = 16, 128, 64, 128, 64
QDIM = NOPE + ROPE
PAIRS = HEADS // 2
LN_EPS, RMS_EPS = 1e-5, 1e-6
BANK = 512
MASKED = -1e30
E0, TOP0, CAP, I0 = 64, 8, 128, 96
SLOTS = E0 * CAP
E1, TOP1, I1, SH = 8, 2, 512, 1024
BLOCKS = T * TOP1 // P + E1 - 1
ZEROINGS = SLOTS // T + -(-BLOCKS * P // T)


def build(nc, x, xT, wq, wq_ropeT, wkv_aT, kv_ln, wkv_b, woT, router0T, gate_up0, down0, w_in, init_state,
          w_mix, router1, w1, w2, sh_gate, sh_up, sh_down, out):
    f32, f32r, bf16, i32, u32 = (mybir.dt.float32, mybir.dt.float32r, mybir.dt.bfloat16,
                                 mybir.dt.int32, mybir.dt.uint32)
    ALU, ACT, AX = mybir.AluOpType, mybir.ActivationFunctionType, mybir.AxisListType
    ctx = ExitStack()
    with ctx:
        def sb(name, shape, dt=f32):
            return ctx.enter_context(nc.sbuf_tensor(name, shape, dt))

        def sem(name):
            return ctx.enter_context(nc.semaphore(name))

        def carve(area):
            at = [0]

            def cut(*dims):
                n = 1
                for d in dims:
                    n *= d
                piece = area[:, at[0]:at[0] + n]
                at[0] += n
                if len(dims) == 2:
                    piece = piece.rearrange("p (a b) -> p a b", a=dims[0])
                elif len(dims) == 3:
                    piece = piece.rearrange("p (a b c) -> p a b c", a=dims[0], b=dims[1])
                return piece
            return cut

        area1 = sb("area1", [P, HEADS * T])
        area2 = sb("area2", [P, 4 * HC * T])
        area3 = sb("area3", [P, 8192])
        area4 = sb("area4", [P, 6144])
        cutA2, cutA3, cutB4 = carve(area2), carve(area3), carve(area4)
        cutB3, cutC2, cutC3, cutD3, cutD4 = (carve(a) for a in (area3, area2, area3, area3, area4))
        ident = sb("ident", [P, P])
        ident_bf = sb("ident_bf", [P, P], bf16)
        causal = sb("causal", [P, P], bf16)
        minus_half = sb("minus_half", [P, TILES])
        x_in = cutA2(TILES, HID)
        xT_in = cutA2(HC, T)
        xT_hi = sb("xT_hi", [P, HC, T], f32r)
        xT_lo = sb("xT_lo", [P, HC, T], f32r)
        wkv_a = cutA3(HC, P)
        lnw = sb("lnw", [P, RANK])
        wkb = cutA3(HEADS, RANK)
        wq_h = cutA3(2, HID)
        wv_h = cutA3(2, RANK)
        wo_h = cutA3(2, HID)
        weff = cutA3(2, HC, P)
        weff_hi = sb("weff_hi", [P, 2, HC, P], f32r)
        weff_lo = sb("weff_lo", [P, 2, HC, P], f32r)
        wvo = cutA3(PAIRS * HID)
        qT = area1
        q_hi = sb("q_hi", [P, 2, P], f32r)
        q_lo = sb("q_lo", [P, 2, P], f32r)
        sq = cutA3(TILES, RANK)
        ms = sb("ms", [P, TILES])
        rms = sb("rms", [P, TILES])
        keys = cutA3(TILES, P)
        latent = cutA3(TILES, RANK + 1)
        kT_hi = sb("kT_hi", [P, T], f32r)
        kT_lo = sb("kT_lo", [P, T], f32r)
        neg_max = sb("neg_max", [P, 2])
        probs = cutA2(2, T)
        probsT = cutA2(2, T)
        rsum = sb("rsum", [P, 2])
        ctx_n = sb("ctx_n", [P, P])
        ctxT = sb("ctxT", [P, P])
        y = sb("y", [P, HID])
        zeros_bf = sb("zeros_bf", [P, HID], bf16)
        stats = sb("stats", [P, 6])
        mv = sb("mv", [P, 2])
        rstd = sb("rstd", [P, 1])
        x1 = sb("x1", [P, TILES, HID])

        zero_rows = area4[:, 6144 - 2 * T:]
        cutB4b = carve(area4[:, 1024:])
        router0 = sb("router0", [P, HC, E0])
        earlier = sb("earlier", [P, P], bf16)
        ones_bf = sb("ones_bf", [P, P], bf16)
        iota_e = sb("iota_e", [P, E0])
        spare = cutB4(TILES, TOP0)
        x1T = sb("x1T", [P, HC, P])
        logits = cutB4(E0)
        left = cutB4(E0)
        top_v = cutB4(TILES, TOP0)
        top_i = sb("top_i", [P, TILES, TOP0], u32)
        top_f = cutB4(TILES, TOP0)
        chosen = sb("chosen", [P, TILES, E0], bf16)
        chosen_before = sb("chosen_before", [P, TILES, E0], bf16)
        place = cutB4(E0)
        onehot = wkb.rearrange("p h r -> p (h r)")[:, 0:TOP0 * E0].rearrange("p (a b) -> p a b", a=TOP0)
        placed = wkb.rearrange("p h r -> p (h r)")[:, TOP0 * E0:].rearrange("p (a b) -> p a b", a=TOP0)
        place8 = cutB4(TILES, TOP0)
        valid = sb("valid", [P, TILES, TOP0])
        slot = cutB4(TILES, TOP0)
        slot_t = sb("slot_t", [P, TOP0])
        send_i = sb("send_i", [P, TILES, TOP0], i32)
        fetch_i = sb("fetch_i", [P, TILES, TOP0], i32)
        weight = sb("weight", [P, TILES, TOP0])
        wsum = sb("wsum", [P, TILES])
        RING = 8
        gu_w = cutB4b(RING * HC * 2 * I0).rearrange("p (e c n) -> p e c n", e=RING, c=HC)
        dn_w = cutB4b(RING, HID)[0:I0]
        xe = cutB3(RING, HID)
        xeT = cutB3(2, HC, P)
        sg = cutB3(2, P)[0:I0]
        hT = cutB3(2, P)[0:I0]
        ye = cutB3(RING, HID)
        gathered = cutC2(2, TOP0, HID)
        w_c = cutC2(6, HC, HID)
        wo_c = cutC2(2, HC, HID)
        x2 = cutC3(2, HID)
        forget, igate, value, lgate, state, zq, readout, local = (cutC3(2, HC, P) for _ in range(8))
        x2T = cutC3(2, HC, P)
        init2 = sb("init2", [P, HC])
        fetch_now = sb("fetch_now", [P, 2, TOP0], i32)
        w1_s = area1
        w2_s = area2
        last_rows = area1[:, 0:TILES * TOP1 * HID].rearrange("p (t k n) -> p t k n", t=TILES, k=TOP1)
        sh_g, sh_u, sh_d = cutD4(HC, SH), cutD4(HC, SH), cutD4(SH // P, HID)
        shared = cutD3(TILES, HID)
        x3T = cutD3(HC, T)
        SC = SH // P
        hs = cutD3(SC, BANK)
        cutE3 = carve(area3[:, TILES * HID + HC * T:])
        xd, xdT = cutE3(2, HID), cutE3(2, HC, P)
        hd, hdT, yd = cutE3(BANK), cutE3(2, BANK), cutE3(2, HID)
        sgd = sb("sgd", [P, 2, BANK])
        router1_s = sb("router1_s", [P, HC, E1])
        iota_b = sb("iota_b", [P, BLOCKS])
        iota_r = sb("iota_r", [P, TILES])
        lg1 = sb("lg1", [P, TILES, E1])
        tv1 = sb("tv1", [P, TILES, E1])
        ti1 = sb("ti1", [P, TILES, E1], u32)
        tf1 = sb("tf1", [P, TILES, E1])
        oh1 = sb("oh1", [P, TILES, TOP1, E1])
        ch1 = sb("ch1", [P, TILES, E1], bf16)
        cb1 = sb("cb1", [P, TILES + 1, E1], bf16)
        pl1 = sb("pl1", [P, TILES + 1, E1])
        blk_cmp = sb("blk_cmp", [P, E1, TILES])
        nblk = sb("nblk", [P, E1])
        ones_e = sb("ones_e", [P, E1])
        blk_end = sb("blk_end", [P, E1])
        blk_start = sb("blk_start", [P, E1])
        own_cmp = sb("own_cmp", [P, BLOCKS, E1])
        owner = sb("owner", [P, BLOCKS])
        owner_i = sb("owner_i", [P, BLOCKS], i32)
        sl1 = sb("sl1", [P, TILES, TOP1])
        slot1 = sb("slot1", [P, TILES, TOP1], i32)
        weight1 = sb("weight1", [P, TILES, TOP1])
        result = area1[:, TILES * TOP1 * HID:(TILES * TOP1 + 2) * HID].rearrange("p (a n) -> p a n", a=2)
        xd_d = nc.dram_tensor("xd_d", (BLOCKS * P, HID), f32).ap()
        yd_d = nc.dram_tensor("yd_d", (BLOCKS * P, HID), f32).ap()
        xe_d = nc.dram_tensor("xe_d", (SLOTS + T * TOP0, HID), f32).ap()
        ye_d = nc.dram_tensor("ye_d", (SLOTS, HID), f32).ap()

        banks = [ctx.enter_context(nc.psum_tensor(f"scores{u}", [P, 2 * BANK], f32)) for u in range(2)]
        pT = [ctx.enter_context(nc.psum_tensor(f"probsT_ps{u}", [P, BANK], f32)) for u in range(2)]
        misc = ctx.enter_context(nc.psum_tensor("misc_ps", [P, BANK], f32))
        acc = ctx.enter_context(nc.psum_tensor("acc_ps", [P, BANK], f32))
        CW = RANK + 1
        ctx_ps = misc[:, 0:CW]
        ctxT_ps = misc[:, P:2 * P]
        x1T_ps = misc[:, 2 * P:4 * P]
        place_ps = misc[:, 0:E0]
        logits_ps = misc[:, 2 * P:2 * P + E0]
        half = [banks[u][:, b * BANK:(b + 1) * BANK] for u in range(2) for b in range(2)]

        ld_x, ld_xT, ld_kv, ld_lnw, ld_wkb = (sem(n) for n in ("ld_x", "ld_xT", "ld_kv", "ld_lnw", "ld_wkb"))
        ld_head = [sem(f"ld_head{u}") for u in range(2)]
        consts, made = sem("consts"), sem("made")
        x_split, kv_ready, sq_done, ms_done, rms_done, keys_done, ones_done, kT_ps, k_split = (
            sem(n) for n in ("x_split", "kv_ready", "sq_done", "ms_done", "rms_done", "keys_done", "ones_done", "kT_ps", "k_split"))
        weff_ps, weff_f32, weff_split, wvo_ps, wvo_done, qT_ps, qT_done = (
            sem(n) for n in ("weff_ps", "weff_f32", "weff_split", "wvo_ps", "wvo_done", "qT_ps", "qT_done"))
        q_half, q_split, scores_ready, max_ready, probs_ready = (
            sem(n) for n in ("q_half", "q_split", "scores_ready", "max_ready", "probs_ready"))
        pT_ps = [sem(f"pT_ps{c}") for c in range(2)]
        pT_done = [sem(f"pT_done{c}") for c in range(2)]
        ctx_ready, rsum_done, ctx_normed, ctxT_psd, ctxT_done, acc_ready, acc_read = (
            sem(n) for n in ("ctx_ready", "rsum_done", "ctx_normed", "ctxT_psd", "ctxT_done", "acc_ready", "acc_read"))
        dve_w, dve_ln = sem("dve_w"), sem("dve_ln")
        dve_step, var_done, rstd_done, x1_done, stored = (
            sem(n) for n in ("dve_step", "var_done", "rstd_done", "x1_done", "stored"))

        block = ctx.enter_context(nc.Block())

        zeroed, ld_router0, x1T_psd, x1T_done, logits_done, logits_read, chosen_done, place_done, place_read, send_done, sent = (
            sem(n) for n in ("zeroed", "ld_router0", "x1T_psd", "x1T_done", "logits_done", "logits_read", "chosen_done",
                             "place_done", "place_read", "send_done", "sent"))
        consts0, route_step, exp0, weight_done, fetch_ready = (
            sem(n) for n in ("consts0", "route_step", "exp0", "weight_done", "fetch_ready"))
        ld_gu = [sem(f"ld_gu{u}") for u in range(RING // 2)]
        ld_dn = [sem(f"ld_dn{u}") for u in range(RING // 2)]
        ld_xe = [sem(f"ld_xe{u}") for u in range(RING // 2)]
        st_ye = [sem(f"st_ye{u}") for u in range(RING // 2)]
        xeT_ps, xeT_done, gu_ready, silu_done, h_done, ye_ps, ye_done = (
            sem(n) for n in ("xeT_ps", "xeT_done", "gu_ready", "silu_done", "h_done", "ye_ps", "ye_done"))
        (ld_wc, ld_woc, ld_init, gath_idx, combined, comb_step, x2_done, x2T_psd, x2T_done, fi_ready, vq_ready,
         ug_ready, gates_done, mid_step, z_done, r_done, lu_done, mix_ready, mix_read, x3_done, init_done) = (
            sem(n) for n in ("ld_wc", "ld_woc", "ld_init", "gath_idx", "combined", "comb_step", "x2_done", "x2T_psd",
                             "x2T_done", "fi_ready", "vq_ready", "ug_ready", "gates_done", "mid_step", "z_done",
                             "r_done", "lu_done", "mix_ready", "mix_read", "x3_done", "init_done"))
        gath = [sem(f"gath{u}") for u in range(2)]
        (ld_w1, ld_w2, ld_sh, ld_router1, x3T_ps, x3T_done, lg1_ready, d_step, ch1_done, pl1_ready, slots1_ready,
         sent1, tanh1, consts1, gs_ready, gs_silu, hs_done, sh_ready, sh_read, last_go) = (
            sem(n) for n in ("ld_w1", "ld_w2", "ld_sh", "ld_router1", "x3T_ps", "x3T_done", "lg1_ready", "d_step",
                             "ch1_done", "pl1_ready", "slots1_ready", "sent1", "tanh1", "consts1", "gs_ready",
                             "gs_silu", "hs_done", "sh_ready", "sh_read", "last_go"))
        ld_xd = [sem(f"ld_xd{u}") for u in range(2)]
        st_yd = [sem(f"st_yd{u}") for u in range(2)]
        (xdT_ps, xdT_done, f1_ready, sgd_done, hd_done, hdT_ps, hdT_done, yd_ps, yd_done, final_step, result_done) = (
            sem(n) for n in ("xdT_ps", "xdT_done", "f1_ready", "sgd_done", "hd_done", "hdT_ps", "hdT_done", "yd_ps",
                             "yd_done", "final_step", "result_done"))
        last_in = [sem(f"last_in{t}") for t in range(TILES)]
        st_out = [sem(f"st_out{u}") for u in range(2)]
        rec_ps = [[half[0], half[1], half[2]], [half[3], pT[0], pT[1]]]
        passed = sem("passed")

        def chain(eng, signal, base=0):
            count = [0]

            def link(ins):
                count[0] += 1
                ins.then_inc(signal, 1)
                eng.wait_ge(signal, base + count[0])
            return link

        def turn(e, u):
            return 16 // RING * (e - u) + 16

        def tiles_two(eng, body):
            body(0, 0)
            body(1, 1)
            with eng.Fori(1, TILES // 2) as i:
                for u in range(2):
                    body(2 * i + u, u)

        def blocks_two(eng, body):
            body(0, 0)
            body(1, 1)
            with eng.Fori(1, BLOCKS // 2) as i:
                for u in range(2):
                    body(2 * i + u, u)
            body(BLOCKS - 1, 0)

        def past(n, first):
            return not isinstance(n, int) or n >= first

        def hold(eng, signal, value):
            eng.wait_ge(signal, value)
            eng.sem_inc(passed, 1)

        def rank2(t):
            return TILES + (t if isinstance(t, int) and t < 2 else 2 * t - 1)

        def rank3(t):
            return TILES + (2 * t + 2 if not isinstance(t, int) or t < TILES - 1 else 2 * TILES - 1)

        def nth(qt, h):
            return qt * HEADS + h

        def chunks(qt):
            return 1 if qt < 4 else 2

        @block.sync
        def _(sp):
            sp.dma_start(xT_in[:], xT.rearrange("(c p) t -> p c t", p=P)).then_inc(ld_xT, 16)
            sp.dma_start(wkv_a[:], wkv_aT.rearrange("(c p) n -> p c n", p=P)).then_inc(ld_kv, 16)
            sp.dma_start(wkb[:], wkv_b.rearrange("(h a p) r -> a p h r", a=2, p=P)[0]).then_inc(ld_wkb, 16)
            wq_v = wq.rearrange("(h d) n -> d h n", d=QDIM)
            wr_v = wq_ropeT.rearrange("(c p) (h r) -> p c h r", p=P, h=HEADS)
            wv_v = wkv_b.rearrange("(h a p) r -> a p h r", a=2, p=P)[1]
            wo_v = woT.rearrange("(h p) n -> p h n", p=P)

            def load_head(h, u):
                sp.dma_start(wq_h[:, u, :], wq_v[0:P, h, :]).then_inc(ld_head[u], 16)
                sp.dma_start(weff[:, u, :, RANK:], wr_v[:, :, h, :]).then_inc(ld_head[u], 16)
                sp.dma_start(wv_h[:, u, :], wv_v[:, h, :]).then_inc(ld_head[u], 16)
                sp.dma_start(wo_h[:, u, :], wo_v[:, h, :]).then_inc(ld_head[u], 16)

            load_head(0, 0)
            load_head(1, 1)
            sp.dma_start(lnw[:], bass.AP(kv_ln.tensor, 0, [[0, P], [1, RANK]])).then_inc(ld_lnw, 16)
            sp.dma_start(x_in[:], x.rearrange("(t p) n -> p t n", p=P)).then_inc(ld_x, 16)
            with sp.Fori(1, PAIRS) as j:
                for u in range(2):
                    sp.wait_ge(wvo_ps, 2 * j - 1 + u)
                    sp.wait_ge(weff_split, 2 * j - 1 + u)
                    for dst, src in ((wq_h[:, u, :], wq_v[0:P, bass.ds(2 * j + u, 1), :]),
                                     (weff[:, u, :, RANK:], wr_v[:, :, bass.ds(2 * j + u, 1), :]),
                                     (wv_h[:, u, :], wv_v[:, bass.ds(2 * j + u, 1), :]),
                                     (wo_h[:, u, :], wo_v[:, bass.ds(2 * j + u, 1), :])):
                        sp.dma_start(dst, src).then_inc(ld_head[u], 16)
            sp.wait_ge(consts0, 1)
            for b in range(SLOTS // T):
                sp.dma_start(xe_d[b * T:(b + 1) * T, :].rearrange("(p a) n -> p (a n)", p=P),
                             zero_rows[:]).then_inc(zeroed, 16)
            for b in range(0, BLOCKS * P, T):
                n = min(T, BLOCKS * P - b)
                sp.dma_start(xd_d[b:b + n, :].rearrange("(p a) n -> p (a n)", p=P),
                             zero_rows[:, 0:n * HID // P]).then_inc(zeroed, 16)
            sp.dma_start(router0[:], router0T.rearrange("(c p) e -> p c e", p=P)).then_inc(ld_router0, 16)
            gu_v = gate_up0.rearrange("e (c p) f -> p e c f", p=P)
            dn_v = down0.rearrange("e i n -> i e n")
            xe_v = xe_d[0:SLOTS, :].rearrange("(e p) n -> p e n", p=P)

            def load_weights(e, u):
                if past(e, RING):
                    sp.wait_ge(ye_ps, e + 2 - RING)
                sp.dma_start(gu_w[:, u:u + 2], gu_v[:, bass.ds(e, 2)]).then_inc(ld_gu[u // 2], 16)
                sp.dma_start(dn_w[:, u:u + 2, :], dn_v[:, bass.ds(e, 2), :]).then_inc(ld_dn[u // 2], 16)

            def load_rows(e, u):
                if past(e, RING):
                    sp.wait_ge(xeT_ps, e + 2 - RING)
                sp.dma_start(xe[:, u:u + 2, :], xe_v[:, bass.ds(e, 2), :]).then_inc(ld_xe[u // 2], 16)

            sp.wait_ge(zeroed, 16 * ZEROINGS)
            for e in range(0, RING, 2):
                load_weights(e, e)
            sp.wait_ge(x1_done, TILES)
            sp.dma_start(w_c, w_in.rearrange("m (c p) n -> p m c n", p=P)).then_inc(ld_wc, 16)
            sp.dma_start(wo_c, w_mix.rearrange("m (c p) n -> p m c n", p=P)).then_inc(ld_woc, 16)
            sp.dma_start(init2[:], init_state).then_inc(ld_init, 16)
            sp.dma_start(router1_s[:], router1.rearrange("(c p) e -> p c e", p=P)).then_inc(ld_router1, 16)
            sp.wait_ge(sent, 16 * TILES * TOP0)
            for e in range(0, RING, 2):
                load_rows(e, e)
            with sp.Fori(1, E0 // RING) as i:
                for u in range(0, RING, 2):
                    load_rows(RING * i + u, u)
                    load_weights(RING * i + u, u)
            sp.wait_ge(ye_ps, E0)
            sp.dma_start(sh_g, sh_gate.rearrange("(c p) f -> p c f", p=P)).then_inc(ld_sh, 16)
            sp.dma_start(sh_u, sh_up.rearrange("(c p) f -> p c f", p=P)).then_inc(ld_sh, 16)
            sp.dma_start(sh_d, sh_down.rearrange("(c p) n -> p c n", p=P)).then_inc(ld_sh, 16)
            for e in range(E1):
                sp.wait_ge(combined, e + 1)
                sp.dma_start(w1_s[:, e * HC * 2 * I1:(e + 1) * HC * 2 * I1].rearrange("p (c f) -> p c f", c=HC),
                             w1[e].rearrange("(c p) f -> p c f", p=P)).then_inc(ld_w1, 16)
            sp.wait_ge(x3_done, TILES)
            for e in range(E1):
                sp.dma_start(w2_s[:, e * I1 * HID // P:(e + 1) * I1 * HID // P].rearrange("p (c n) -> p c n", n=HID),
                             w2[e].rearrange("(c p) n -> p c n", p=P)).then_inc(ld_w2, 16)
            xd_v = xd_d.rearrange("(i p) n -> p i n", p=P)

            def load_block(i, u):
                if past(i, 2):
                    sp.wait_ge(xdT_ps, i - 1)
                sp.dma_start(xd[:, u, :], xd_v[:, bass.ds(i, 1), :]).then_inc(ld_xd[u], 16)

            sp.wait_ge(sh_read, TILES)
            sp.wait_ge(sent1, 16 * TILES * TOP1)
            blocks_two(sp, load_block)
            for t in range(TILES):
                sp.wait_ge(result_done, t + 1)
                sp.dma_start(out[t * P:(t + 1) * P, :], result[:, t % 2, :]).then_inc(st_out[t % 2], 16)
            for u in range(2):
                sp.wait_ge(st_out[u], 16 * TILES // 2)

        @block.gpsimd
        def _(pool):
            pool.memset(ident[:], 0.0).then_inc(made, 1)
            pool.memset(causal[:], 0.0).then_inc(made, 1)
            pool.memset(minus_half[:], -0.5).then_inc(made, 1)
            pool.memset(zeros_bf[:], 0.0).then_inc(made, 1)
            pool.wait_ge(made, 4)
            pool.affine_select(out=ident[:], in_=ident[:], compare_op=ALU.not_equal, fill=1.0, base=0,
                               pattern=[[-1, P]], channel_multiplier=1).then_inc(made, 1)
            pool.affine_select(out=causal[:], in_=causal[:], compare_op=ALU.is_ge, fill=MASKED, base=0,
                               pattern=[[-1, P]], channel_multiplier=1).then_inc(made, 1)
            pool.memset(latent[:, :, RANK:], 1.0).then_inc(ones_done, 1)
            pool.wait_ge(made, 6)
            pool.tensor_copy(ident_bf[:], ident[:]).then_inc(consts, 1)
            pool.memset(zero_rows[:], 0.0).then_inc(consts0, 1)
            pool.memset(ones_bf[:], 1.0).then_inc(made, 1)
            pool.memset(earlier[:], 1.0).then_inc(made, 1)
            pool.memset(chosen_before[:, 0, :], 0.0).then_inc(made, 1)
            pool.wait_ge(made, 9)
            pool.affine_select(out=earlier[:], in_=earlier[:], compare_op=ALU.is_gt, fill=0.0, base=0,
                               pattern=[[1, P]], channel_multiplier=-1).then_inc(consts0, 1)
            pool.iota(iota_e[:], pattern=[[1, E0]], base=0, channel_multiplier=0,
                      allow_small_or_imprecise_dtypes=True).then_inc(consts0, 1)
            pool.iota(spare, pattern=[[P, TILES], [T, TOP0]], base=SLOTS, channel_multiplier=1,
                      allow_small_or_imprecise_dtypes=True).then_inc(consts0, 1)
            pool.iota(iota_b[:], pattern=[[1, BLOCKS]], base=0, channel_multiplier=0,
                      allow_small_or_imprecise_dtypes=True).then_inc(consts1, 1)
            pool.iota(iota_r[:], pattern=[[P, TILES]], base=0, channel_multiplier=0,
                      allow_small_or_imprecise_dtypes=True).then_inc(consts1, 1)
            pool.memset(ones_e[:], 1.0).then_inc(consts1, 1)
            pool.memset(cb1[:, 0, :], 0.0).then_inc(consts1, 1)
            pool.wait_ge(ms_done, 1)
            pool.tensor_tensor(rms[:], ms[:], minus_half[:], ALU.pow).then_inc(rms_done, 1)

            def split_q(qt, h, u, n):
                src = qT[:, bass.ds(h * T + qt * P, P)]
                pool.tensor_copy(q_hi[:, u, :], src).then_inc(q_half, 1)
                hold(pool, q_half, n + 1)
                pool.tensor_tensor(q_lo[:, u, :], src, q_hi[:, u, :].bitcast(f32), ALU.subtract).then_inc(q_split, 1)

            def rstd_of(k):
                pool.wait_ge(var_done, k + 1)
                pool.tensor_tensor(rstd[:], mv[:, 1:2], minus_half[:, 0:1], ALU.pow).then_inc(rstd_done, 1)

            pool.wait_ge(qT_done, HEADS)
            def send(t):
                pool.wait_ge(send_done, t + 1)
                for k in range(TOP0):
                    pool.indirect_dma_start(xe_d, bass.IndirectOffsetOnAxis(send_i[:, t, k:k + 1], 0),
                                            x1[:, t, :], None).then_inc(sent, 16)

            for qt in range(TILES):
                if qt == 2:
                    pool.wait_ge(zeroed, 16 * ZEROINGS)
                for u in range(2):
                    if nth(qt, u) >= 2:
                        pool.wait_ge(scores_ready, nth(qt, u) - 1)
                    split_q(qt, u, u, nth(qt, u))
                if qt:
                    rstd_of(qt - 1)
                if qt >= 3:
                    send(qt - 3)
                with pool.Fori(1, PAIRS) as j:
                    for u in range(2):
                        pool.wait_ge(scores_ready, nth(qt, 2 * j + u) - 1)
                        split_q(qt, 2 * j + u, u, nth(qt, 2 * j + u))
            rstd_of(TILES - 1)
            for t in range(TILES - 3, TILES):
                send(t)
            def fetch(t, u, i):
                if past(t, 2):
                    pool.wait_ge(combined, t - 1)
                pool.sem_inc(passed, 1)
                pool.tensor_copy(fetch_now[:, u, :], fetch_flat[:, bass.ds(t * TOP0, TOP0)]).then_inc(gath_idx, 1)
                hold(pool, gath_idx, t + 1)
                for k in range(TOP0):
                    pool.indirect_dma_start(gathered[:, u, k, :], None, ye_d,
                                            bass.IndirectOffsetOnAxis(fetch_now[:, u, k:k + 1], 0)).then_inc(gath[u], 16)

            fetch_flat = fetch_i[:].rearrange("p t k -> p (t k)")
            pool.wait_ge(weight_done, 1)
            for u in range(RING // 2):
                pool.wait_ge(st_ye[u], 16 * E0 // RING)
            fetch(0, 0, 0)
            fetch(1, 1, 0)
            rstd_of(rank2(0))
            fetch(2, 0, 1)
            rstd_of(rank2(1))
            fetch(3, 1, 1)
            rstd_of(rank3(0))
            with pool.Fori(1, TILES // 2 - 1) as i:
                for u in range(2):
                    rstd_of(rank2(2 * i + u))
                    fetch(2 * i + u + 2, u, i + 1)
                    rstd_of(rank3(2 * i + u - 1))
            for t in range(TILES - 2, TILES):
                rstd_of(rank2(t))
                rstd_of(rank3(t - 1))
            rstd_of(rank3(TILES - 1))
            pool.wait_ge(slots1_ready, 1)
            for t in range(TILES):
                for k in range(TOP1):
                    pool.indirect_dma_start(xd_d, bass.IndirectOffsetOnAxis(slot1[:, t, k:k + 1], 0),
                                            x1[:, t, :], None).then_inc(sent1, 16)
            pool.wait_ge(st_yd[0], 16 * (BLOCKS - BLOCKS // 2))
            pool.wait_ge(st_yd[1], 16 * (BLOCKS // 2))
            for t in range(TILES):
                for k in range(TOP1):
                    pool.indirect_dma_start(last_rows[:, t, k, :], None, yd_d,
                                            bass.IndirectOffsetOnAxis(slot1[:, t, k:k + 1], 0)).then_inc(last_in[t], 16)
                if t >= 1:
                    rstd_of(3 * TILES + t - 1)
            rstd_of(4 * TILES - 1)

        @block.scalar
        def _(act):
            act.wait_ge(kv_ready, 1)
            act.activation(sq[:], banks[0][:].rearrange("p (t n) -> p t n", t=TILES)[:, :, 0:RANK],
                           ACT.Square).then_inc(sq_done, 1)

            def weff_copy(h, u):
                act.wait_ge(weff_ps, h + 1)
                act.copy(weff[:, u, :, 0:RANK],
                         pT[u][:, 0:HC * RANK].rearrange("p (c r) -> p c r", c=HC)).then_inc(weff_f32, 1)

            def q_copy(h, u):
                hold(act, qT_ps, h + 1)
                act.activation(qT[:, bass.ds(h * T, T)], banks[u][:], ACT.Copy,
                               scale=float(QDIM) ** -0.5).then_inc(qT_done, 1)

            weff_copy(0, 0)
            weff_copy(1, 1)
            q_copy(0, 0)
            with act.Fori(1, PAIRS) as j:
                weff_copy(2 * j, 0)
                q_copy(2 * j - 1, 1)
                weff_copy(2 * j + 1, 1)
                q_copy(2 * j, 0)
            q_copy(HEADS - 1, 1)

            def exp_probs(qt, n, u):
                L = (qt + 1) * P
                act.wait_ge(max_ready, n + 1)
                if not isinstance(n, int) or n >= 2:
                    act.wait_ge(ctx_ready, n - 1)
                act.activation(probs[:, u, 0:L], banks[u][:, 0:L], ACT.Exp,
                               bias=neg_max[:, u:u + 1]).then_inc(probs_ready, 1)

            def copy_pT(qt, n, u):
                w = min(qt + 1, 4) * P
                act.wait_ge(pT_ps[0], n + 1)
                act.copy(probsT[:, u, 0:w], pT[u if chunks(qt) == 1 else 0][:, 0:w]).then_inc(pT_done[0], 1)

            def copy_ctxT(m):
                act.wait_ge(ctxT_psd, m + 1)
                act.copy(ctxT[:], ctxT_ps).then_inc(ctxT_done, 1)

            def copy_x1T(t):
                act.wait_ge(x1T_psd, t + 1)
                if t:
                    act.wait_ge(logits_done, t)
                act.copy(x1T[:], x1T_ps.rearrange("p (c n) -> p c n", c=HC)).then_inc(x1T_done, 1)

            for qt in range(TILES):
                if qt:
                    copy_pT(qt - 1, nth(qt, -1), 1)
                exp_probs(qt, nth(qt, 0), 0)
                if qt >= 3:
                    act.wait_ge(place_read, qt - 2)
                if qt:
                    copy_ctxT(qt * PAIRS - 1)
                if qt >= 2:
                    copy_x1T(qt - 2)
                copy_pT(qt, nth(qt, 0), 0)
                exp_probs(qt, nth(qt, 1), 1)
                with act.Fori(1, PAIRS) as j:
                    copy_pT(qt, nth(qt, 2 * j - 1), 1)
                    exp_probs(qt, nth(qt, 2 * j), 0)
                    copy_ctxT(qt * PAIRS + j - 1)
                    copy_pT(qt, nth(qt, 2 * j), 0)
                    exp_probs(qt, nth(qt, 2 * j + 1), 1)
            copy_pT(TILES - 1, nth(TILES, -1), 1)
            copy_ctxT(TILES * PAIRS - 1)
            for t in range(TILES - 2, TILES):
                copy_x1T(t)
            act.wait_ge(exp0, 1)
            act.activation(weight[:], weight[:], ACT.Exp).then_inc(exp0, 1)

            def expert_act(e, u):
                b = u % 2
                act.wait_ge(gu_ready, e + 1)
                act.activation(sg[:, b, :], half[b][0:I0, 0:P], ACT.Silu).then_inc(silu_done, 1)

            ye_v = ye_d.rearrange("(e p) n -> p e n", p=P)

            def expert_out(e, u):
                act.wait_ge(ye_ps, e + 1)
                if past(e, RING) and u % 2 == 0:
                    act.wait_ge(st_ye[u // 2], turn(e, u) - 16)
                act.copy(ye[:, u, :], half[2 + u % 2][:, 0:HID]).then_inc(ye_done, 1)
                if u % 2:
                    act.wait_ge(ye_done, e + 1)
                    act.dma_start(ye_v[:, bass.ds(e - 1, 2), :], ye[:, u - 1:u + 1, :]).then_inc(st_ye[u // 2], 16)

            expert_act(0, 0)
            for e in range(RING):
                expert_act(e + 1, (e + 1) % RING)
                expert_out(e, e)
            with act.Fori(1, E0 // RING - 1) as i:
                for u in range(RING):
                    expert_act(RING * i + u + 1, (u + 1) % RING)
                    expert_out(RING * i + u, u)
            for e in range(E0 - RING, E0):
                if e + 1 < E0:
                    expert_act(e + 1, (e + 1) % RING)
                expert_out(e, e % RING)
            def copy_x2T(t, u):
                act.wait_ge(x2T_psd, t + 1)
                act.copy(x2T[:, u], x1T_ps_c).then_inc(x2T_done, 1)

            def gates(t, u):
                (a, b, c), n = rec_ps[u], HC * P

                def of(ap):
                    return ap.rearrange("p (c n) -> p c n", c=HC)
                act.wait_ge(fi_ready, t + 1)
                if past(t, 2):
                    act.wait_ge(lu_done, t - 1)
                act.activation(forget[:, u], of(a[:, 0:n]), ACT.Tanh).then_inc(gates_done, 1)
                act.activation(igate[:, u], of(a[:, n:]), ACT.Tanh, scale=0.5).then_inc(gates_done, 1)
                act.wait_ge(vq_ready, t + 1)
                act.activation(value[:, u], of(b[:, 0:n]), ACT.Silu).then_inc(gates_done, 1)
                act.wait_ge(ug_ready, t + 1)
                act.activation(lgate[:, u], of(c[:, n:]), ACT.Silu).then_inc(gates_done, 1)

            def read_out(t, u):
                act.wait_ge(z_done, t + 1)
                if past(t, 2):
                    act.wait_ge(mix_ready, t - 1)
                act.activation(readout[:, u], zq[:, u], ACT.Silu, scale=0.5).then_inc(r_done, 1)

            x1T_ps_c = misc[:, 0:HID].rearrange("p (c n) -> p c n", c=HC)
            copy_x2T(0, 0)
            gates(0, 0)
            copy_x2T(1, 1)
            read_out(0, 0)
            gates(1, 1)
            with act.Fori(1, TILES // 2) as i:
                for u in range(2):
                    copy_x2T(2 * i + u, u)
                    read_out(2 * i + u - 1, 1 - u)
                    gates(2 * i + u, u)
            read_out(TILES - 1, 1)
            for b in range(2):
                act.wait_ge(x3T_ps, b + 1)
                act.copy(x3T[:, 0, b * BANK:(b + 1) * BANK], half[b]).then_inc(x3T_done, 1)
            act.wait_ge(tanh1, 1)
            act.activation(weight1[:, :, 1:2], weight1[:, :, 0:1], ACT.Tanh, scale=0.5).then_inc(tanh1, 1)
            for n in range(2 * SC):
                act.wait_ge(gs_ready, n + 1)
                if n >= 2:
                    act.wait_ge(hs_done, n - 1)
                act.activation(sgd[:, n % 2, :], half[n % 2], ACT.Silu).then_inc(gs_silu, 1)

            def block_act(i, u):
                act.wait_ge(f1_ready, i + 1)
                if past(i, 2):
                    act.wait_ge(hd_done, i - 1)
                act.activation(sgd[:, u, :], half[2 * u], ACT.Silu).then_inc(sgd_done, 1)

            def block_T(i, u):
                act.wait_ge(xdT_ps, i + 1)
                if past(i, 2):
                    act.wait_ge(f1_ready, i - 1)
                act.copy(xdT[:, u], x1T_ps_c).then_inc(xdT_done, 1)

            def block_out(i, u):
                act.wait_ge(yd_ps, i + 1)
                if past(i, 2):
                    act.wait_ge(st_yd[u], 8 * (i - u))
                act.copy(yd[:, u, :], acc[:, 0:HID]).then_inc(yd_done, 1)
                act.wait_ge(yd_done, i + 1)
                act.dma_start(yd_v[:, bass.ds(i, 1), :], yd[:, u, :]).then_inc(st_yd[u], 16)

            yd_v = yd_d.rearrange("(i p) n -> p i n", p=P)
            act.wait_ge(hs_done, 2 * SC)
            block_T(0, 0)
            block_act(0, 0)
            block_T(1, 1)

            def block_steps(i, u):
                if not (isinstance(i, int) and i >= BLOCKS - 2):
                    block_T(i + 2, u)
                if not (isinstance(i, int) and i >= BLOCKS - 1):
                    block_act(i + 1, 1 - u)
                block_out(i, u)

            block_steps(0, 0)
            block_steps(1, 1)
            with act.Fori(1, BLOCKS // 2 - 1) as i:
                for u in range(2):
                    block_steps(2 * i + u, u)
            for i in range(BLOCKS - 3, BLOCKS):
                block_steps(i, i % 2)

        @block.vector
        def _(dve):
            dve.wait_ge(ld_xT, 16)
            dve.tensor_copy(xT_hi[:], xT_in[:]).then_inc(x_split, 1)
            dve.wait_ge(x_split, 1)
            dve.tensor_tensor(xT_lo[:], xT_in[:], xT_hi[:].bitcast(f32), ALU.subtract).then_inc(x_split, 1)
            kv_ps = banks[0][:].rearrange("p (t n) -> p t n", t=TILES)
            dve.wait_ge(sq_done, 1)
            dve.tensor_reduce(ms[:], sq[:], AX.X, ALU.add).then_inc(dve_step, 1)
            dve.wait_ge(dve_step, 1)
            dve.tensor_scalar(ms[:], ms[:], 1.0 / RANK, RMS_EPS, ALU.mult, ALU.add).then_inc(ms_done, 1)
            dve.tensor_copy(keys[:, :, RANK:], kv_ps[:, :, RANK:]).then_inc(keys_done, 1)
            dve.wait_ge(rms_done, 1)
            dve.wait_ge(ld_lnw, 16)
            for t in range(TILES):
                dve.scalar_tensor_tensor(keys[:, t, 0:RANK], kv_ps[:, t, 0:RANK], rms[:, t:t + 1], lnw[:],
                                         ALU.mult, ALU.mult).then_inc(keys_done, 1)
            dve.wait_ge(keys_done, TILES + 1)
            dve.tensor_copy(latent[:, :, 0:RANK], keys[:, :, 0:RANK]).then_inc(ones_done, 1)
            dve.wait_ge(kT_ps, 1)
            dve.tensor_copy(kT_hi[:], banks[1][:]).then_inc(k_split, 1)
            dve.wait_ge(k_split, 1)
            dve.tensor_tensor(kT_lo[:], banks[1][:], kT_hi[:].bitcast(f32), ALU.subtract).then_inc(k_split, 1)

            def split_weff(h, u, i):
                dve.wait_ge(weff_f32, h + 1)
                dve.wait_ge(ld_head[u], 64 * (i + 1))
                if not (isinstance(h, int) and h < 2):
                    dve.wait_ge(qT_ps, h - 1)
                dve.tensor_copy(weff_hi[:, u], weff[:, u]).then_inc(dve_w, 1)
                dve.wait_ge(dve_w, h + 1)
                dve.tensor_tensor(weff_lo[:, u], weff[:, u], weff_hi[:, u].bitcast(f32),
                                  ALU.subtract).then_inc(weff_split, 1)

            def wvo_copy(m):
                hold(dve, wvo_ps, 2 * m + 2)
                dve.tensor_copy(wvo[:, bass.ds(m * HID, HID)], misc[:, 0:HID]).then_inc(wvo_done, 1)

            split_weff(0, 0, 0)
            split_weff(1, 1, 0)
            wvo_copy(0)
            with dve.Fori(1, PAIRS) as j:
                split_weff(2 * j, 0, j)
                split_weff(2 * j + 1, 1, j)
                wvo_copy(j)

            def row_max(qt, n, u):
                dve.wait_ge(scores_ready, n + 1)
                dve.tensor_reduce(neg_max[:, u:u + 1], banks[u][:, 0:(qt + 1) * P], AX.X, ALU.max,
                                  negate=True).then_inc(max_ready, 1)

            def copy_pT(qt, n, u):
                if chunks(qt) == 2:
                    dve.wait_ge(pT_ps[1], n + 1 - 4 * HEADS)
                    w = (qt + 1 - 4) * P
                    dve.tensor_copy(probsT[:, u, BANK:BANK + w], pT[1][:, 0:w]).then_inc(pT_done[1], 1)

            def norm_ctx(n, u, m=0):
                dve.wait_ge(ctx_ready, n + 1)
                dve.reciprocal(rsum[:, u:u + 1], ctx_ps[:, RANK:]).then_inc(rsum_done, 1)
                dve.wait_ge(rsum_done, n + 1)
                if u == 0 and not (isinstance(m, int) and m < 1):
                    dve.wait_ge(ctxT_psd, m)
                dve.tensor_scalar(ctx_n[:, u * RANK:(u + 1) * RANK], ctx_ps[:, 0:RANK],
                                  rsum[:, u:u + 1], None, ALU.mult).then_inc(ctx_normed, 1)

            def layernorm(k, src, dst, eps):
                dve.bn_stats(stats[:], src).then_inc(dve_ln, 1)
                hold(dve, dve_ln, 2 * k + 1)
                dve.bn_aggr(mv[:], stats[:]).then_inc(dve_ln, 1)
                dve.wait_ge(dve_ln, 2 * k + 2)
                dve.tensor_scalar(mv[:, 1:2], mv[:, 1:2], eps, None, ALU.add).then_inc(var_done, 1)
                dve.wait_ge(rstd_done, k + 1)
                return dve.tensor_scalar(dst, src, mv[:, 0:1], rstd[:, 0:1], ALU.subtract, ALU.mult)

            def finish_tile(qt):
                dve.wait_ge(acc_ready, (qt + 1) * PAIRS)
                dve.wait_ge(ld_x, 16)
                dve.tensor_tensor(y[:], acc[:, 0:HID], x_in[:, qt, :], ALU.add).then_inc(acc_read, 1)
                dve.wait_ge(acc_read, qt + 1)
                layernorm(qt, y[:], x1[:, qt, :], LN_EPS).then_inc(x1_done, 1)

            def read_place(t):
                dve.wait_ge(place_done, t + 1)
                dve.tensor_copy(place, place_ps).then_inc(place_read, 1)

            def choose(t):
                link = chain(dve, route_step, 13 * t)
                dve.wait_ge(logits_done, t + 1)
                dve.tensor_copy(logits, logits_ps).then_inc(logits_read, 1)
                dve.wait_ge(logits_read, t + 1)
                link(dve.max(top_v[:, t, :], logits))
                link(dve.max_index(top_i[:, t, :], top_v[:, t, :], logits))
                link(dve.match_replace(left, top_v[:, t, :], logits, -3e38))
                link(dve.tensor_tensor(chosen[:, t, :], logits, left, ALU.not_equal))
                if t + 1 < TILES:
                    link(dve.tensor_tensor(chosen_before[:, t + 1, :], chosen_before[:, t, :], chosen[:, t, :], ALU.add))
                else:
                    dve.sem_inc(route_step, 1)
                dve.tensor_copy(top_f[:, t, :], top_i[:, t, :]).then_inc(chosen_done, 1)

            def assign(t):
                link = chain(dve, route_step, 13 * t + 5)
                dve.wait_ge(place_read, t + 1)
                dve.wait_ge(chosen_done, t + 1)
                shape = [P, TOP0, E0]
                link(dve.tensor_tensor(onehot, iota_e[:].unsqueeze(1).broadcast_to(shape),
                                       top_f[:, t, :].unsqueeze(2).broadcast_to(shape), ALU.is_equal))
                link(dve.tensor_tensor(placed, onehot, place.unsqueeze(1).broadcast_to(shape), ALU.mult))
                link(dve.tensor_reduce(place8[:, t, :], placed, AX.X, ALU.add))
                dve.tensor_scalar(valid[:, t, :], place8[:, t, :], float(CAP), None, ALU.is_lt)
                link(dve.tensor_scalar(slot_t[:], place8[:, t, :], float(CAP - 1), None, ALU.min))
                link(dve.scalar_tensor_tensor(slot[:, t, :], top_f[:, t, :], float(CAP), slot_t[:], ALU.mult, ALU.add))
                link(dve.tensor_tensor(slot_t[:], slot[:, t, :], spare[:, t, :], ALU.subtract))
                link(dve.tensor_tensor(slot_t[:], slot_t[:], valid[:, t, :], ALU.mult))
                link(dve.tensor_copy(fetch_i[:, t, :], slot[:, t, :]))
                dve.tensor_tensor(send_i[:, t, :], slot_t[:], spare[:, t, :], ALU.add).then_inc(send_done, 1)

            for qt in range(TILES):
                row_max(qt, nth(qt, 0), 0)
                if qt:
                    copy_pT(qt - 1, nth(qt, -1), 1)
                    norm_ctx(nth(qt, -1), 1)
                row_max(qt, nth(qt, 1), 1)
                if qt >= 3:
                    dve.wait_ge(ctxT_psd, qt * PAIRS)
                    read_place(qt - 3)
                copy_pT(qt, nth(qt, 0), 0)
                norm_ctx(nth(qt, 0), 0, qt * PAIRS)
                if qt:
                    finish_tile(qt - 1)
                if qt == 2:
                    dve.wait_ge(consts0, 4)
                if qt >= 3:
                    assign(qt - 3)
                if qt >= 2:
                    choose(qt - 2)
                with dve.Fori(1, PAIRS) as j:
                    row_max(qt, nth(qt, 2 * j), 0)
                    copy_pT(qt, nth(qt, 2 * j - 1), 1)
                    norm_ctx(nth(qt, 2 * j - 1), 1)
                    row_max(qt, nth(qt, 2 * j + 1), 1)
                    copy_pT(qt, nth(qt, 2 * j), 0)
                    norm_ctx(nth(qt, 2 * j), 0, qt * PAIRS + j)
            copy_pT(TILES - 1, nth(TILES, -1), 1)
            norm_ctx(nth(TILES, -1), 1)
            finish_tile(TILES - 1)
            for t in range(TILES - 2, TILES):
                read_place(t - 1)
                assign(t - 1)
                choose(t)
            read_place(TILES - 1)
            assign(TILES - 1)
            link = chain(dve, route_step, 13 * TILES)
            shape = [P, TILES, TOP0]
            dve.tensor_tensor(weight[:], top_v, top_v[:, :, 0:1].broadcast_to(shape), ALU.subtract).then_inc(exp0, 1)
            dve.wait_ge(exp0, 2)
            link(dve.tensor_reduce(wsum[:], weight[:], AX.X, ALU.add))
            link(dve.reciprocal(wsum[:], wsum[:]))
            link(dve.tensor_tensor(weight[:], weight[:], wsum[:].unsqueeze(2).broadcast_to(shape), ALU.mult))
            dve.tensor_tensor(weight[:], weight[:], valid[:], ALU.mult).then_inc(weight_done, 1)

            def copy_xeT(e, u):
                dve.wait_ge(xeT_ps, e + 1)
                if past(e, 2):
                    dve.wait_ge(gu_ready, e - 1)
                dve.tensor_copy(xeT[:, u % 2], pT[u % 2][:, 0:HID].rearrange("p (c n) -> p c n", c=HC)).then_inc(xeT_done, 1)

            def gated(e, u):
                dve.wait_ge(silu_done, e + 1)
                if past(e, 2):
                    dve.wait_ge(ye_ps, e - 1)
                dve.tensor_tensor(hT[:, u % 2, :], sg[:, u % 2, :], half[u % 2][0:I0, P:2 * P], ALU.mult).then_inc(h_done, 1)

            copy_xeT(0, 0)
            copy_xeT(1, 1)
            gated(0, 0)
            for e in range(RING):
                copy_xeT(e + 2, (e + 2) % RING)
                gated(e + 1, (e + 1) % RING)
            with dve.Fori(1, E0 // RING - 1) as i:
                for u in range(RING):
                    copy_xeT(RING * i + u + 2, (u + 2) % RING)
                    gated(RING * i + u + 1, (u + 1) % RING)
            for e in range(E0 - RING, E0):
                if e + 2 < E0:
                    copy_xeT(e + 2, (e + 2) % RING)
                if e + 1 < E0:
                    gated(e + 1, (e + 1) % RING)
            def combine(t, u, i):
                link = chain(dve, comb_step, (TOP0 - 1) * t)
                dve.wait_ge(gath[u], 16 * TOP0 * (i + 1))
                if isinstance(t, int) and t == 1:
                    dve.wait_ge(x2_done, 1)
                if past(t, 2):
                    dve.wait_ge(x3_done, t - 1)
                for k in range(TOP0):
                    ins = dve.scalar_tensor_tensor(y[:], gathered[:, u, k, :], weight_flat[:, bass.ds(t * TOP0 + k, 1)],
                                                   y[:] if k else x1_flat[:, bass.ds(t * HID, HID)], ALU.mult, ALU.add)
                    if k < TOP0 - 1:
                        link(ins)
                ins.then_inc(combined, 1)
                dve.wait_ge(combined, t + 1)
                layernorm(rank2(t), y[:], x2[:, u, :], LN_EPS).then_inc(x2_done, 1)

            def middle(t, u):
                link = chain(dve, mid_step, 3 * t)
                dve.wait_ge(gates_done, 4 * t + 3)
                link(dve.scalar_tensor_tensor(value[:, u], igate[:, u], 1.0, value[:, u], ALU.add, ALU.mult))
                for c in range(HC):
                    init = init2[:, c:c + 1] if isinstance(t, int) and t == 0 else state[:, 1 - u, c, P - 1:P]
                    link(dve.tensor_tensor_scan(state[:, u, c, :], forget[:, u, c, :], value[:, u, c, :], init,
                                                ALU.mult, ALU.add))
                q = rec_ps[u][1][:, HC * P:].rearrange("p (c n) -> p c n", c=HC)
                dve.tensor_tensor(zq[:, u], state[:, u], q, ALU.mult).then_inc(z_done, 1)
                dve.wait_ge(gates_done, 4 * t + 4)
                if past(t, 2):
                    dve.wait_ge(mix_ready, t - 1)
                up = rec_ps[u][2][:, 0:HC * P].rearrange("p (c n) -> p c n", c=HC)
                dve.tensor_tensor(local[:, u], lgate[:, u], up, ALU.mult).then_inc(lu_done, 1)

            def finish_mix(t, u):
                dve.wait_ge(mix_ready, t + 1)
                dve.wait_ge(x2_done, min(t + 2, TILES) if isinstance(t, int) else t + 2)
                dve.tensor_tensor(y[:], acc[:, 0:HID], x2[:, u, :], ALU.add).then_inc(mix_read, 1)
                dve.wait_ge(mix_read, t + 1)
                layernorm(rank3(t), y[:], x1_flat[:, bass.ds(t * HID, HID)], LN_EPS).then_inc(x3_done, 1)

            weight_flat = weight[:].rearrange("p t k -> p (t k)")
            x1_flat = x1[:].rearrange("p t n -> p (t n)")
            dve.wait_ge(ld_init, 16)
            dve.tensor_scalar(init2[:], init2[:], 2.0, None, ALU.mult).then_inc(init_done, 1)
            dve.wait_ge(weight_done, 1)
            dve.wait_ge(init_done, 1)
            combine(0, 0, 0)
            combine(1, 1, 0)
            middle(0, 0)
            finish_mix(0, 0)
            with dve.Fori(1, TILES // 2) as i:
                for u in range(2):
                    combine(2 * i + u, u, i)
                    middle(2 * i + u - 1, 1 - u)
                    finish_mix(2 * i + u - 1, 1 - u)
            middle(TILES - 1, 1)
            finish_mix(TILES - 1, 1)
            for b in range(2):
                dve.wait_ge(x3T_ps, b + 3)
                dve.tensor_copy(x3T[:, 1, b * BANK:(b + 1) * BANK], half[2 + b]).then_inc(x3T_done, 1)

            link = chain(dve, d_step)
            dve.wait_ge(lg1_ready, 1)
            dve.wait_ge(consts1, 4)
            link(dve.tensor_copy(lg1[:], misc[:, 0:TILES * E1].rearrange("p (t e) -> p t e", t=TILES)))
            for t in range(TILES):
                ins = dve.max(tv1[:, t, :], lg1[:, t, :])
            link(ins)
            for t in range(TILES):
                ins = dve.max_index(ti1[:, t, :], tv1[:, t, :], lg1[:, t, :])
            link(ins)
            dve.tensor_tensor(weight1[:, :, 0:1], tv1[:, :, 1:2], tv1[:, :, 0:1], ALU.subtract).then_inc(tanh1, 1)
            link(dve.tensor_copy(tf1[:], ti1[:]))
            sh4 = [P, TILES, E1]
            for k in range(TOP1):
                link(dve.tensor_tensor(oh1[:, :, k, :], iota_e[:, 0:E1].unsqueeze(1).broadcast_to(sh4),
                                       tf1[:, :, k:k + 1].broadcast_to(sh4), ALU.is_equal))
            link(dve.tensor_tensor(ch1[:], oh1[:, :, 0, :], oh1[:, :, 1, :], ALU.add))
            for t in range(TILES):
                link(dve.tensor_tensor(cb1[:, t + 1, :], cb1[:, t, :], ch1[:, t, :], ALU.add))
            dve.sem_inc(ch1_done, 1)
            dve.wait_ge(pl1_ready, 1)
            link(dve.tensor_copy(pl1[:], acc[:, 0:(TILES + 1) * E1].rearrange("p (t e) -> p t e", e=E1)))
            sh5 = [P, E1, TILES]
            link(dve.tensor_tensor(blk_cmp[:], pl1[:, TILES, :].unsqueeze(2).broadcast_to(sh5),
                                   iota_r[:].unsqueeze(1).broadcast_to(sh5), ALU.is_gt))
            link(dve.tensor_reduce(nblk[:], blk_cmp[:], AX.X, ALU.add))
            link(dve.tensor_tensor_scan(blk_end[:], ones_e[:], nblk[:], 0.0, ALU.mult, ALU.add))
            link(dve.tensor_tensor(blk_start[:], blk_end[:], nblk[:], ALU.subtract))
            link(dve.tensor_scalar(blk_start[:], blk_start[:], float(P), None, ALU.mult))
            link(dve.tensor_tensor(pl1[:, 0:TILES, :], pl1[:, 0:TILES, :],
                                   blk_start[:].unsqueeze(1).broadcast_to(sh4), ALU.add))
            for k in range(TOP1):
                link(dve.tensor_tensor(oh1[:, :, k, :], oh1[:, :, k, :], pl1[:, 0:TILES, :], ALU.mult))
            link(dve.tensor_reduce(sl1[:], oh1[:], AX.X, ALU.add))
            dve.tensor_copy(slot1[:], sl1[:]).then_inc(slots1_ready, 1)
            sh6 = [P, BLOCKS, E1]
            link(dve.tensor_tensor(own_cmp[:], blk_end[:].unsqueeze(1).broadcast_to(sh6),
                                   iota_b[:].unsqueeze(2).broadcast_to(sh6), ALU.is_le))
            link(dve.tensor_reduce(owner[:], own_cmp[:], AX.X, ALU.add))
            dve.tensor_scalar(owner_i[:], owner[:], float(E1 - 1), None, ALU.min).then_inc(slots1_ready, 1)
            dve.wait_ge(tanh1, 2)
            link(dve.tensor_scalar(weight1[:, :, 0:1], weight1[:, :, 1:2], -0.5, 0.5, ALU.mult, ALU.add))
            link(dve.tensor_scalar(weight1[:, :, 1:2], weight1[:, :, 1:2], 0.5, 0.5, ALU.mult, ALU.add))

            for b in range(2):
                for c in range(SC):
                    n = b * SC + c
                    dve.wait_ge(gs_silu, n + 1)
                    dve.tensor_tensor(hs[:, c, :], sgd[:, n % 2, :], half[2 + n % 2], ALU.mult).then_inc(hs_done, 1)
                for q in range(4):
                    t = 4 * b + q
                    dve.wait_ge(sh_ready, t + 1)
                    dve.tensor_tensor(shared[:, t, :], pT[q % 2][:, 0:HID], x1[:, t, :], ALU.add).then_inc(sh_read, 1)

            def block_gated(i, u):
                dve.wait_ge(sgd_done, i + 1)
                if past(i, 1):
                    dve.wait_ge(hdT_ps, i)
                dve.tensor_tensor(hd, sgd[:, u, :], half[2 * u + 1], ALU.mult).then_inc(hd_done, 1)

            def block_hT(i, u):
                dve.wait_ge(hdT_ps, i + 1)
                if past(i, 2):
                    dve.wait_ge(yd_ps, i - 1)
                dve.tensor_copy(hdT[:, u, :], pT[u][:]).then_inc(hdT_done, 1)

            def block_dve(i, u):
                block_gated(i, u)
                block_hT(i, u)

            blocks_two(dve, block_dve)
            for t in range(TILES):
                link = chain(dve, final_step, 1 * t)
                dve.wait_ge(last_in[t], 16 * TOP1)
                if t:
                    dve.wait_ge(result_done, t)
                link(dve.scalar_tensor_tensor(y[:], last_rows[:, t, 0, :], weight1[:, t, 0:1], shared[:, t, :],
                                              ALU.mult, ALU.add))
                dve.scalar_tensor_tensor(y[:], last_rows[:, t, 1, :], weight1[:, t, 1:2], y[:],
                                         ALU.mult, ALU.add).then_inc(last_go, 1)
                dve.wait_ge(last_go, t + 1)
                if t >= 2:
                    dve.wait_ge(st_out[t % 2], 16 * (t // 2))
                layernorm(3 * TILES + t, y[:], result[:, t % 2, :], LN_EPS).then_inc(result_done, 1)

        @block.tensor
        def _(pe):
            def product3(out_ap, lhs, rhs, start, stop):
                (lh, ll), (rh, rl) = lhs, rhs
                pe.matmul(out_ap, lh, rh, start=start, stop=False)
                pe.matmul(out_ap, lh, rl, start=False, stop=False)
                return pe.matmul(out_ap, ll, rh, start=False, stop=stop)

            pe.wait_ge(ld_xT, 16)
            pe.wait_ge(ld_kv, 16)
            for t in range(TILES):
                for c in range(HC):
                    last = pe.matmul(banks[0][:, t * P:(t + 1) * P], xT_in[:, c, t * P:(t + 1) * P], wkv_a[:, c, :],
                                     start=c == 0, stop=c == HC - 1)
            last.then_inc(kv_ready, 1)
            pe.wait_ge(consts, 1)
            pe.wait_ge(keys_done, TILES + 1)
            for t in range(TILES):
                last = pe.transpose(banks[1][:, t * P:(t + 1) * P], keys[:, t, :], ident[:])
            last.then_inc(kT_ps, 1)

            def absorb(h, u, i):
                pe.wait_ge(ld_head[u], 64 * (i + 1))
                if not (isinstance(h, int) and h < 2):
                    pe.wait_ge(weff_f32, h - 1)
                for c in range(HC):
                    last = pe.matmul(pT[u][:, c * RANK:(c + 1) * RANK], wq_h[:, u, c * P:(c + 1) * P],
                                     wkb[:, bass.ds(h, 1), :], start=True, stop=True)
                last.then_inc(weff_ps, 1)
                if u == 0 and not (isinstance(i, int) and i < 1):
                    pe.wait_ge(wvo_done, i)
                pe.matmul(misc[u * RANK:(u + 1) * RANK, 0:HID], wv_h[:, u, :], wo_h[:, u, :],
                          start=True, stop=True).then_inc(wvo_ps, 1)

            def project_q(h, u):
                pe.wait_ge(weff_split, h + 1)
                if not (isinstance(h, int) and h < 2):
                    pe.wait_ge(qT_done, h - 1)
                for b in range(2):
                    for c in range(HC):
                        last = product3(banks[u][:, b * BANK:(b + 1) * BANK],
                                        (weff_hi[:, u, c, :], weff_lo[:, u, c, :]),
                                        (xT_hi[:, c, b * BANK:(b + 1) * BANK], xT_lo[:, c, b * BANK:(b + 1) * BANK]),
                                        c == 0, c == HC - 1)
                last.then_inc(qT_ps, 1)

            pe.wait_ge(ld_wkb, 16)
            absorb(0, 0, 0)
            absorb(1, 1, 0)
            pe.wait_ge(x_split, 2)
            pe.wait_ge(k_split, 2)
            project_q(0, 0)
            with pe.Fori(1, PAIRS) as j:
                absorb(2 * j, 0, j)
                project_q(2 * j - 1, 1)
                absorb(2 * j + 1, 1, j)
                project_q(2 * j, 0)
            project_q(HEADS - 1, 1)
            pe.wait_ge(qT_done, HEADS)
            pe.wait_ge(weff_f32, HEADS)
            pe.wait_ge(wvo_done, PAIRS)

            def scores(qt, n, u):
                pe.wait_ge(q_split, n + 1)
                if not (isinstance(n, int) and n < 2):
                    pe.wait_ge(probs_ready, n - 1)
                L = (qt + 1) * P
                for b in range(0, L, BANK):
                    w = min(BANK, L - b)
                    diag = b + w == L
                    last = product3(banks[u][:, b:b + w], (q_hi[:, u, :], q_lo[:, u, :]),
                                    (kT_hi[:, b:b + w], kT_lo[:, b:b + w]), True, not diag)
                    if diag:
                        last = pe.matmul(banks[u][:, L - P:L], ident_bf[:], causal[:], start=False, stop=True)
                last.then_inc(scores_ready, 1)

            def context(qt, n, u, m=0):
                pe.wait_ge(probs_ready, n + 1)
                for c in range(chunks(qt)):
                    bank = pT[u if chunks(qt) == 1 else c]
                    for k in range(4 * c, min(qt + 1, 4 * c + 4)):
                        last = pe.transpose(bank[:, (k % 4) * P:(k % 4 + 1) * P], probs[:, u, k * P:(k + 1) * P],
                                            ident[:])
                    last.then_inc(pT_ps[c], 1)
                pe.wait_ge(pT_done[0], n + 1)
                if not (isinstance(n, int) and n < 1):
                    pe.wait_ge(ctx_normed, n)
                if u == 0 and not (isinstance(m, int) and m < 1):
                    pe.wait_ge(ctxT_done, m)
                for k in range(qt + 1):
                    if k == 4:
                        pe.wait_ge(pT_done[1], n + 1 - 4 * HEADS)
                    last = pe.matmul(ctx_ps, probsT[:, u, k * P:(k + 1) * P], latent[:, k, :],
                                     start=k == 0, stop=k == qt)
                last.then_inc(ctx_ready, 1)


            def transpose_ctx(m):
                pe.wait_ge(ctx_normed, 2 * m + 2)
                pe.transpose(ctxT_ps, ctx_n[:], ident[:]).then_inc(ctxT_psd, 1)

            def output(m, j):
                pe.wait_ge(ctxT_done, m + 1)
                pe.matmul(acc[:, 0:HID], ctxT[:], wvo[:, bass.ds(j * HID, HID)], start=False,
                          stop=isinstance(j, int)).then_inc(acc_ready, 1)

            def transpose_x1(t):
                pe.wait_ge(x1_done, t + 1)
                for c in range(HC):
                    last = pe.transpose(x1T_ps[:, c * P:(c + 1) * P], x1[:, t, c * P:(c + 1) * P], ident[:])
                last.then_inc(x1T_psd, 1)

            def route(t):
                pe.wait_ge(x1T_done, t + 1)
                for c in range(HC):
                    last = pe.matmul(logits_ps, x1T[:, c, :], router0[:, c, :], start=c == 0, stop=c == HC - 1)
                last.then_inc(logits_done, 1)

            def count_places(t):
                pe.wait_ge(chosen_done, t + 1)
                pe.matmul(place_ps, ones_bf[:], chosen_before[:, t, :], start=True, stop=False)
                pe.matmul(place_ps, earlier[:], chosen[:, t, :], start=False, stop=True).then_inc(place_done, 1)

            for qt in range(TILES):
                scores(qt, nth(qt, 0), 0)
                if qt:
                    context(qt - 1, nth(qt, -1), 1)
                scores(qt, nth(qt, 1), 1)
                if qt >= 2:
                    pe.wait_ge(ctx_normed, nth(qt, 0))
                    transpose_x1(qt - 2)
                if qt >= 3:
                    count_places(qt - 3)
                if qt:
                    transpose_ctx(qt * PAIRS - 1)
                if qt >= 3:
                    pe.wait_ge(place_read, qt - 2)
                if qt >= 2:
                    pe.wait_ge(x1T_done, qt - 1)
                context(qt, nth(qt, 0), 0, qt * PAIRS)
                if qt:
                    output(qt * PAIRS - 1, PAIRS - 1)
                    pe.wait_ge(acc_read, qt)
                if qt >= 2:
                    pe.wait_ge(ctx_normed, nth(qt, 0) + 1)
                    pe.wait_ge(ld_router0, 16)
                    route(qt - 2)
                    pe.wait_ge(logits_read, qt - 1)
                pe.matmul(acc[:, 0:HID], zeros_bf[:, 0:P], zeros_bf[:], start=True, stop=False)
                with pe.Fori(1, PAIRS) as j:
                    scores(qt, nth(qt, 2 * j), 0)
                    context(qt, nth(qt, 2 * j - 1), 1)
                    scores(qt, nth(qt, 2 * j + 1), 1)
                    transpose_ctx(qt * PAIRS + j - 1)
                    context(qt, nth(qt, 2 * j), 0, qt * PAIRS + j)
                    output(qt * PAIRS + j - 1, j - 1)
            context(TILES - 1, nth(TILES, -1), 1)
            transpose_ctx(TILES * PAIRS - 1)
            output(TILES * PAIRS - 1, PAIRS - 1)
            pe.wait_ge(ctxT_done, TILES * PAIRS)
            for t in range(TILES - 2, TILES):
                count_places(t - 1)
                pe.wait_ge(place_read, t)
                transpose_x1(t)
                route(t)
                pe.wait_ge(logits_read, t + 1)
            count_places(TILES - 1)

            def transpose_rows(e, u):
                pe.wait_ge(ld_xe[u // 2], turn(e, u))
                if past(e, 2):
                    pe.wait_ge(xeT_done, e - 1)
                for c in range(HC):
                    last = pe.transpose(pT[u % 2][:, c * P:(c + 1) * P], xe[:, u, c * P:(c + 1) * P], ident[:])
                last.then_inc(xeT_ps, 1)

            def gate_up(e, u):
                b = u % 2
                pe.wait_ge(xeT_done, e + 1)
                pe.wait_ge(ld_gu[u // 2], turn(e, u))
                if past(e, 2):
                    pe.wait_ge(h_done, e - 1)
                for part in range(2):
                    for c in range(HC):
                        last = pe.matmul(half[b][0:I0, part * P:(part + 1) * P],
                                         gu_w[:, u, c, part * I0:(part + 1) * I0], xeT[:, b, c, :],
                                         start=c == 0, stop=c == HC - 1)
                last.then_inc(gu_ready, 1)

            def down(e, u):
                b = u % 2
                pe.wait_ge(h_done, e + 1)
                pe.wait_ge(ld_dn[u // 2], turn(e, u))
                if past(e, 2):
                    pe.wait_ge(ye_done, e - 1)
                pe.matmul(half[2 + b][:, 0:HID], hT[:, b, :], dn_w[:, u, :], start=True, stop=True).then_inc(ye_ps, 1)

            transpose_rows(0, 0)
            transpose_rows(1, 1)
            gate_up(0, 0)
            for e in range(RING):
                transpose_rows(e + 2, (e + 2) % RING)
                gate_up(e + 1, (e + 1) % RING)
                down(e, e)
            with pe.Fori(1, E0 // RING - 1) as i:
                for u in range(RING):
                    transpose_rows(RING * i + u + 2, (u + 2) % RING)
                    gate_up(RING * i + u + 1, (u + 1) % RING)
                    down(RING * i + u, u)
            for e in range(E0 - RING, E0):
                if e + 2 < E0:
                    transpose_rows(e + 2, (e + 2) % RING)
                if e + 1 < E0:
                    gate_up(e + 1, (e + 1) % RING)
                down(e, e % RING)
            def transpose_x2(t, u):
                pe.wait_ge(x2_done, t + 1)
                for c in range(HC):
                    last = pe.transpose(misc[:, c * P:(c + 1) * P], x2[:, u, c * P:(c + 1) * P], ident[:])
                last.then_inc(x2T_psd, 1)

            def project(t, u):
                pe.wait_ge(x2T_done, t + 1)
                if past(t, 2):
                    pe.wait_ge(lu_done, t - 1)
                for m in range(6):
                    bank = rec_ps[u][m // 2]
                    for r in range(HC):
                        o = (m % 2) * HC * P + r * P
                        for c in range(HC):
                            last = pe.matmul(bank[:, o:o + P], w_c[:, m, c, r * P:(r + 1) * P], x2T[:, u, c, :],
                                             start=c == 0, stop=c == HC - 1)
                    if m % 2:
                        last.then_inc((fi_ready, vq_ready, ug_ready)[m // 2], 1)

            def mix(t, u):
                pe.wait_ge(r_done, t + 1)
                pe.wait_ge(lu_done, t + 1)
                if past(t, 1):
                    pe.wait_ge(mix_read, t)
                for m, src in enumerate((readout, local)):
                    for c in range(HC):
                        last = pe.matmul(acc[:, 0:HID], src[:, u, c, :], wo_c[:, m, c, :], start=m + c == 0,
                                         stop=m + c == HC)
                last.then_inc(mix_ready, 1)

            pe.wait_ge(ld_wc, 16)
            pe.wait_ge(ld_woc, 16)
            pe.wait_ge(ye_done, E0)
            transpose_x2(0, 0)
            project(0, 0)
            transpose_x2(1, 1)
            project(1, 1)
            mix(0, 0)
            with pe.Fori(1, TILES // 2) as i:
                for u in range(2):
                    transpose_x2(2 * i + u, u)
                    project(2 * i + u, u)
                    mix(2 * i + u - 1, 1 - u)
            mix(TILES - 1, 1)

            pe.wait_ge(x3_done, TILES)
            for c in range(HC):
                for t in range(TILES):
                    last = pe.transpose(half[2 * c + t // 4][:, t % 4 * P:(t % 4 + 1) * P],
                                        x1[:, t, c * P:(c + 1) * P], ident[:])
                    if t % 4 == 3:
                        last.then_inc(x3T_ps, 1)
            pe.wait_ge(x3T_done, 4)
            pe.wait_ge(ld_router1, 16)
            for t in range(TILES):
                for c in range(HC):
                    last = pe.matmul(misc[:, t * E1:(t + 1) * E1], x3T[:, c, t * P:(t + 1) * P], router1_s[:, c, :],
                                     start=c == 0, stop=c == HC - 1)
            last.then_inc(lg1_ready, 1)
            pe.wait_ge(ch1_done, 1)
            n = TILES * E1
            pe.matmul(acc[:, 0:n], ones_bf[:], cb1[:, 0:TILES, :].rearrange("p t e -> p (t e)"), start=True, stop=False)
            pe.matmul(acc[:, 0:n], earlier[:], ch1[:].rearrange("p t e -> p (t e)"), start=False, stop=True)
            pe.matmul(acc[:, n:n + E1], ones_bf[:], cb1[:, TILES, :], start=True, stop=True).then_inc(pl1_ready, 1)
            pe.wait_ge(ld_sh, 48)
            for b in range(2):
                for k in range(SC):
                    n = b * SC + k
                    if n >= 2:
                        pe.wait_ge(hs_done, n - 1)
                    for bank, w in ((half[n % 2], sh_g), (half[2 + n % 2], sh_u)):
                        for c in range(HC):
                            last = pe.matmul(bank, w[:, c, k * P:(k + 1) * P], x3T[:, c, b * BANK:(b + 1) * BANK],
                                             start=c == 0, stop=c == HC - 1)
                    last.then_inc(gs_ready, 1)
                pe.wait_ge(hs_done, (b + 1) * SC)
                for q in range(4):
                    if 4 * b + q >= 2:
                        pe.wait_ge(sh_read, 4 * b + q - 1)
                    for k in range(SC):
                        last = pe.matmul(pT[q % 2][:, 0:HID], hs[:, k, q * P:(q + 1) * P], sh_d[:, k, :],
                                         start=k == 0, stop=k == SC - 1)
                    last.then_inc(sh_ready, 1)

            def block_T(i, u):
                pe.wait_ge(ld_xd[u], 8 * (i - u) + 16)
                if past(i, 1):
                    pe.wait_ge(xdT_done, i)
                for c in range(HC):
                    last = pe.transpose(misc[:, c * P:(c + 1) * P], xd[:, u, c * P:(c + 1) * P], ident[:])
                last.then_inc(xdT_ps, 1)

            def owner_of(i):
                return pe.value_load(owner_i[0:1, bass.ds(i, 1)], min_val=0, max_val=E1 - 1)

            def block_in(i, u):
                pe.wait_ge(xdT_done, i + 1)
                if past(i, 2):
                    pe.wait_ge(hd_done, i - 1)
                pe.sem_inc(passed, 1)
                e = owner_of(i)
                for part in range(2):
                    for c in range(HC):
                        last = pe.matmul(half[2 * u + part], xdT[:, u, c, :],
                                         w1_s[:, bass.ds(e * (HC * 2 * I1) + (c * 2 * I1 + part * I1), I1)],
                                         start=c == 0, stop=c == HC - 1)
                last.then_inc(f1_ready, 1)

            def block_hT(i, u):
                pe.wait_ge(hd_done, i + 1)
                if past(i, 2):
                    pe.wait_ge(hdT_done, i - 1)
                for c in range(I1 // P):
                    last = pe.transpose(pT[u][:, c * P:(c + 1) * P], hd[:, c * P:(c + 1) * P], ident[:])
                last.then_inc(hdT_ps, 1)

            def block_out(i, u):
                pe.wait_ge(hdT_done, i + 1)
                if past(i, 1):
                    pe.wait_ge(yd_done, i)
                pe.sem_inc(passed, 1)
                e = owner_of(i)
                for c in range(I1 // P):
                    last = pe.matmul(acc[:, 0:HID], hdT[:, u, c * P:(c + 1) * P],
                                     w2_s[:, bass.ds(e * (I1 * HID // P) + c * HID, HID)],
                                     start=c == 0, stop=c == I1 // P - 1)
                last.then_inc(yd_ps, 1)

            def block_pe(i, u):
                if not (isinstance(i, int) and i >= BLOCKS - 2):
                    block_T(i + 2, u)
                block_hT(i, u)
                if not (isinstance(i, int) and i >= BLOCKS - 1):
                    block_in(i + 1, 1 - u)
                block_out(i, u)

            pe.wait_ge(slots1_ready, 2)
            pe.wait_ge(sh_read, TILES)
            pe.wait_ge(ld_w1, 16 * E1)
            pe.wait_ge(ld_w2, 16 * E1)
            block_T(0, 0)
            block_in(0, 0)
            block_T(1, 1)
            block_pe(0, 0)
            block_pe(1, 1)
            with pe.Fori(1, BLOCKS // 2 - 1) as i:
                for u in range(2):
                    block_pe(2 * i + u, u)
            for i in range(BLOCKS - 3, BLOCKS):
                block_pe(i, i % 2)


def kernel(**inputs):
    import numpy as np
    import concourse.bacc as bacc
    from concourse import mybir as mb
    from concourse.bass_utils import run_bass_kernel_spmd as run

    def arr(name):
        return np.asarray(inputs[name])

    wq = arr("L0_attn_q_proj_w")
    laid_out = {
        "x": arr("L0_attn_hidden_states").reshape(T, HID),
        "xT": arr("L0_attn_hidden_states").reshape(T, HID).T,
        "wq": wq,
        "wq_ropeT": wq.reshape(HEADS, QDIM, HID)[:, NOPE:].transpose(2, 0, 1).reshape(HID, HEADS * ROPE),
        "wkv_aT": arr("L0_attn_kv_a_proj_w").T,
        "kv_ln": arr("L0_attn_kv_a_ln_w"),
        "wkv_b": arr("L0_attn_kv_b_proj_w"),
        "woT": arr("L0_attn_o_proj_w").T,
        "router0T": arr("L0_ffn_router_weight").T,
        "gate_up0": arr("L0_ffn_gate_up_proj"),
        "down0": arr("L0_ffn_down_proj"),
        "w_in": np.stack([arr(f"L1_attn_w_{n}") for n in ("f", "i", "v", "q", "up", "gate")]),
        "init_state": arr("L1_attn_init_state").reshape(HC, P).T,
        "w_mix": np.stack([arr("L1_attn_w_ro"), arr("L1_attn_w_down")]),
        "router1": arr("L1_ffn_router_w"),
        "w1": arr("L1_ffn_w1"),
        "w2": arr("L1_ffn_w2"),
        "sh_gate": arr("L1_ffn_w_gate"),
        "sh_up": arr("L1_ffn_w_up"),
        "sh_down": arr("L1_ffn_w_down"),
    }
    nc = bacc.Bacc("TRN2", target_bir_lowering=False, num_devices=1)
    arrays, args = {}, {}
    for name, a in laid_out.items():
        a = np.ascontiguousarray(a)
        arrays[name] = a
        args[name] = nc.dram_tensor(name, a.shape, mb.dt.from_np(a.dtype), kind="ExternalInput").ap()
    out = nc.dram_tensor("result", (T, HID), mb.dt.float32, kind="ExternalOutput").ap()
    build(nc, out=out, **args)
    r = run(nc, [arrays], core_ids=[0])
    return r.results[0]["result"].reshape(1, T, HID)
```

```python
import concourse.bass as bass
from concourse import mybir
from contextlib import ExitStack

P = 128
T, HID = 1024, 256
TILES = T // P
HC = HID // P
HEADS, NOPE, ROPE, VDIM, RANK = 16, 128, 64, 128, 64
QDIM = NOPE + ROPE
PAIRS = HEADS // 2
LN_EPS, RMS_EPS = 1e-5, 1e-6
BANK = 512
MASKED = -1e30
E0, TOP0, CAP, I0 = 64, 8, 128, 96
SLOTS = E0 * CAP
E1, TOP1, I1, SH = 8, 2, 512, 1024
FREE = 3
BLOCKS = T * TOP1 // P + E1 - 1
ZEROINGS = SLOTS // T + -(-BLOCKS * P // T)


def build(nc, x, xT, wq, wq_ropeT, wkv_aT, kv_ln, wkv_b, woT, router0T, gate_up0, down0, w_in, init_state,
          w_mix, router1, w1, w2, sh_gate, sh_up, sh_down, out):
    f32, f32r, bf16, i32, u32 = (mybir.dt.float32, mybir.dt.float32r, mybir.dt.bfloat16,
                                 mybir.dt.int32, mybir.dt.uint32)
    ALU, ACT, AX = mybir.AluOpType, mybir.ActivationFunctionType, mybir.AxisListType
    ctx = ExitStack()
    with ctx:
        def sb(name, shape, dt=f32):
            return ctx.enter_context(nc.sbuf_tensor(name, shape, dt))

        def sem(name):
            return ctx.enter_context(nc.semaphore(name))

        def carve(area):
            at = [0]

            def cut(*dims):
                n = 1
                for d in dims:
                    n *= d
                piece = area[:, at[0]:at[0] + n]
                at[0] += n
                if len(dims) == 2:
                    piece = piece.rearrange("p (a b) -> p a b", a=dims[0])
                elif len(dims) == 3:
                    piece = piece.rearrange("p (a b c) -> p a b c", a=dims[0], b=dims[1])
                return piece
            return cut

        area1 = sb("area1", [P, HEADS * T])
        area2 = sb("area2", [P, 4 * HC * T])
        area3 = sb("area3", [P, 8192])
        area4 = sb("area4", [P, 6144])
        cutA2, cutA3, cutB4 = carve(area2), carve(area3), carve(area4)
        cutB3, cutC2, cutC3, cutD3, cutD4 = (carve(a) for a in (area3, area2, area3, area3, area4))
        ident = sb("ident", [P, P])
        ident_bf = sb("ident_bf", [P, P], bf16)
        causal = sb("causal", [P, P], bf16)
        minus_half = sb("minus_half", [P, TILES])
        x_in = cutA2(TILES, HID)
        xT_in = cutA2(HC, T)
        xT_hi = sb("xT_hi", [P, HC, T], f32r)
        xT_lo = sb("xT_lo", [P, HC, T], f32r)
        wkv_a = cutA3(HC, P)
        lnw = sb("lnw", [P, RANK])
        wkb = cutA3(HEADS, RANK)
        wq_h = cutA3(2, HID)
        wv_h = cutA3(2, RANK)
        wo_h = cutA3(2, HID)
        weff = cutA3(2, HC, P)
        weff_hi = sb("weff_hi", [P, 2, HC, P], f32r)
        weff_lo = sb("weff_lo", [P, 2, HC, P], f32r)
        wvo = cutA3(PAIRS * HID)
        qT = area1
        q_hi = sb("q_hi", [P, 2, P], f32r)
        q_lo = sb("q_lo", [P, 2, P], f32r)
        sq = cutA3(TILES, RANK)
        ms = sb("ms", [P, TILES])
        rms = sb("rms", [P, TILES])
        keys = cutA3(TILES, P)
        latent = cutA3(TILES, RANK + 1)
        kT_hi = sb("kT_hi", [P, T], f32r)
        kT_lo = sb("kT_lo", [P, T], f32r)
        neg_max = sb("neg_max", [P, 2])
        probs = cutA2(2, T)
        probsT = cutA2(2, T)
        rsum = sb("rsum", [P, 2])
        ctx_n = sb("ctx_n", [P, P])
        ctxT = sb("ctxT", [P, P])
        y = sb("y", [P, HID])
        zeros_bf = sb("zeros_bf", [P, HID], bf16)
        stats = sb("stats", [P, 6])
        mv = sb("mv", [P, 2])
        rstd = sb("rstd", [P, 1])
        x1 = sb("x1", [P, TILES, HID])

        zero_rows = area4[:, 6144 - 2 * T:]
        cutB4b = carve(area4[:, 1024:])
        router0 = sb("router0", [P, HC, E0])
        earlier = sb("earlier", [P, P], bf16)
        ones_bf = sb("ones_bf", [P, P], bf16)
        iota_e = sb("iota_e", [P, E0])
        spare = cutB4(TILES, TOP0)
        x1T = sb("x1T", [P, HC, P])
        logits = cutB4(E0)
        left = cutB4(E0)
        top_v = cutB4(TILES, TOP0)
        top_i = sb("top_i", [P, TILES, TOP0], u32)
        top_f = cutB4(TILES, TOP0)
        chosen = sb("chosen", [P, TILES, E0], bf16)
        chosen_before = sb("chosen_before", [P, TILES, E0], bf16)
        place = cutB4(E0)
        onehot = wkb.rearrange("p h r -> p (h r)")[:, 0:TOP0 * E0].rearrange("p (a b) -> p a b", a=TOP0)
        placed = wkb.rearrange("p h r -> p (h r)")[:, TOP0 * E0:].rearrange("p (a b) -> p a b", a=TOP0)
        place8 = cutB4(TILES, TOP0)
        valid = sb("valid", [P, TILES, TOP0])
        slot = cutB4(TILES, TOP0)
        slot_t = sb("slot_t", [P, TOP0])
        send_i = sb("send_i", [P, TILES, TOP0], i32)
        fetch_i = sb("fetch_i", [P, TILES, TOP0], i32)
        weight = sb("weight", [P, TILES, TOP0])
        wsum = sb("wsum", [P, TILES])
        RING = 8
        gu_w = cutB4b(RING * HC * 2 * I0).rearrange("p (e c n) -> p e c n", e=RING, c=HC)
        dn_w = cutB4b(RING, HID)[0:I0]
        xe = cutB3(RING, HID)
        xeT = cutB3(2, HC, P)
        sg = cutB3(2, P)[0:I0]
        hT = cutB3(2, P)[0:I0]
        ye = cutB3(RING, HID)
        gathered = cutC2(2, TOP0, HID)
        w_c = cutC2(6, HC, HID)
        wo_c = cutC2(2, HC, HID)
        x2 = cutC3(2, HID)
        forget, igate, value, lgate, state, zq, readout, local = (cutC3(2, HC, P) for _ in range(8))
        x2T = cutC3(2, HC, P)
        init2 = sb("init2", [P, HC])
        send_now = sb("send_now", [P, 2], i32)
        fetch_now = sb("fetch_now", [P, 2, TOP0], i32)
        w1_s = area1
        w2_s = area2
        last_rows = area1[:, 0:TILES * TOP1 * HID].rearrange("p (t k n) -> p t k n", t=TILES, k=TOP1)
        sh_g, sh_u, sh_d = cutD4(HC, SH), cutD4(HC, SH), cutD4(SH // P, HID)
        shared = cutD3(TILES, HID)
        x3T = cutD3(HC, T)
        SC = SH // P
        hs = cutD3(SC, BANK)
        cutE3 = carve(area3[:, TILES * HID + HC * T:])
        xd, xdT = cutE3(2, HID), cutE3(2, HC, P)
        hd, hdT, yd = cutE3(BANK), cutE3(2, BANK), cutE3(2, HID)
        sgd = sb("sgd", [P, 2, BANK])
        router1_s = sb("router1_s", [P, HC, E1])
        iota_b = sb("iota_b", [P, BLOCKS])
        iota_r = sb("iota_r", [P, TILES])
        lg1 = sb("lg1", [P, TILES, E1])
        tv1 = sb("tv1", [P, TILES, E1])
        ti1 = sb("ti1", [P, TILES, E1], u32)
        tf1 = sb("tf1", [P, TILES, E1])
        oh1 = sb("oh1", [P, TILES, TOP1, E1])
        ch1 = sb("ch1", [P, TILES, E1], bf16)
        cb1 = sb("cb1", [P, TILES + 1, E1], bf16)
        pl1 = sb("pl1", [P, TILES + 1, E1])
        blk_cmp = sb("blk_cmp", [P, E1, TILES])
        nblk = sb("nblk", [P, E1])
        ones_e = sb("ones_e", [P, E1])
        blk_end = sb("blk_end", [P, E1])
        blk_start = sb("blk_start", [P, E1])
        own_cmp = sb("own_cmp", [P, BLOCKS, E1])
        owner = sb("owner", [P, BLOCKS])
        owner_i = sb("owner_i", [P, BLOCKS], i32)
        sl1 = sb("sl1", [P, TILES, TOP1])
        slot1 = sb("slot1", [P, TILES, TOP1], i32)
        weight1 = sb("weight1", [P, TILES, TOP1])
        result = area1[:, TILES * TOP1 * HID:(TILES * TOP1 + 2) * HID].rearrange("p (a n) -> p a n", a=2)
        xd_d = nc.dram_tensor("xd_d", (BLOCKS * P, HID), f32).ap()
        yd_d = nc.dram_tensor("yd_d", (BLOCKS * P, HID), f32).ap()
        xe_d = nc.dram_tensor("xe_d", (SLOTS + T * TOP0, HID), f32).ap()
        ye_d = nc.dram_tensor("ye_d", (SLOTS, HID), f32).ap()

        banks = [ctx.enter_context(nc.psum_tensor(f"scores{u}", [P, 2 * BANK], f32)) for u in range(2)]
        pT = [ctx.enter_context(nc.psum_tensor(f"probsT_ps{u}", [P, BANK], f32)) for u in range(2)]
        misc = ctx.enter_context(nc.psum_tensor("misc_ps", [P, BANK], f32))
        acc = ctx.enter_context(nc.psum_tensor("acc_ps", [P, BANK], f32))
        CW = RANK + 1
        ctx_ps = misc[:, 0:CW]
        x1T_ps = pT[1][:, 0:HID]
        place_ps = pT[1][:, 0:E0]
        logits_ps = pT[1][:, 0:E0]
        half = [banks[u][:, b * BANK:(b + 1) * BANK] for u in range(2) for b in range(2)]

        ld_x, ld_xT, ld_kv, ld_lnw, ld_wkb = (sem(n) for n in ("ld_x", "ld_xT", "ld_kv", "ld_lnw", "ld_wkb"))
        ld_head = [sem(f"ld_head{u}") for u in range(2)]
        consts, made = sem("consts"), sem("made")
        x_split, kv_ready, sq_done, rms_done, keys_done, ones_done, kT_ps, k_split = (
            sem(n) for n in ("x_split", "kv_ready", "sq_done", "rms_done", "keys_done", "ones_done", "kT_ps", "k_split"))
        weff_ps, weff_f32, weff_split, wvo_ps, wvo_done, qT_ps, qT_done = (
            sem(n) for n in ("weff_ps", "weff_f32", "weff_split", "wvo_ps", "wvo_done", "qT_ps", "qT_done"))
        q_half, q_split, scores_ready, max_ready, probs_ready = (
            sem(n) for n in ("q_half", "q_split", "scores_ready", "max_ready", "probs_ready"))
        pT_ps = [sem(f"pT_ps{c}") for c in range(2)]
        pT_done = [sem(f"pT_done{c}") for c in range(2)]
        ctx_ready, rsum_done, ctx_normed, ctxT_psd, ctxT_done, acc_ready, acc_read = (
            sem(n) for n in ("ctx_ready", "rsum_done", "ctx_normed", "ctxT_psd", "ctxT_done", "acc_ready", "acc_read"))
        dve_w, dve_ln = sem("dve_w"), sem("dve_ln")
        dve_step, var_done, rstd_done, x1_done, stored = (
            sem(n) for n in ("dve_step", "var_done", "rstd_done", "x1_done", "stored"))

        block = ctx.enter_context(nc.Block())

        zeroed, ld_router0, x1T_psd, x1T_done, logits_done, logits_read, chosen_done, place_done, place_read, send_done = (
            sem(n) for n in ("zeroed", "ld_router0", "x1T_psd", "x1T_done", "logits_done", "logits_read", "chosen_done",
                             "place_done", "place_read", "send_done"))
        sent = [sem(f"sent0_{u}") for u in range(2)]
        consts0, route_step, exp0, weight_done, fetch_ready = (
            sem(n) for n in ("consts0", "route_step", "exp0", "weight_done", "fetch_ready"))
        ld_gu = [sem(f"ld_gu{u}") for u in range(RING // 2)]
        ld_dn = [sem(f"ld_dn{u}") for u in range(RING // 2)]
        ld_xe = [sem(f"ld_xe{u}") for u in range(RING // 2)]
        st_ye = [sem(f"st_ye{u}") for u in range(RING // 2)]
        xeT_ps, xeT_done, gu_ready, silu_done, h_done, ye_ps, ye_done = (
            sem(n) for n in ("xeT_ps", "xeT_done", "gu_ready", "silu_done", "h_done", "ye_ps", "ye_done"))
        (ld_wc, ld_woc, ld_init, gath_idx, combined, comb_step, x2_done, x2T_psd, x2T_done, fi_ready, vq_ready,
         ug_ready, gates_done, mid_step, z_done, r_done, lu_done, mix_ready, mix_read, x3_done) = (
            sem(n) for n in ("ld_wc", "ld_woc", "ld_init", "gath_idx", "combined", "comb_step", "x2_done", "x2T_psd",
                             "x2T_done", "fi_ready", "vq_ready", "ug_ready", "gates_done", "mid_step", "z_done",
                             "r_done", "lu_done", "mix_ready", "mix_read", "x3_done"))
        gath = [sem(f"gath{u}") for u in range(2)]
        (ld_w1, ld_w2, ld_sh, ld_router1, x3T_ps, x3T_done, lg1_ready, d_step, ch1_done, pl1_ready, slots1_ready,
         sent1, tanh1, consts1, gs_ready, gs_silu, hs_done, sh_ready, sh_read, last_go) = (
            sem(n) for n in ("ld_w1", "ld_w2", "ld_sh", "ld_router1", "x3T_ps", "x3T_done", "lg1_ready", "d_step",
                             "ch1_done", "pl1_ready", "slots1_ready", "sent1", "tanh1", "consts1", "gs_ready",
                             "gs_silu", "hs_done", "sh_ready", "sh_read", "last_go"))
        ld_xd = [sem(f"ld_xd{u}") for u in range(2)]
        st_yd = [sem(f"st_yd{u}") for u in range(2)]
        (xdT_ps, xdT_done, f1_ready, sgd_done, hd_done, hdT_ps, hdT_done, yd_ps, yd_done, final_step, result_done) = (
            sem(n) for n in ("xdT_ps", "xdT_done", "f1_ready", "sgd_done", "hd_done", "hdT_ps", "hdT_done", "yd_ps",
                             "yd_done", "final_step", "result_done"))
        last_in = [sem(f"last_in{t}") for t in range(TILES)]
        st_out = [sem(f"st_out{u}") for u in range(2)]
        rec_ps = [[half[0], half[1], half[2]], [half[3], pT[0], pT[1]]]
        passed = sem("passed")
        send_idx = sem("send_idx")

        def chain(eng, signal, base=0):
            count = [0]

            def link(ins):
                count[0] += 1
                ins.then_inc(signal, 1)
                eng.wait_ge(signal, base + count[0])
            return link

        def turn(e, u):
            return 16 // RING * (e - u) + 16

        def tiles_two(eng, body):
            body(0, 0)
            body(1, 1)
            with eng.Fori(1, TILES // 2) as i:
                for u in range(2):
                    body(2 * i + u, u)

        def blocks_two(eng, body):
            body(0, 0)
            body(1, 1)
            with eng.Fori(1, BLOCKS // 2) as i:
                for u in range(2):
                    body(2 * i + u, u)
            body(BLOCKS - 1, 0)

        def past(n, first):
            return not isinstance(n, int) or n >= first

        def hold(eng, signal, value):
            eng.wait_ge(signal, value)
            eng.sem_inc(passed, 1)

        def rank2(t):
            return TILES + (t if isinstance(t, int) and t < 2 else 2 * t - 1)

        def rank3(t):
            return TILES + (2 * t + 2 if not isinstance(t, int) or t < TILES - 1 else 2 * TILES - 1)

        def nth(qt, h):
            return qt * HEADS + h

        def chunks(qt):
            return 1 if qt < 4 else 2

        def ctxT_ps(qt):
            return pT[chunks(qt) - 1][:, 0:P]

        def pairs_of(eng, body):
            for j in range(FREE):
                body(j)
            with eng.Fori(FREE, PAIRS - 1) as j:
                body(j)
            body(PAIRS - 1)

        def ahead(qt, j, u):
            if isinstance(j, int) and j == PAIRS - 1:
                return None if qt == TILES - 1 else (qt + 1, u, nth(qt + 1, u))
            return qt, 2 * j + 2 + u, nth(qt, 2 * j + 2 + u)

        @block.sync
        def _(sp):
            sp.dma_start(xT_in[:], xT.rearrange("(c p) t -> p c t", p=P)).then_inc(ld_xT, 16)
            sp.dma_start(wkv_a[:], wkv_aT.rearrange("(c p) n -> p c n", p=P)).then_inc(ld_kv, 16)
            sp.dma_start(wkb[:], wkv_b.rearrange("(h a p) r -> a p h r", a=2, p=P)[0]).then_inc(ld_wkb, 16)
            wq_v = wq.rearrange("(h d) n -> d h n", d=QDIM)
            wr_v = wq_ropeT.rearrange("(c p) (h r) -> p c h r", p=P, h=HEADS)
            wv_v = wkv_b.rearrange("(h a p) r -> a p h r", a=2, p=P)[1]
            wo_v = woT.rearrange("(h p) n -> p h n", p=P)

            def load_head(h, u):
                sp.dma_start(wq_h[:, u, :], wq_v[0:P, h, :]).then_inc(ld_head[u], 16)
                sp.dma_start(weff[:, u, :, RANK:], wr_v[:, :, h, :]).then_inc(ld_head[u], 16)
                sp.dma_start(wv_h[:, u, :], wv_v[:, h, :]).then_inc(ld_head[u], 16)
                sp.dma_start(wo_h[:, u, :], wo_v[:, h, :]).then_inc(ld_head[u], 16)

            load_head(0, 0)
            load_head(1, 1)
            sp.dma_start(lnw[:], bass.AP(kv_ln.tensor, 0, [[0, P], [1, RANK]])).then_inc(ld_lnw, 16)
            sp.dma_start(x_in[:], x.rearrange("(t p) n -> p t n", p=P)).then_inc(ld_x, 16)
            with sp.Fori(1, PAIRS) as j:
                for u in range(2):
                    sp.wait_ge(wvo_ps, 2 * j - 1 + u)
                    sp.wait_ge(weff_split, 2 * j - 1 + u)
                    for dst, src in ((wq_h[:, u, :], wq_v[0:P, bass.ds(2 * j + u, 1), :]),
                                     (weff[:, u, :, RANK:], wr_v[:, :, bass.ds(2 * j + u, 1), :]),
                                     (wv_h[:, u, :], wv_v[:, bass.ds(2 * j + u, 1), :]),
                                     (wo_h[:, u, :], wo_v[:, bass.ds(2 * j + u, 1), :])):
                        sp.dma_start(dst, src).then_inc(ld_head[u], 16)
            sp.dma_start(router0[:], router0T.rearrange("(c p) e -> p c e", p=P)).then_inc(ld_router0, 16)
            sp.wait_ge(consts0, 1)
            for b in range(SLOTS // T):
                sp.dma_start(xe_d[b * T:(b + 1) * T, :].rearrange("(p a) n -> p (a n)", p=P),
                             zero_rows[:]).then_inc(zeroed, 16)
            for b in range(0, BLOCKS * P, T):
                n = min(T, BLOCKS * P - b)
                sp.dma_start(xd_d[b:b + n, :].rearrange("(p a) n -> p (a n)", p=P),
                             zero_rows[:, 0:n * HID // P]).then_inc(zeroed, 16)
            gu_v = gate_up0.rearrange("e (c p) f -> p e c f", p=P)
            dn_v = down0.rearrange("e i n -> i e n")
            xe_v = xe_d[0:SLOTS, :].rearrange("(e p) n -> p e n", p=P)

            def load_weights(e, u):
                if past(e, RING):
                    sp.wait_ge(ye_ps, e + 2 - RING)
                sp.dma_start(gu_w[:, u:u + 2], gu_v[:, bass.ds(e, 2)]).then_inc(ld_gu[u // 2], 16)
                sp.dma_start(dn_w[:, u:u + 2, :], dn_v[:, bass.ds(e, 2), :]).then_inc(ld_dn[u // 2], 16)

            def load_rows(e, u):
                if past(e, RING):
                    sp.wait_ge(xeT_ps, e + 2 - RING)
                sp.dma_start(xe[:, u:u + 2, :], xe_v[:, bass.ds(e, 2), :]).then_inc(ld_xe[u // 2], 16)

            sp.wait_ge(zeroed, 16 * ZEROINGS)
            for e in range(0, RING, 2):
                load_weights(e, e)
            sp.wait_ge(x1_done, TILES)
            sp.dma_start(w_c, w_in.rearrange("m (c p) n -> p m c n", p=P)).then_inc(ld_wc, 16)
            sp.dma_start(wo_c, w_mix.rearrange("m (c p) n -> p m c n", p=P)).then_inc(ld_woc, 16)
            sp.dma_start(init2[:], init_state).then_inc(ld_init, 16)
            sp.dma_start(router1_s[:], router1.rearrange("(c p) e -> p c e", p=P)).then_inc(ld_router1, 16)
            for u in range(2):
                sp.wait_ge(sent[u], 16 * TILES * TOP0 // 2)
            for e in range(0, RING, 2):
                load_rows(e, e)
            with sp.Fori(1, E0 // RING) as i:
                for u in range(0, RING, 2):
                    load_rows(RING * i + u, u)
                    load_weights(RING * i + u, u)
            sp.wait_ge(ye_ps, E0)
            sp.dma_start(sh_g, sh_gate.rearrange("(c p) f -> p c f", p=P)).then_inc(ld_sh, 16)
            sp.dma_start(sh_u, sh_up.rearrange("(c p) f -> p c f", p=P)).then_inc(ld_sh, 16)
            sp.dma_start(sh_d, sh_down.rearrange("(c p) n -> p c n", p=P)).then_inc(ld_sh, 16)
            for e in range(E1):
                sp.wait_ge(combined, e + 1)
                sp.dma_start(w1_s[:, e * HC * 2 * I1:(e + 1) * HC * 2 * I1].rearrange("p (c f) -> p c f", c=HC),
                             w1[e].rearrange("(c p) f -> p c f", p=P)).then_inc(ld_w1, 16)
            sp.wait_ge(x3_done, TILES)
            for e in range(E1):
                sp.dma_start(w2_s[:, e * I1 * HID // P:(e + 1) * I1 * HID // P].rearrange("p (c n) -> p c n", n=HID),
                             w2[e].rearrange("(c p) n -> p c n", p=P)).then_inc(ld_w2, 16)
            xd_v = xd_d.rearrange("(i p) n -> p i n", p=P)

            def load_block(i, u):
                if past(i, 2):
                    sp.wait_ge(xdT_ps, i - 1)
                sp.dma_start(xd[:, u, :], xd_v[:, bass.ds(i, 1), :]).then_inc(ld_xd[u], 16)

            sp.wait_ge(sh_read, TILES)
            sp.wait_ge(sent1, 16 * TILES * TOP1)
            blocks_two(sp, load_block)
            for t in range(TILES):
                sp.wait_ge(result_done, t + 1)
                sp.dma_start(out[t * P:(t + 1) * P, :], result[:, t % 2, :]).then_inc(st_out[t % 2], 16)
            for u in range(2):
                sp.wait_ge(st_out[u], 16 * TILES // 2)

        @block.gpsimd
        def _(pool):
            pool.memset(ident[:], 0.0).then_inc(made, 1)
            pool.memset(causal[:], 0.0).then_inc(made, 1)
            pool.memset(minus_half[:], -0.5).then_inc(made, 1)
            pool.memset(zeros_bf[:], 0.0).then_inc(made, 1)
            pool.wait_ge(made, 4)
            pool.affine_select(out=ident[:], in_=ident[:], compare_op=ALU.not_equal, fill=1.0, base=0,
                               pattern=[[-1, P]], channel_multiplier=1).then_inc(made, 1)
            pool.affine_select(out=causal[:], in_=causal[:], compare_op=ALU.is_ge, fill=MASKED, base=0,
                               pattern=[[-1, P]], channel_multiplier=1).then_inc(made, 1)
            pool.memset(latent[:, :, RANK:], 1.0).then_inc(ones_done, 1)
            pool.wait_ge(made, 6)
            pool.tensor_copy(ident_bf[:], ident[:]).then_inc(consts, 1)
            pool.memset(zero_rows[:], 0.0).then_inc(consts0, 1)
            pool.memset(ones_bf[:], 1.0).then_inc(made, 1)
            pool.memset(earlier[:], 1.0).then_inc(made, 1)
            pool.memset(chosen_before[:, 0, :], 0.0).then_inc(made, 1)
            pool.wait_ge(made, 9)
            pool.affine_select(out=earlier[:], in_=earlier[:], compare_op=ALU.is_gt, fill=0.0, base=0,
                               pattern=[[1, P]], channel_multiplier=-1).then_inc(consts0, 1)
            pool.iota(iota_e[:], pattern=[[1, E0]], base=0, channel_multiplier=0,
                      allow_small_or_imprecise_dtypes=True).then_inc(consts0, 1)
            pool.iota(spare, pattern=[[P, TILES], [T, TOP0]], base=SLOTS, channel_multiplier=1,
                      allow_small_or_imprecise_dtypes=True).then_inc(consts0, 1)
            pool.iota(iota_b[:], pattern=[[1, BLOCKS]], base=0, channel_multiplier=0,
                      allow_small_or_imprecise_dtypes=True).then_inc(consts1, 1)
            pool.iota(iota_r[:], pattern=[[P, TILES]], base=0, channel_multiplier=0,
                      allow_small_or_imprecise_dtypes=True).then_inc(consts1, 1)
            pool.memset(ones_e[:], 1.0).then_inc(consts1, 1)
            pool.memset(cb1[:, 0, :], 0.0).then_inc(consts1, 1)
            pool.wait_ge(dve_step, 2)
            pool.tensor_tensor(rms[:], ms[:], minus_half[:], ALU.pow).then_inc(rms_done, 1)

            def split_q(qt, h, u, n):
                src = qT[:, bass.ds(h * T + qt * P, P)]
                pool.tensor_copy(q_hi[:, u, :], src).then_inc(q_half, 1)
                hold(pool, q_half, n + 1)
                pool.tensor_tensor(q_lo[:, u, :], src, q_hi[:, u, :].bitcast(f32), ALU.subtract).then_inc(q_split, 1)

            def rstd_of(k):
                pool.wait_ge(var_done, k + 1)
                pool.tensor_tensor(rstd[:], mv[:, 1:2], minus_half[:, 0:1], ALU.pow).then_inc(rstd_done, 1)

            pool.wait_ge(qT_done, HEADS)

            def send(t):
                pool.wait_ge(send_done, t + 1)
                for k in range(TOP0):
                    pool.indirect_dma_start(xe_d, bass.IndirectOffsetOnAxis(send_i[:, t, k:k + 1], 0),
                                            x1[:, t, :], None).then_inc(sent[k % 2], 16)

            def send_one(t, j, u):
                if not (t == 0 and isinstance(j, int)):
                    hold(pool, sent[u], 16 * (4 * t - FREE + j))
                pool.tensor_copy(send_now[:, u:u + 1],
                                 send_flat[:, bass.ds(t * TOP0 + 2 * (j - FREE) + u, 1)]).then_inc(send_idx, 1)
                hold(pool, send_idx, t * TOP0 + 2 * (j - FREE) + u + 1)
                pool.indirect_dma_start(xe_d, bass.IndirectOffsetOnAxis(send_now[:, u:u + 1], 0),
                                        x1[:, t, :], None).then_inc(sent[u], 16)

            send_flat = send_i[:].rearrange("p t k -> p (t k)")
            split_q(0, 0, 0, 0)
            split_q(0, 1, 1, 1)
            for qt in range(TILES):
                def pair(j):
                    for u in range(2):
                        if ahead(qt, j, u):
                            tile, head, n = ahead(qt, j, u)
                            pool.wait_ge(scores_ready, n - 1)
                            split_q(tile, head, u, n)
                        if qt >= 2 and not isinstance(j, int):
                            send_one(qt - 2, j, u)
                    if qt and isinstance(j, int) and j == 1:
                        rstd_of(qt - 1)
                    if qt >= 2 and isinstance(j, int) and j == FREE - 1:
                        pool.wait_ge(send_done, qt - 1)
                if qt == 2:
                    pool.wait_ge(zeroed, 16 * ZEROINGS)
                pairs_of(pool, pair)
            rstd_of(TILES - 1)
            for t in range(TILES - 2, TILES):
                send(t)
            def fetch(t, u, i):
                if past(t, 2):
                    pool.wait_ge(combined, t - 1)
                pool.sem_inc(passed, 1)
                pool.tensor_copy(fetch_now[:, u, :], fetch_flat[:, bass.ds(t * TOP0, TOP0)]).then_inc(gath_idx, 1)
                hold(pool, gath_idx, t + 1)
                for k in range(TOP0):
                    pool.indirect_dma_start(gathered[:, u, k, :], None, ye_d,
                                            bass.IndirectOffsetOnAxis(fetch_now[:, u, k:k + 1], 0)).then_inc(gath[u], 16)

            fetch_flat = fetch_i[:].rearrange("p t k -> p (t k)")
            pool.wait_ge(weight_done, 1)
            for u in range(RING // 2):
                pool.wait_ge(st_ye[u], 16 * E0 // RING)
            fetch(0, 0, 0)
            fetch(1, 1, 0)
            rstd_of(rank2(0))
            fetch(2, 0, 1)
            rstd_of(rank2(1))
            fetch(3, 1, 1)
            rstd_of(rank3(0))
            with pool.Fori(1, TILES // 2 - 1) as i:
                for u in range(2):
                    rstd_of(rank2(2 * i + u))
                    fetch(2 * i + u + 2, u, i + 1)
                    rstd_of(rank3(2 * i + u - 1))
            for t in range(TILES - 2, TILES):
                rstd_of(rank2(t))
                rstd_of(rank3(t - 1))
            rstd_of(rank3(TILES - 1))
            pool.wait_ge(slots1_ready, 1)
            for t in range(TILES):
                for k in range(TOP1):
                    pool.indirect_dma_start(xd_d, bass.IndirectOffsetOnAxis(slot1[:, t, k:k + 1], 0),
                                            x1[:, t, :], None).then_inc(sent1, 16)
            pool.wait_ge(st_yd[0], 16 * (BLOCKS - BLOCKS // 2))
            pool.wait_ge(st_yd[1], 16 * (BLOCKS // 2))
            for t in range(TILES):
                for k in range(TOP1):
                    pool.indirect_dma_start(last_rows[:, t, k, :], None, yd_d,
                                            bass.IndirectOffsetOnAxis(slot1[:, t, k:k + 1], 0)).then_inc(last_in[t], 16)
                if t >= 1:
                    rstd_of(3 * TILES + t - 1)
            rstd_of(4 * TILES - 1)

        @block.scalar
        def _(act):
            act.wait_ge(kv_ready, 1)
            act.activation(sq[:], banks[0][:].rearrange("p (t n) -> p t n", t=TILES)[:, :, 0:RANK],
                           ACT.Square).then_inc(sq_done, 1)

            def weff_copy(h, u):
                act.wait_ge(weff_ps, h + 1)
                act.copy(weff[:, u, :, 0:RANK],
                         pT[u][:, 0:HC * RANK].rearrange("p (c r) -> p c r", c=HC)).then_inc(weff_f32, 1)

            def q_copy(h, u):
                hold(act, qT_ps, h + 1)
                act.activation(qT[:, bass.ds(h * T, T)], banks[u][:], ACT.Copy,
                               scale=float(QDIM) ** -0.5).then_inc(qT_done, 1)

            weff_copy(0, 0)
            weff_copy(1, 1)
            q_copy(0, 0)
            with act.Fori(1, PAIRS) as j:
                weff_copy(2 * j, 0)
                q_copy(2 * j - 1, 1)
                weff_copy(2 * j + 1, 1)
                q_copy(2 * j, 0)
            q_copy(HEADS - 1, 1)

            def exp_probs(qt, n, u):
                L = (qt + 1) * P
                act.wait_ge(max_ready, n + 1)
                if past(n, 2):
                    act.wait_ge(pT_ps[0], n - 1)
                    if qt > 4 or qt == 4 and past(n, nth(4, 2)):
                        act.wait_ge(pT_ps[1], n - 1 - 4 * HEADS)
                act.activation(probs[:, u, 0:L], banks[u][:, 0:L], ACT.Exp,
                               bias=neg_max[:, u:u + 1]).then_inc(probs_ready, 1)

            def copy_pT(qt, n, u):
                w = min(qt + 1, 4) * P
                act.wait_ge(pT_ps[0], n + 1)
                act.copy(probsT[:, u, 0:w], pT[u if chunks(qt) == 1 else 0][:, 0:w]).then_inc(pT_done[0], 1)

            def copy_ctxT(qt, m):
                act.wait_ge(ctxT_psd, m + 1)
                act.copy(ctxT[:], ctxT_ps(qt)).then_inc(ctxT_done, 1)

            def copy_x1T(t):
                act.wait_ge(x1T_psd, t + 1)
                if t:
                    act.wait_ge(logits_done, t)
                act.copy(x1T[:], x1T_ps.rearrange("p (c n) -> p c n", c=HC)).then_inc(x1T_done, 1)

            exp_probs(0, 0, 0)
            for qt in range(TILES):
                def pair(j):
                    copy_pT(qt, nth(qt, 2 * j), 0)
                    exp_probs(qt, nth(qt, 2 * j + 1), 1)
                    if past(qt * PAIRS + j, 1):
                        copy_ctxT(qt, qt * PAIRS + j - 1)
                    copy_pT(qt, nth(qt, 2 * j + 1), 1)
                    if ahead(qt, j, 0):
                        tile, head, n = ahead(qt, j, 0)
                        exp_probs(tile, n, 0)
                    if qt and isinstance(j, int) and j == FREE - 1:
                        copy_x1T(qt - 1)
                pairs_of(act, pair)
            copy_ctxT(TILES - 1, TILES * PAIRS - 1)
            copy_x1T(TILES - 1)
            act.wait_ge(exp0, 1)
            act.activation(weight[:], weight[:], ACT.Exp).then_inc(exp0, 1)

            def expert_act(e, u):
                b = u % 2
                act.wait_ge(gu_ready, e + 1)
                act.activation(sg[:, b, :], half[b][0:I0, 0:P], ACT.Silu).then_inc(silu_done, 1)

            ye_v = ye_d.rearrange("(e p) n -> p e n", p=P)

            def expert_out(e, u):
                act.wait_ge(ye_ps, e + 1)
                if past(e, RING) and u % 2 == 0:
                    act.wait_ge(st_ye[u // 2], turn(e, u) - 16)
                act.copy(ye[:, u, :], half[2 + u % 2][:, 0:HID]).then_inc(ye_done, 1)
                if u % 2:
                    act.wait_ge(ye_done, e + 1)
                    act.dma_start(ye_v[:, bass.ds(e - 1, 2), :], ye[:, u - 1:u + 1, :]).then_inc(st_ye[u // 2], 16)

            expert_act(0, 0)
            for e in range(RING):
                expert_act(e + 1, (e + 1) % RING)
                expert_out(e, e)
            with act.Fori(1, E0 // RING - 1) as i:
                for u in range(RING):
                    expert_act(RING * i + u + 1, (u + 1) % RING)
                    expert_out(RING * i + u, u)
            for e in range(E0 - RING, E0):
                if e + 1 < E0:
                    expert_act(e + 1, (e + 1) % RING)
                expert_out(e, e % RING)
            def copy_x2T(t, u):
                act.wait_ge(x2T_psd, t + 1)
                act.copy(x2T[:, u], x1T_ps_c).then_inc(x2T_done, 1)

            def gates(t, u):
                (a, b, c), n = rec_ps[u], HC * P

                def of(ap):
                    return ap.rearrange("p (c n) -> p c n", c=HC)
                act.wait_ge(fi_ready, t + 1)
                if past(t, 2):
                    act.wait_ge(lu_done, t - 1)
                act.activation(forget[:, u], of(a[:, 0:n]), ACT.Tanh).then_inc(gates_done, 1)
                act.activation(igate[:, u], of(a[:, n:]), ACT.Tanh, scale=0.5).then_inc(gates_done, 1)
                act.wait_ge(vq_ready, t + 1)
                act.activation(value[:, u], of(b[:, 0:n]), ACT.Silu).then_inc(gates_done, 1)
                act.wait_ge(ug_ready, t + 1)
                act.activation(lgate[:, u], of(c[:, n:]), ACT.Silu).then_inc(gates_done, 1)

            def read_out(t, u):
                act.wait_ge(z_done, t + 1)
                if past(t, 2):
                    act.wait_ge(mix_ready, t - 1)
                act.activation(readout[:, u], zq[:, u], ACT.Silu, scale=0.5).then_inc(r_done, 1)

            x1T_ps_c = misc[:, 0:HID].rearrange("p (c n) -> p c n", c=HC)
            copy_x2T(0, 0)
            gates(0, 0)
            copy_x2T(1, 1)
            read_out(0, 0)
            gates(1, 1)
            with act.Fori(1, TILES // 2) as i:
                for u in range(2):
                    copy_x2T(2 * i + u, u)
                    read_out(2 * i + u - 1, 1 - u)
                    gates(2 * i + u, u)
            read_out(TILES - 1, 1)
            for b in range(2):
                act.wait_ge(x3T_ps, b + 1)
                act.copy(x3T[:, 0, b * BANK:(b + 1) * BANK], half[b]).then_inc(x3T_done, 1)
            act.wait_ge(tanh1, 1)
            act.activation(weight1[:, :, 1:2], weight1[:, :, 0:1], ACT.Tanh, scale=0.5).then_inc(tanh1, 1)
            for n in range(2 * SC):
                act.wait_ge(gs_ready, n + 1)
                if n >= 2:
                    act.wait_ge(hs_done, n - 1)
                act.activation(sgd[:, n % 2, :], half[n % 2], ACT.Silu).then_inc(gs_silu, 1)

            def block_act(i, u):
                act.wait_ge(f1_ready, i + 1)
                if past(i, 2):
                    act.wait_ge(hd_done, i - 1)
                act.activation(sgd[:, u, :], half[2 * u], ACT.Silu).then_inc(sgd_done, 1)

            def block_T(i, u):
                act.wait_ge(xdT_ps, i + 1)
                if past(i, 2):
                    act.wait_ge(f1_ready, i - 1)
                act.copy(xdT[:, u], x1T_ps_c).then_inc(xdT_done, 1)

            def block_out(i, u):
                act.wait_ge(yd_ps, i + 1)
                if past(i, 2):
                    act.wait_ge(st_yd[u], 8 * (i - u))
                act.copy(yd[:, u, :], acc[:, 0:HID]).then_inc(yd_done, 1)
                act.wait_ge(yd_done, i + 1)
                act.dma_start(yd_v[:, bass.ds(i, 1), :], yd[:, u, :]).then_inc(st_yd[u], 16)

            yd_v = yd_d.rearrange("(i p) n -> p i n", p=P)
            act.wait_ge(hs_done, 2 * SC)
            block_T(0, 0)
            block_act(0, 0)
            block_T(1, 1)

            def block_steps(i, u):
                if not (isinstance(i, int) and i >= BLOCKS - 2):
                    block_T(i + 2, u)
                if not (isinstance(i, int) and i >= BLOCKS - 1):
                    block_act(i + 1, 1 - u)
                block_out(i, u)

            block_steps(0, 0)
            block_steps(1, 1)
            with act.Fori(1, BLOCKS // 2 - 1) as i:
                for u in range(2):
                    block_steps(2 * i + u, u)
            for i in range(BLOCKS - 3, BLOCKS):
                block_steps(i, i % 2)

        @block.vector
        def _(dve):
            dve.wait_ge(ld_xT, 16)
            dve.tensor_copy(xT_hi[:], xT_in[:]).then_inc(x_split, 1)
            dve.wait_ge(x_split, 1)
            dve.tensor_tensor(xT_lo[:], xT_in[:], xT_hi[:].bitcast(f32), ALU.subtract).then_inc(x_split, 1)
            kv_ps = banks[0][:].rearrange("p (t n) -> p t n", t=TILES)
            dve.wait_ge(sq_done, 1)
            dve.tensor_reduce(ms[:], sq[:], AX.X, ALU.add).then_inc(dve_step, 1)
            dve.wait_ge(dve_step, 1)
            dve.tensor_scalar(ms[:], ms[:], 1.0 / RANK, RMS_EPS, ALU.mult, ALU.add).then_inc(dve_step, 1)
            dve.tensor_copy(keys[:, :, RANK:], kv_ps[:, :, RANK:]).then_inc(keys_done, 1)
            dve.wait_ge(rms_done, 1)
            dve.wait_ge(ld_lnw, 16)
            for t in range(TILES):
                dve.scalar_tensor_tensor(keys[:, t, 0:RANK], kv_ps[:, t, 0:RANK], rms[:, t:t + 1], lnw[:],
                                         ALU.mult, ALU.mult).then_inc(keys_done, 1)
            dve.wait_ge(keys_done, TILES + 1)
            dve.tensor_copy(latent[:, :, 0:RANK], keys[:, :, 0:RANK]).then_inc(ones_done, 1)
            dve.wait_ge(kT_ps, 1)
            dve.tensor_copy(kT_hi[:], banks[1][:]).then_inc(k_split, 1)
            dve.wait_ge(k_split, 1)
            dve.tensor_tensor(kT_lo[:], banks[1][:], kT_hi[:].bitcast(f32), ALU.subtract).then_inc(k_split, 1)

            def split_weff(h, u, i):
                dve.wait_ge(weff_f32, h + 1)
                dve.wait_ge(ld_head[u], 64 * (i + 1))
                if not (isinstance(h, int) and h < 2):
                    dve.wait_ge(qT_ps, h - 1)
                dve.tensor_copy(weff_hi[:, u], weff[:, u]).then_inc(dve_w, 1)
                dve.wait_ge(dve_w, h + 1)
                dve.tensor_tensor(weff_lo[:, u], weff[:, u], weff_hi[:, u].bitcast(f32),
                                  ALU.subtract).then_inc(weff_split, 1)

            def wvo_copy(m):
                hold(dve, wvo_ps, 2 * m + 2)
                dve.tensor_copy(wvo[:, bass.ds(m * HID, HID)], misc[:, 0:HID]).then_inc(wvo_done, 1)

            split_weff(0, 0, 0)
            split_weff(1, 1, 0)
            wvo_copy(0)
            with dve.Fori(1, PAIRS) as j:
                split_weff(2 * j, 0, j)
                split_weff(2 * j + 1, 1, j)
                wvo_copy(j)

            def row_max(qt, n, u):
                dve.wait_ge(scores_ready, n + 1)
                dve.tensor_reduce(neg_max[:, u:u + 1], banks[u][:, 0:(qt + 1) * P], AX.X, ALU.max,
                                  negate=True).then_inc(max_ready, 1)

            def copy_pT(qt, n, u):
                if chunks(qt) == 2:
                    dve.wait_ge(pT_ps[1], n + 1 - 4 * HEADS)
                    w = (qt + 1 - 4) * P
                    dve.tensor_copy(probsT[:, u, BANK:BANK + w], pT[1][:, 0:w]).then_inc(pT_done[1], 1)

            def norm_ctx(n, u, m=0):
                dve.wait_ge(ctx_ready, n + 1)
                dve.reciprocal(rsum[:, u:u + 1], ctx_ps[:, RANK:]).then_inc(rsum_done, 1)
                dve.wait_ge(rsum_done, n + 1)
                if u == 0 and not (isinstance(m, int) and m < 1):
                    dve.wait_ge(ctxT_psd, m)
                dve.tensor_scalar(ctx_n[:, u * RANK:(u + 1) * RANK], ctx_ps[:, 0:RANK],
                                  rsum[:, u:u + 1], None, ALU.mult).then_inc(ctx_normed, 1)

            def variance(k, src, eps):
                dve.bn_stats(stats[:], src).then_inc(dve_ln, 1)
                hold(dve, dve_ln, 2 * k + 1)
                dve.bn_aggr(mv[:], stats[:]).then_inc(dve_ln, 1)
                dve.wait_ge(dve_ln, 2 * k + 2)
                dve.tensor_scalar(mv[:, 1:2], mv[:, 1:2], eps, None, ALU.add).then_inc(var_done, 1)

            def normalise(k, src, dst):
                dve.wait_ge(rstd_done, k + 1)
                return dve.tensor_scalar(dst, src, mv[:, 0:1], rstd[:, 0:1], ALU.subtract, ALU.mult)

            def layernorm(k, src, dst, eps):
                variance(k, src, eps)
                return normalise(k, src, dst)

            def add_residual(qt):
                dve.wait_ge(acc_ready, (qt + 1) * PAIRS)
                dve.wait_ge(ld_x, 16)
                dve.tensor_tensor(y[:], acc[:, 0:HID], x_in[:, qt, :], ALU.add).then_inc(acc_read, 1)
                dve.wait_ge(acc_read, qt + 1)
                variance(qt, y[:], LN_EPS)

            def finish_tile(qt):
                normalise(qt, y[:], x1[:, qt, :]).then_inc(x1_done, 1)

            def read_place(t):
                dve.wait_ge(place_done, t + 1)
                dve.tensor_copy(place, place_ps).then_inc(place_read, 1)

            def read_logits(t):
                dve.wait_ge(logits_done, t + 1)
                dve.tensor_copy(logits, logits_ps).then_inc(logits_read, 1)

            def choose(t):
                link = chain(dve, route_step, 13 * t)
                dve.wait_ge(logits_read, t + 1)
                link(dve.max(top_v[:, t, :], logits))
                link(dve.max_index(top_i[:, t, :], top_v[:, t, :], logits))
                link(dve.match_replace(left, top_v[:, t, :], logits, -3e38))
                link(dve.tensor_tensor(chosen[:, t, :], logits, left, ALU.not_equal))
                if t + 1 < TILES:
                    link(dve.tensor_tensor(chosen_before[:, t + 1, :], chosen_before[:, t, :], chosen[:, t, :], ALU.add))
                else:
                    dve.sem_inc(route_step, 1)
                dve.tensor_copy(top_f[:, t, :], top_i[:, t, :]).then_inc(chosen_done, 1)

            def assign(t):
                link = chain(dve, route_step, 13 * t + 5)
                dve.wait_ge(place_read, t + 1)
                dve.wait_ge(chosen_done, t + 1)
                shape = [P, TOP0, E0]
                dve.wait_ge(consts0, 4)
                link(dve.tensor_tensor(onehot, iota_e[:].unsqueeze(1).broadcast_to(shape),
                                       top_f[:, t, :].unsqueeze(2).broadcast_to(shape), ALU.is_equal))
                link(dve.tensor_tensor(placed, onehot, place.unsqueeze(1).broadcast_to(shape), ALU.mult))
                yield
                link(dve.tensor_reduce(place8[:, t, :], placed, AX.X, ALU.add))
                dve.tensor_scalar(valid[:, t, :], place8[:, t, :], float(CAP), None, ALU.is_lt)
                link(dve.tensor_scalar(slot_t[:], place8[:, t, :], float(CAP - 1), None, ALU.min))
                link(dve.scalar_tensor_tensor(slot[:, t, :], top_f[:, t, :], float(CAP), slot_t[:], ALU.mult, ALU.add))
                link(dve.tensor_tensor(slot_t[:], slot[:, t, :], spare[:, t, :], ALU.subtract))
                link(dve.tensor_tensor(slot_t[:], slot_t[:], valid[:, t, :], ALU.mult))
                link(dve.tensor_copy(fetch_i[:, t, :], slot[:, t, :]))
                dve.tensor_tensor(send_i[:, t, :], slot_t[:], spare[:, t, :], ALU.add).then_inc(send_done, 1)
                yield

            row_max(0, 0, 0)
            row_max(0, 1, 1)
            for qt in range(TILES):
                parts = assign(qt - 2) if qt >= 2 else None

                def pair(j):
                    if past(nth(qt, 2 * j), 1):
                        norm_ctx(nth(qt, 2 * j - 1), 1)
                    copy_pT(qt, nth(qt, 2 * j), 0)
                    if ahead(qt, j, 0):
                        tile, head, n = ahead(qt, j, 0)
                        row_max(tile, n, 0)
                    if qt and isinstance(j, int) and j == 1:
                        finish_tile(qt - 1)
                    if qt >= 2 and isinstance(j, int) and j == 0:
                        choose(qt - 2)
                    if qt >= 2 and isinstance(j, int) and j == 2:
                        next(parts)
                    norm_ctx(nth(qt, 2 * j), 0, qt * PAIRS + j)
                    copy_pT(qt, nth(qt, 2 * j + 1), 1)
                    if qt >= 2 and isinstance(j, int) and j == 1:
                        read_place(qt - 2)
                    if qt and isinstance(j, int) and j == PAIRS - 1:
                        read_logits(qt - 1)
                    if ahead(qt, j, 1):
                        tile, head, n = ahead(qt, j, 1)
                        row_max(tile, n, 1)
                    if qt and isinstance(j, int) and j == 0:
                        add_residual(qt - 1)
                    if qt >= 2 and isinstance(j, int) and j == 2:
                        next(parts)
                pairs_of(dve, pair)
            norm_ctx(nth(TILES, -1), 1)
            choose(TILES - 2)
            add_residual(TILES - 1)
            finish_tile(TILES - 1)
            read_place(TILES - 2)
            for part in assign(TILES - 2):
                pass
            read_logits(TILES - 1)
            choose(TILES - 1)
            read_place(TILES - 1)
            for part in assign(TILES - 1):
                pass
            link = chain(dve, route_step, 13 * TILES)
            shape = [P, TILES, TOP0]
            dve.tensor_tensor(weight[:], top_v, top_v[:, :, 0:1].broadcast_to(shape), ALU.subtract).then_inc(exp0, 1)
            dve.wait_ge(exp0, 2)
            link(dve.tensor_reduce(wsum[:], weight[:], AX.X, ALU.add))
            link(dve.reciprocal(wsum[:], wsum[:]))
            link(dve.tensor_tensor(weight[:], weight[:], wsum[:].unsqueeze(2).broadcast_to(shape), ALU.mult))
            dve.tensor_tensor(weight[:], weight[:], valid[:], ALU.mult).then_inc(weight_done, 1)

            def copy_xeT(e, u):
                dve.wait_ge(xeT_ps, e + 1)
                if past(e, 2):
                    dve.wait_ge(gu_ready, e - 1)
                dve.tensor_copy(xeT[:, u % 2], pT[u % 2][:, 0:HID].rearrange("p (c n) -> p c n", c=HC)).then_inc(xeT_done, 1)

            def gated(e, u):
                dve.wait_ge(silu_done, e + 1)
                if past(e, 2):
                    dve.wait_ge(ye_ps, e - 1)
                dve.tensor_tensor(hT[:, u % 2, :], sg[:, u % 2, :], half[u % 2][0:I0, P:2 * P], ALU.mult).then_inc(h_done, 1)

            copy_xeT(0, 0)
            copy_xeT(1, 1)
            gated(0, 0)
            for e in range(RING):
                copy_xeT(e + 2, (e + 2) % RING)
                gated(e + 1, (e + 1) % RING)
            with dve.Fori(1, E0 // RING - 1) as i:
                for u in range(RING):
                    copy_xeT(RING * i + u + 2, (u + 2) % RING)
                    gated(RING * i + u + 1, (u + 1) % RING)
            for e in range(E0 - RING, E0):
                if e + 2 < E0:
                    copy_xeT(e + 2, (e + 2) % RING)
                if e + 1 < E0:
                    gated(e + 1, (e + 1) % RING)
            def combine(t, u, i):
                link = chain(dve, comb_step, (TOP0 - 1) * t)
                dve.wait_ge(gath[u], 16 * TOP0 * (i + 1))
                if isinstance(t, int) and t == 1:
                    dve.wait_ge(x2_done, 1)
                if past(t, 2):
                    dve.wait_ge(x3_done, t - 1)
                for k in range(TOP0):
                    ins = dve.scalar_tensor_tensor(y[:], gathered[:, u, k, :], weight_flat[:, bass.ds(t * TOP0 + k, 1)],
                                                   y[:] if k else x1_flat[:, bass.ds(t * HID, HID)], ALU.mult, ALU.add)
                    if k < TOP0 - 1:
                        link(ins)
                ins.then_inc(combined, 1)
                dve.wait_ge(combined, t + 1)
                layernorm(rank2(t), y[:], x2[:, u, :], LN_EPS).then_inc(x2_done, 1)

            def middle(t, u):
                link = chain(dve, mid_step, 3 * t)
                dve.wait_ge(gates_done, 4 * t + 3)
                link(dve.scalar_tensor_tensor(value[:, u], igate[:, u], 1.0, value[:, u], ALU.add, ALU.mult))
                for c in range(HC):
                    init = init2[:, c:c + 1] if isinstance(t, int) and t == 0 else state[:, 1 - u, c, P - 1:P]
                    link(dve.tensor_tensor_scan(state[:, u, c, :], forget[:, u, c, :], value[:, u, c, :], init,
                                                ALU.mult, ALU.add))
                q = rec_ps[u][1][:, HC * P:].rearrange("p (c n) -> p c n", c=HC)
                dve.tensor_tensor(zq[:, u], state[:, u], q, ALU.mult).then_inc(z_done, 1)
                dve.wait_ge(gates_done, 4 * t + 4)
                if past(t, 2):
                    dve.wait_ge(mix_ready, t - 1)
                up = rec_ps[u][2][:, 0:HC * P].rearrange("p (c n) -> p c n", c=HC)
                dve.tensor_tensor(local[:, u], lgate[:, u], up, ALU.mult).then_inc(lu_done, 1)

            def finish_mix(t, u):
                dve.wait_ge(mix_ready, t + 1)
                dve.wait_ge(x2_done, min(t + 2, TILES) if isinstance(t, int) else t + 2)
                dve.tensor_tensor(y[:], acc[:, 0:HID], x2[:, u, :], ALU.add).then_inc(mix_read, 1)
                dve.wait_ge(mix_read, t + 1)
                layernorm(rank3(t), y[:], x1_flat[:, bass.ds(t * HID, HID)], LN_EPS).then_inc(x3_done, 1)

            weight_flat = weight[:].rearrange("p t k -> p (t k)")
            x1_flat = x1[:].rearrange("p t n -> p (t n)")
            dve.wait_ge(ld_init, 16)
            dve.tensor_scalar(init2[:], init2[:], 2.0, None, ALU.mult).then_inc(dve_step, 1)
            dve.wait_ge(weight_done, 1)
            dve.wait_ge(dve_step, 3)
            combine(0, 0, 0)
            combine(1, 1, 0)
            middle(0, 0)
            finish_mix(0, 0)
            with dve.Fori(1, TILES // 2) as i:
                for u in range(2):
                    combine(2 * i + u, u, i)
                    middle(2 * i + u - 1, 1 - u)
                    finish_mix(2 * i + u - 1, 1 - u)
            middle(TILES - 1, 1)
            finish_mix(TILES - 1, 1)
            for b in range(2):
                dve.wait_ge(x3T_ps, b + 3)
                dve.tensor_copy(x3T[:, 1, b * BANK:(b + 1) * BANK], half[2 + b]).then_inc(x3T_done, 1)

            link = chain(dve, d_step)
            dve.wait_ge(lg1_ready, 1)
            dve.wait_ge(consts1, 4)
            link(dve.tensor_copy(lg1[:], misc[:, 0:TILES * E1].rearrange("p (t e) -> p t e", t=TILES)))
            for t in range(TILES):
                ins = dve.max(tv1[:, t, :], lg1[:, t, :])
            link(ins)
            for t in range(TILES):
                ins = dve.max_index(ti1[:, t, :], tv1[:, t, :], lg1[:, t, :])
            link(ins)
            dve.tensor_tensor(weight1[:, :, 0:1], tv1[:, :, 1:2], tv1[:, :, 0:1], ALU.subtract).then_inc(tanh1, 1)
            link(dve.tensor_copy(tf1[:], ti1[:]))
            sh4 = [P, TILES, E1]
            for k in range(TOP1):
                link(dve.tensor_tensor(oh1[:, :, k, :], iota_e[:, 0:E1].unsqueeze(1).broadcast_to(sh4),
                                       tf1[:, :, k:k + 1].broadcast_to(sh4), ALU.is_equal))
            link(dve.tensor_tensor(ch1[:], oh1[:, :, 0, :], oh1[:, :, 1, :], ALU.add))
            for t in range(TILES):
                link(dve.tensor_tensor(cb1[:, t + 1, :], cb1[:, t, :], ch1[:, t, :], ALU.add))
            dve.sem_inc(ch1_done, 1)
            dve.wait_ge(pl1_ready, 1)
            link(dve.tensor_copy(pl1[:], acc[:, 0:(TILES + 1) * E1].rearrange("p (t e) -> p t e", e=E1)))
            sh5 = [P, E1, TILES]
            link(dve.tensor_tensor(blk_cmp[:], pl1[:, TILES, :].unsqueeze(2).broadcast_to(sh5),
                                   iota_r[:].unsqueeze(1).broadcast_to(sh5), ALU.is_gt))
            link(dve.tensor_reduce(nblk[:], blk_cmp[:], AX.X, ALU.add))
            link(dve.tensor_tensor_scan(blk_end[:], ones_e[:], nblk[:], 0.0, ALU.mult, ALU.add))
            link(dve.tensor_tensor(blk_start[:], blk_end[:], nblk[:], ALU.subtract))
            link(dve.tensor_scalar(blk_start[:], blk_start[:], float(P), None, ALU.mult))
            link(dve.tensor_tensor(pl1[:, 0:TILES, :], pl1[:, 0:TILES, :],
                                   blk_start[:].unsqueeze(1).broadcast_to(sh4), ALU.add))
            for k in range(TOP1):
                link(dve.tensor_tensor(oh1[:, :, k, :], oh1[:, :, k, :], pl1[:, 0:TILES, :], ALU.mult))
            link(dve.tensor_reduce(sl1[:], oh1[:], AX.X, ALU.add))
            dve.tensor_copy(slot1[:], sl1[:]).then_inc(slots1_ready, 1)
            sh6 = [P, BLOCKS, E1]
            link(dve.tensor_tensor(own_cmp[:], blk_end[:].unsqueeze(1).broadcast_to(sh6),
                                   iota_b[:].unsqueeze(2).broadcast_to(sh6), ALU.is_le))
            link(dve.tensor_reduce(owner[:], own_cmp[:], AX.X, ALU.add))
            dve.tensor_scalar(owner_i[:], owner[:], float(E1 - 1), None, ALU.min).then_inc(slots1_ready, 1)
            dve.wait_ge(tanh1, 2)
            link(dve.tensor_scalar(weight1[:, :, 0:1], weight1[:, :, 1:2], -0.5, 0.5, ALU.mult, ALU.add))
            link(dve.tensor_scalar(weight1[:, :, 1:2], weight1[:, :, 1:2], 0.5, 0.5, ALU.mult, ALU.add))

            for b in range(2):
                for c in range(SC):
                    n = b * SC + c
                    dve.wait_ge(gs_silu, n + 1)
                    dve.tensor_tensor(hs[:, c, :], sgd[:, n % 2, :], half[2 + n % 2], ALU.mult).then_inc(hs_done, 1)
                for q in range(4):
                    t = 4 * b + q
                    dve.wait_ge(sh_ready, t + 1)
                    dve.tensor_tensor(shared[:, t, :], pT[q % 2][:, 0:HID], x1[:, t, :], ALU.add).then_inc(sh_read, 1)

            def block_gated(i, u):
                dve.wait_ge(sgd_done, i + 1)
                if past(i, 1):
                    dve.wait_ge(hdT_ps, i)
                dve.tensor_tensor(hd, sgd[:, u, :], half[2 * u + 1], ALU.mult).then_inc(hd_done, 1)

            def block_hT(i, u):
                dve.wait_ge(hdT_ps, i + 1)
                if past(i, 2):
                    dve.wait_ge(yd_ps, i - 1)
                dve.tensor_copy(hdT[:, u, :], pT[u][:]).then_inc(hdT_done, 1)

            def block_dve(i, u):
                block_gated(i, u)
                block_hT(i, u)

            blocks_two(dve, block_dve)
            for t in range(TILES):
                link = chain(dve, final_step, 1 * t)
                dve.wait_ge(last_in[t], 16 * TOP1)
                if t:
                    dve.wait_ge(result_done, t)
                link(dve.scalar_tensor_tensor(y[:], last_rows[:, t, 0, :], weight1[:, t, 0:1], shared[:, t, :],
                                              ALU.mult, ALU.add))
                dve.scalar_tensor_tensor(y[:], last_rows[:, t, 1, :], weight1[:, t, 1:2], y[:],
                                         ALU.mult, ALU.add).then_inc(last_go, 1)
                dve.wait_ge(last_go, t + 1)
                if t >= 2:
                    dve.wait_ge(st_out[t % 2], 16 * (t // 2))
                layernorm(3 * TILES + t, y[:], result[:, t % 2, :], LN_EPS).then_inc(result_done, 1)

        @block.tensor
        def _(pe):
            def product3(out_ap, lhs, rhs, start, stop):
                (lh, ll), (rh, rl) = lhs, rhs
                pe.matmul(out_ap, lh, rh, start=start, stop=False)
                pe.matmul(out_ap, lh, rl, start=False, stop=False)
                return pe.matmul(out_ap, ll, rh, start=False, stop=stop)

            pe.wait_ge(ld_xT, 16)
            pe.wait_ge(ld_kv, 16)
            for t in range(TILES):
                for c in range(HC):
                    last = pe.matmul(banks[0][:, t * P:(t + 1) * P], xT_in[:, c, t * P:(t + 1) * P], wkv_a[:, c, :],
                                     start=c == 0, stop=c == HC - 1)
            last.then_inc(kv_ready, 1)
            pe.wait_ge(consts, 1)
            pe.wait_ge(keys_done, TILES + 1)
            for t in range(TILES):
                last = pe.transpose(banks[1][:, t * P:(t + 1) * P], keys[:, t, :], ident[:])
            last.then_inc(kT_ps, 1)

            def absorb(h, u, i):
                pe.wait_ge(ld_head[u], 64 * (i + 1))
                if not (isinstance(h, int) and h < 2):
                    pe.wait_ge(weff_f32, h - 1)
                for c in range(HC):
                    last = pe.matmul(pT[u][:, c * RANK:(c + 1) * RANK], wq_h[:, u, c * P:(c + 1) * P],
                                     wkb[:, bass.ds(h, 1), :], start=True, stop=True)
                last.then_inc(weff_ps, 1)
                if u == 0 and not (isinstance(i, int) and i < 1):
                    pe.wait_ge(wvo_done, i)
                pe.matmul(misc[u * RANK:(u + 1) * RANK, 0:HID], wv_h[:, u, :], wo_h[:, u, :],
                          start=True, stop=True).then_inc(wvo_ps, 1)

            def project_q(h, u):
                pe.wait_ge(weff_split, h + 1)
                if not (isinstance(h, int) and h < 2):
                    pe.wait_ge(qT_done, h - 1)
                for b in range(2):
                    for c in range(HC):
                        last = product3(banks[u][:, b * BANK:(b + 1) * BANK],
                                        (weff_hi[:, u, c, :], weff_lo[:, u, c, :]),
                                        (xT_hi[:, c, b * BANK:(b + 1) * BANK], xT_lo[:, c, b * BANK:(b + 1) * BANK]),
                                        c == 0, c == HC - 1)
                last.then_inc(qT_ps, 1)

            pe.wait_ge(ld_wkb, 16)
            absorb(0, 0, 0)
            absorb(1, 1, 0)
            pe.wait_ge(x_split, 2)
            pe.wait_ge(k_split, 2)
            project_q(0, 0)
            with pe.Fori(1, PAIRS) as j:
                absorb(2 * j, 0, j)
                project_q(2 * j - 1, 1)
                absorb(2 * j + 1, 1, j)
                project_q(2 * j, 0)
            project_q(HEADS - 1, 1)
            pe.wait_ge(qT_done, HEADS)
            pe.wait_ge(weff_f32, HEADS)
            pe.wait_ge(wvo_done, PAIRS)

            def scores(qt, n, u):
                pe.wait_ge(q_split, n + 1)
                if not (isinstance(n, int) and n < 2):
                    pe.wait_ge(probs_ready, n - 1)
                L = (qt + 1) * P
                for b in range(0, L, BANK):
                    w = min(BANK, L - b)
                    diag = b + w == L
                    last = product3(banks[u][:, b:b + w], (q_hi[:, u, :], q_lo[:, u, :]),
                                    (kT_hi[:, b:b + w], kT_lo[:, b:b + w]), True, not diag)
                    if diag:
                        last = pe.matmul(banks[u][:, L - P:L], ident_bf[:], causal[:], start=False, stop=True)
                last.then_inc(scores_ready, 1)

            def transpose_probs(qt, n, u, m=None):
                pe.wait_ge(probs_ready, n + 1)
                for c in range(chunks(qt)):
                    if m is not None and c == 1:
                        pe.wait_ge(ctxT_done, m)
                    bank = pT[u if chunks(qt) == 1 else c]
                    for k in range(4 * c, min(qt + 1, 4 * c + 4)):
                        last = pe.transpose(bank[:, (k % 4) * P:(k % 4 + 1) * P], probs[:, u, k * P:(k + 1) * P],
                                            ident[:])
                    last.then_inc(pT_ps[c], 1)

            def context(qt, n, u, between=None):
                pe.wait_ge(pT_done[0], n + 1)
                if between:
                    if chunks(qt) == 2:
                        pe.wait_ge(pT_done[1], n + 1 - 4 * HEADS)
                    between()
                if past(n, 1):
                    pe.wait_ge(ctx_normed, n)
                for k in range(qt + 1):
                    if k == 4:
                        pe.wait_ge(pT_done[1], n + 1 - 4 * HEADS)
                    last = pe.matmul(ctx_ps, probsT[:, u, k * P:(k + 1) * P], latent[:, k, :],
                                     start=k == 0, stop=k == qt)
                last.then_inc(ctx_ready, 1)

            def transpose_ctx(qt, m):
                pe.wait_ge(ctx_normed, 2 * m + 2)
                pe.transpose(ctxT_ps(qt), ctx_n[:], ident[:]).then_inc(ctxT_psd, 1)

            def output(m, j):
                pe.wait_ge(ctxT_done, m + 1)
                pe.matmul(acc[:, 0:HID], ctxT[:], wvo[:, bass.ds(j * HID, HID)], start=isinstance(j, int) and j == 0,
                          stop=isinstance(j, int) and j == PAIRS - 1).then_inc(acc_ready, 1)

            def transpose_x1(t):
                pe.wait_ge(x1_done, t + 1)
                for c in range(HC):
                    last = pe.transpose(x1T_ps[:, c * P:(c + 1) * P], x1[:, t, c * P:(c + 1) * P], ident[:])
                last.then_inc(x1T_psd, 1)

            def route(t):
                pe.wait_ge(ld_router0, 16)
                pe.wait_ge(x1T_done, t + 1)
                for c in range(HC):
                    last = pe.matmul(logits_ps, x1T[:, c, :], router0[:, c, :], start=c == 0, stop=c == HC - 1)
                last.then_inc(logits_done, 1)

            def count_places(t):
                pe.wait_ge(chosen_done, t + 1)
                pe.matmul(place_ps, ones_bf[:], chosen_before[:, t, :], start=True, stop=False)
                pe.matmul(place_ps, earlier[:], chosen[:, t, :], start=False, stop=True).then_inc(place_done, 1)

            scores(0, 0, 0)
            scores(0, 1, 1)
            for qt in range(TILES):
                def pair(j):
                    m = qt * PAIRS + j
                    transpose_probs(qt, nth(qt, 2 * j), 0)
                    if ahead(qt, j, 0):
                        tile, head, n = ahead(qt, j, 0)
                        scores(tile, n, 0)
                    context(qt, nth(qt, 2 * j), 0)
                    if past(m, 1):
                        transpose_ctx(qt, m - 1)
                        transpose_probs(qt, nth(qt, 2 * j + 1), 1, m)
                    else:
                        transpose_probs(qt, nth(qt, 2 * j + 1), 1)
                    if ahead(qt, j, 1):
                        tile, head, n = ahead(qt, j, 1)
                        scores(tile, n, 1)
                    if qt and isinstance(j, int) and j == 1:
                        pe.wait_ge(acc_read, qt)
                    if past(m, 1):
                        output(m - 1, (j - 1) % PAIRS if isinstance(j, int) else j - 1)
                    if qt >= 2 and isinstance(j, int) and j == 1:
                        context(qt, nth(qt, 2 * j + 1), 1, lambda: count_places(qt - 2))
                        pe.wait_ge(place_read, qt - 1)
                    elif qt and isinstance(j, int) and j == FREE - 1:
                        context(qt, nth(qt, 2 * j + 1), 1, lambda: transpose_x1(qt - 1))
                        pe.wait_ge(x1T_done, qt)
                    elif qt and isinstance(j, int) and j == PAIRS - 1:
                        context(qt, nth(qt, 2 * j + 1), 1, lambda: route(qt - 1))
                        pe.wait_ge(logits_read, qt)
                    else:
                        context(qt, nth(qt, 2 * j + 1), 1)
                pairs_of(pe, pair)
            transpose_ctx(TILES - 1, TILES * PAIRS - 1)
            output(TILES * PAIRS - 1, PAIRS - 1)
            pe.wait_ge(acc_read, TILES)
            pe.wait_ge(ctxT_done, TILES * PAIRS)
            count_places(TILES - 2)
            pe.wait_ge(place_read, TILES - 1)
            transpose_x1(TILES - 1)
            route(TILES - 1)
            pe.wait_ge(logits_read, TILES)
            count_places(TILES - 1)

            def transpose_rows(e, u):
                pe.wait_ge(ld_xe[u // 2], turn(e, u))
                if past(e, 2):
                    pe.wait_ge(xeT_done, e - 1)
                for c in range(HC):
                    last = pe.transpose(pT[u % 2][:, c * P:(c + 1) * P], xe[:, u, c * P:(c + 1) * P], ident[:])
                last.then_inc(xeT_ps, 1)

            def gate_up(e, u):
                b = u % 2
                pe.wait_ge(xeT_done, e + 1)
                pe.wait_ge(ld_gu[u // 2], turn(e, u))
                if past(e, 2):
                    pe.wait_ge(h_done, e - 1)
                for part in range(2):
                    for c in range(HC):
                        last = pe.matmul(half[b][0:I0, part * P:(part + 1) * P],
                                         gu_w[:, u, c, part * I0:(part + 1) * I0], xeT[:, b, c, :],
                                         start=c == 0, stop=c == HC - 1)
                last.then_inc(gu_ready, 1)

            def down(e, u):
                b = u % 2
                pe.wait_ge(h_done, e + 1)
                pe.wait_ge(ld_dn[u // 2], turn(e, u))
                if past(e, 2):
                    pe.wait_ge(ye_done, e - 1)
                pe.matmul(half[2 + b][:, 0:HID], hT[:, b, :], dn_w[:, u, :], start=True, stop=True).then_inc(ye_ps, 1)

            transpose_rows(0, 0)
            transpose_rows(1, 1)
            gate_up(0, 0)
            for e in range(RING):
                transpose_rows(e + 2, (e + 2) % RING)
                gate_up(e + 1, (e + 1) % RING)
                down(e, e)
            with pe.Fori(1, E0 // RING - 1) as i:
                for u in range(RING):
                    transpose_rows(RING * i + u + 2, (u + 2) % RING)
                    gate_up(RING * i + u + 1, (u + 1) % RING)
                    down(RING * i + u, u)
            for e in range(E0 - RING, E0):
                if e + 2 < E0:
                    transpose_rows(e + 2, (e + 2) % RING)
                if e + 1 < E0:
                    gate_up(e + 1, (e + 1) % RING)
                down(e, e % RING)
            def transpose_x2(t, u):
                pe.wait_ge(x2_done, t + 1)
                for c in range(HC):
                    last = pe.transpose(misc[:, c * P:(c + 1) * P], x2[:, u, c * P:(c + 1) * P], ident[:])
                last.then_inc(x2T_psd, 1)

            def project(t, u):
                pe.wait_ge(x2T_done, t + 1)
                if past(t, 2):
                    pe.wait_ge(lu_done, t - 1)
                for m in range(6):
                    bank = rec_ps[u][m // 2]
                    for r in range(HC):
                        o = (m % 2) * HC * P + r * P
                        for c in range(HC):
                            last = pe.matmul(bank[:, o:o + P], w_c[:, m, c, r * P:(r + 1) * P], x2T[:, u, c, :],
                                             start=c == 0, stop=c == HC - 1)
                    if m % 2:
                        last.then_inc((fi_ready, vq_ready, ug_ready)[m // 2], 1)

            def mix(t, u):
                pe.wait_ge(r_done, t + 1)
                pe.wait_ge(lu_done, t + 1)
                if past(t, 1):
                    pe.wait_ge(mix_read, t)
                for m, src in enumerate((readout, local)):
                    for c in range(HC):
                        last = pe.matmul(acc[:, 0:HID], src[:, u, c, :], wo_c[:, m, c, :], start=m + c == 0,
                                         stop=m + c == HC)
                last.then_inc(mix_ready, 1)

            pe.wait_ge(ld_wc, 16)
            pe.wait_ge(ld_woc, 16)
            pe.wait_ge(ye_done, E0)
            transpose_x2(0, 0)
            project(0, 0)
            transpose_x2(1, 1)
            project(1, 1)
            mix(0, 0)
            with pe.Fori(1, TILES // 2) as i:
                for u in range(2):
                    transpose_x2(2 * i + u, u)
                    project(2 * i + u, u)
                    mix(2 * i + u - 1, 1 - u)
            mix(TILES - 1, 1)

            pe.wait_ge(x3_done, TILES)
            for c in range(HC):
                for t in range(TILES):
                    last = pe.transpose(half[2 * c + t // 4][:, t % 4 * P:(t % 4 + 1) * P],
                                        x1[:, t, c * P:(c + 1) * P], ident[:])
                    if t % 4 == 3:
                        last.then_inc(x3T_ps, 1)
            pe.wait_ge(x3T_done, 4)
            pe.wait_ge(ld_router1, 16)
            for t in range(TILES):
                for c in range(HC):
                    last = pe.matmul(misc[:, t * E1:(t + 1) * E1], x3T[:, c, t * P:(t + 1) * P], router1_s[:, c, :],
                                     start=c == 0, stop=c == HC - 1)
            last.then_inc(lg1_ready, 1)
            pe.wait_ge(ch1_done, 1)
            n = TILES * E1
            pe.matmul(acc[:, 0:n], ones_bf[:], cb1[:, 0:TILES, :].rearrange("p t e -> p (t e)"), start=True, stop=False)
            pe.matmul(acc[:, 0:n], earlier[:], ch1[:].rearrange("p t e -> p (t e)"), start=False, stop=True)
            pe.matmul(acc[:, n:n + E1], ones_bf[:], cb1[:, TILES, :], start=True, stop=True).then_inc(pl1_ready, 1)
            pe.wait_ge(ld_sh, 48)
            for b in range(2):
                for k in range(SC):
                    n = b * SC + k
                    if n >= 2:
                        pe.wait_ge(hs_done, n - 1)
                    for bank, w in ((half[n % 2], sh_g), (half[2 + n % 2], sh_u)):
                        for c in range(HC):
                            last = pe.matmul(bank, w[:, c, k * P:(k + 1) * P], x3T[:, c, b * BANK:(b + 1) * BANK],
                                             start=c == 0, stop=c == HC - 1)
                    last.then_inc(gs_ready, 1)
                pe.wait_ge(hs_done, (b + 1) * SC)
                for q in range(4):
                    if 4 * b + q >= 2:
                        pe.wait_ge(sh_read, 4 * b + q - 1)
                    for k in range(SC):
                        last = pe.matmul(pT[q % 2][:, 0:HID], hs[:, k, q * P:(q + 1) * P], sh_d[:, k, :],
                                         start=k == 0, stop=k == SC - 1)
                    last.then_inc(sh_ready, 1)

            def block_T(i, u):
                pe.wait_ge(ld_xd[u], 8 * (i - u) + 16)
                if past(i, 1):
                    pe.wait_ge(xdT_done, i)
                for c in range(HC):
                    last = pe.transpose(misc[:, c * P:(c + 1) * P], xd[:, u, c * P:(c + 1) * P], ident[:])
                last.then_inc(xdT_ps, 1)

            def owner_of(i):
                return pe.value_load(owner_i[0:1, bass.ds(i, 1)], min_val=0, max_val=E1 - 1)

            def block_in(i, u):
                pe.wait_ge(xdT_done, i + 1)
                if past(i, 2):
                    pe.wait_ge(hd_done, i - 1)
                pe.sem_inc(passed, 1)
                e = owner_of(i)
                for part in range(2):
                    for c in range(HC):
                        last = pe.matmul(half[2 * u + part], xdT[:, u, c, :],
                                         w1_s[:, bass.ds(e * (HC * 2 * I1) + (c * 2 * I1 + part * I1), I1)],
                                         start=c == 0, stop=c == HC - 1)
                last.then_inc(f1_ready, 1)

            def block_hT(i, u):
                pe.wait_ge(hd_done, i + 1)
                if past(i, 2):
                    pe.wait_ge(hdT_done, i - 1)
                for c in range(I1 // P):
                    last = pe.transpose(pT[u][:, c * P:(c + 1) * P], hd[:, c * P:(c + 1) * P], ident[:])
                last.then_inc(hdT_ps, 1)

            def block_out(i, u):
                pe.wait_ge(hdT_done, i + 1)
                if past(i, 1):
                    pe.wait_ge(yd_done, i)
                pe.sem_inc(passed, 1)
                e = owner_of(i)
                for c in range(I1 // P):
                    last = pe.matmul(acc[:, 0:HID], hdT[:, u, c * P:(c + 1) * P],
                                     w2_s[:, bass.ds(e * (I1 * HID // P) + c * HID, HID)],
                                     start=c == 0, stop=c == I1 // P - 1)
                last.then_inc(yd_ps, 1)

            def block_pe(i, u):
                if not (isinstance(i, int) and i >= BLOCKS - 2):
                    block_T(i + 2, u)
                block_hT(i, u)
                if not (isinstance(i, int) and i >= BLOCKS - 1):
                    block_in(i + 1, 1 - u)
                block_out(i, u)

            pe.wait_ge(slots1_ready, 2)
            pe.wait_ge(sh_read, TILES)
            pe.wait_ge(ld_w1, 16 * E1)
            pe.wait_ge(ld_w2, 16 * E1)
            block_T(0, 0)
            block_in(0, 0)
            block_T(1, 1)
            block_pe(0, 0)
            block_pe(1, 1)
            with pe.Fori(1, BLOCKS // 2 - 1) as i:
                for u in range(2):
                    block_pe(2 * i + u, u)
            for i in range(BLOCKS - 3, BLOCKS):
                block_pe(i, i % 2)


def kernel(**inputs):
    import numpy as np
    import concourse.bacc as bacc
    from concourse import mybir as mb
    from concourse.bass_utils import run_bass_kernel_spmd as run

    def arr(name):
        return np.asarray(inputs[name])

    wq = arr("L0_attn_q_proj_w")
    laid_out = {
        "x": arr("L0_attn_hidden_states").reshape(T, HID),
        "xT": arr("L0_attn_hidden_states").reshape(T, HID).T,
        "wq": wq,
        "wq_ropeT": wq.reshape(HEADS, QDIM, HID)[:, NOPE:].transpose(2, 0, 1).reshape(HID, HEADS * ROPE),
        "wkv_aT": arr("L0_attn_kv_a_proj_w").T,
        "kv_ln": arr("L0_attn_kv_a_ln_w"),
        "wkv_b": arr("L0_attn_kv_b_proj_w"),
        "woT": arr("L0_attn_o_proj_w").T,
        "router0T": arr("L0_ffn_router_weight").T,
        "gate_up0": arr("L0_ffn_gate_up_proj"),
        "down0": arr("L0_ffn_down_proj"),
        "w_in": np.stack([arr(f"L1_attn_w_{n}") for n in ("f", "i", "v", "q", "up", "gate")]),
        "init_state": arr("L1_attn_init_state").reshape(HC, P).T,
        "w_mix": np.stack([arr("L1_attn_w_ro"), arr("L1_attn_w_down")]),
        "router1": arr("L1_ffn_router_w"),
        "w1": arr("L1_ffn_w1"),
        "w2": arr("L1_ffn_w2"),
        "sh_gate": arr("L1_ffn_w_gate"),
        "sh_up": arr("L1_ffn_w_up"),
        "sh_down": arr("L1_ffn_w_down"),
    }
    nc = bacc.Bacc("TRN2", target_bir_lowering=False, num_devices=1)
    arrays, args = {}, {}
    for name, a in laid_out.items():
        a = np.ascontiguousarray(a)
        arrays[name] = a
        args[name] = nc.dram_tensor(name, a.shape, mb.dt.from_np(a.dtype), kind="ExternalInput").ap()
    out = nc.dram_tensor("result", (T, HID), mb.dt.float32, kind="ExternalOutput").ap()
    build(nc, out=out, **args)
    r = run(nc, [arrays], core_ids=[0])
    return r.results[0]["result"].reshape(1, T, HID)
```

```python
import concourse.bass as bass
from concourse import mybir
from contextlib import ExitStack

P = 128
T, HID = 1024, 256
TILES = T // P
HC = HID // P
HEADS, NOPE, ROPE, VDIM, RANK = 16, 128, 64, 128, 64
QDIM = NOPE + ROPE
PAIRS = HEADS // 2
LN_EPS, RMS_EPS = 1e-5, 1e-6
BANK = 512
MASKED = -1e30
E0, TOP0, CAP, I0 = 64, 8, 128, 96
SLOTS = E0 * CAP
E1, TOP1, I1, SH = 8, 2, 512, 1024
ACT_ROUNDS = 2
FREE = 3
BLOCKS = T * TOP1 // P + E1 - 1
ZEROINGS = SLOTS // T + -(-BLOCKS * P // T)


def build(nc, x, xT, wq, wq_ropeT, wkv_aT, kv_ln, wkv_b, woT, router0T, gate_up0, down0, w_in, init_state,
          w_mix, router1, w1, w2, sh_gate, sh_up, sh_down, out):
    f32, f32r, bf16, i32, u32 = (mybir.dt.float32, mybir.dt.float32r, mybir.dt.bfloat16,
                                 mybir.dt.int32, mybir.dt.uint32)
    ALU, ACT, AX = mybir.AluOpType, mybir.ActivationFunctionType, mybir.AxisListType
    ctx = ExitStack()
    with ctx:
        def sb(name, shape, dt=f32):
            return ctx.enter_context(nc.sbuf_tensor(name, shape, dt))

        def sem(name):
            return ctx.enter_context(nc.semaphore(name))

        def carve(area):
            at = [0]

            def cut(*dims):
                n = 1
                for d in dims:
                    n *= d
                piece = area[:, at[0]:at[0] + n]
                at[0] += n
                if len(dims) == 2:
                    piece = piece.rearrange("p (a b) -> p a b", a=dims[0])
                elif len(dims) == 3:
                    piece = piece.rearrange("p (a b c) -> p a b c", a=dims[0], b=dims[1])
                return piece
            return cut

        area1 = sb("area1", [P, HEADS * T])
        area2 = sb("area2", [P, 4 * HC * T])
        area3 = sb("area3", [P, 8192])
        area4 = sb("area4", [P, 6144])
        cutA2, cutA3, cutB4 = carve(area2), carve(area3), carve(area4)
        cutB3, cutC2, cutC3, cutD3, cutD4 = (carve(a) for a in (area3, area2, area3, area3, area4))
        ident = sb("ident", [P, P])
        ident_bf = sb("ident_bf", [P, P], bf16)
        causal = sb("causal", [P, P], bf16)
        minus_half = sb("minus_half", [P, TILES])
        x_in = cutA2(TILES, HID)
        xT_in = cutA2(HC, T)
        xT_hi = sb("xT_hi", [P, HC, T], f32r)
        xT_lo = sb("xT_lo", [P, HC, T], f32r)
        wkv_a = cutA3(HC, P)
        lnw = sb("lnw", [P, RANK])
        wkb = cutA3(HEADS, RANK)
        wq_h = cutA3(2, HID)
        wv_h = cutA3(2, RANK)
        wo_h = cutA3(2, HID)
        weff = cutA3(2, HC, P)
        weff_hi = sb("weff_hi", [P, 2, HC, P], f32r)
        weff_lo = sb("weff_lo", [P, 2, HC, P], f32r)
        wvo = cutA3(PAIRS * HID)
        qT = area1
        q_hi = sb("q_hi", [P, 2, P], f32r)
        q_lo = sb("q_lo", [P, 2, P], f32r)
        sq = cutA3(TILES, RANK)
        ms = sb("ms", [P, TILES])
        rms = sb("rms", [P, TILES])
        keys = cutA3(TILES, P)
        latent = cutA3(TILES, RANK + 1)
        kT_hi = sb("kT_hi", [P, T], f32r)
        kT_lo = sb("kT_lo", [P, T], f32r)
        neg_max = sb("neg_max", [P, 2])
        probs = cutA2(2, T)
        probsT = cutA2(2, T)
        rsum = sb("rsum", [P, 2])
        ctx_n = sb("ctx_n", [P, P])
        ctxT = sb("ctxT", [P, P])
        y = sb("y", [P, HID])
        zeros_bf = sb("zeros_bf", [P, HID], bf16)
        stats = sb("stats", [P, 6])
        mv = sb("mv", [P, 2, 2])
        rstd = sb("rstd", [P, 2])
        x1 = sb("x1", [P, TILES, HID])

        zero_rows = area4[:, 6144 - 2 * T:]
        cutB4b = carve(area4[:, 1024:])
        router0 = sb("router0", [P, HC, E0])
        earlier = sb("earlier", [P, P], bf16)
        ones_bf = sb("ones_bf", [P, P], bf16)
        iota_e = sb("iota_e", [P, E0])
        spare = cutB4(TILES, TOP0)
        x1T = sb("x1T", [P, HC, P])
        logits = cutB4(E0)
        left = cutB4(E0)
        top_v = cutB4(TILES, TOP0)
        top_i = sb("top_i", [P, TILES, TOP0], u32)
        top_f = cutB4(TILES, TOP0)
        chosen = sb("chosen", [P, TILES, E0], bf16)
        chosen_before = sb("chosen_before", [P, TILES, E0], bf16)
        place = cutB4(E0)
        onehot = wkb.rearrange("p h r -> p (h r)")[:, 0:TOP0 * E0].rearrange("p (a b) -> p a b", a=TOP0)
        placed = wkb.rearrange("p h r -> p (h r)")[:, TOP0 * E0:].rearrange("p (a b) -> p a b", a=TOP0)
        place8 = cutB4(TILES, TOP0)
        valid = sb("valid", [P, TILES, TOP0])
        slot = cutB4(TILES, TOP0)
        slot_t = sb("slot_t", [P, TOP0])
        send_i = sb("send_i", [P, TILES, TOP0], i32)
        fetch_i = sb("fetch_i", [P, TILES, TOP0], i32)
        weight = sb("weight", [P, TILES, TOP0])
        wsum = sb("wsum", [P, TILES])
        RING = 8
        gu_w = cutB4b(RING * HC * 2 * I0).rearrange("p (e c n) -> p e c n", e=RING, c=HC)
        dn_w = cutB4b(RING, HID)[0:I0]
        xe = cutB3(RING, HID)
        xeT = cutB3(2, HC, P)
        sg = cutB3(2, P)[0:I0]
        hT = cutB3(2, P)[0:I0]
        ye = cutB3(RING, HID)
        gathered = cutC2(2, TOP0, HID)
        w_c = cutC2(6, HC, HID)
        wo_c = cutC2(2, HC, HID)
        x2 = cutC3(2, HID)
        forget, igate, value, lgate, state, zq, readout, local = (cutC3(2, HC, P) for _ in range(8))
        x2T = cutC3(2, HC, P)
        y_even, y_odd = cutC3(HID), cutC3(HID)
        init2 = sb("init2", [P, HC])
        send_now = sb("send_now", [P, 2], i32)
        fetch_now = sb("fetch_now", [P, 2, TOP0], i32)
        w1_s = area1
        w2_s = area2
        last_rows = area1[:, 0:TILES * TOP1 * HID].rearrange("p (t k n) -> p t k n", t=TILES, k=TOP1)
        sh_g, sh_u, sh_d = cutD4(HC, SH), cutD4(HC, SH), cutD4(SH // P, HID)
        shared = cutD3(TILES, HID)
        x3T = cutD3(HC, T)
        SC = SH // P
        x3T_hi, x3T_lo = xT_hi, xT_lo
        shw_hi, shw_lo = (k[:].rearrange("p (u m c n) -> p u m c n", u=2, m=2, c=HC) for k in (kT_hi, kT_lo))
        hs = cutD3(SC, BANK)
        cutE3 = carve(area3[:, TILES * HID + HC * T:])
        xd, xdT = cutE3(2, HID), cutE3(2, HC, P)
        hd, hdT = cutE3(BANK), cutE3(2, BANK)
        yd = hs[:, SC - 1, :].rearrange("p (u n) -> p u n", u=2)
        sgd = sb("sgd", [P, 2, BANK])
        router1_s = sb("router1_s", [P, HC, E1])
        iota_b = sb("iota_b", [P, BLOCKS])
        iota_r = sb("iota_r", [P, TILES])
        lg1 = sb("lg1", [P, TILES, E1])
        tv1 = sb("tv1", [P, TILES, E1])
        ti1 = sb("ti1", [P, TILES, E1], u32)
        tf1 = sb("tf1", [P, TILES, E1])
        oh1 = sb("oh1", [P, TILES, TOP1, E1])
        ch1 = sb("ch1", [P, TILES, E1], bf16)
        cb1 = sb("cb1", [P, TILES + 1, E1], bf16)
        pl1 = sb("pl1", [P, TILES + 1, E1])
        blk_cmp = sb("blk_cmp", [P, E1, TILES])
        nblk = sb("nblk", [P, E1])
        ones_e = sb("ones_e", [P, E1])
        blk_end = sb("blk_end", [P, E1])
        blk_start = sb("blk_start", [P, E1])
        own_cmp = sb("own_cmp", [P, BLOCKS, E1])
        owner = sb("owner", [P, BLOCKS])
        owner_i = sb("owner_i", [P, BLOCKS], i32)
        sl1 = sb("sl1", [P, TILES, TOP1])
        slot1 = sb("slot1", [P, TILES, TOP1], i32)
        weight1 = sb("weight1", [P, TILES, TOP1])
        result = area1[:, TILES * TOP1 * HID:TILES * (TOP1 + 1) * HID].rearrange("p (t n) -> p t n", t=TILES)
        xd_d = nc.dram_tensor("xd_d", (BLOCKS * P, HID), f32).ap()
        yd_d = nc.dram_tensor("yd_d", (BLOCKS * P, HID), f32).ap()
        xe_d = nc.dram_tensor("xe_d", (SLOTS + T * TOP0, HID), f32).ap()
        ye_d = nc.dram_tensor("ye_d", (SLOTS, HID), f32).ap()

        banks = [ctx.enter_context(nc.psum_tensor(f"scores{u}", [P, 2 * BANK], f32)) for u in range(2)]
        pT = [ctx.enter_context(nc.psum_tensor(f"probsT_ps{u}", [P, BANK], f32)) for u in range(2)]
        misc = ctx.enter_context(nc.psum_tensor("misc_ps", [P, BANK], f32))
        acc = ctx.enter_context(nc.psum_tensor("acc_ps", [P, BANK], f32))
        CW = RANK + 1
        ctx_ps = misc[:, 0:CW]
        x1T_ps = pT[1][:, 0:HID]
        place_ps = pT[1][:, 0:E0]
        logits_ps = pT[1][:, 0:E0]
        half = [banks[u][:, b * BANK:(b + 1) * BANK] for u in range(2) for b in range(2)]

        ld_x, ld_xT, ld_kv = (sem(n) for n in ("ld_x", "ld_xT", "ld_kv"))
        ld_head = [sem(f"ld_head{u}") for u in range(2)]
        consts, made = sem("consts"), sem("made")
        x_split, kv_ready, sq_done, keys_done, kT_ps, k_split = (
            sem(n) for n in ("x_split", "kv_ready", "sq_done", "keys_done", "kT_ps", "k_split"))
        weff_ps, weff_f32, weff_split, wvo_ps, wvo_done, qT_ps, qT_done = (
            sem(n) for n in ("weff_ps", "weff_f32", "weff_split", "wvo_ps", "wvo_done", "qT_ps", "qT_done"))
        q_half, q_split, scores_ready, max_ready, probs_ready = (
            sem(n) for n in ("q_half", "q_split", "scores_ready", "max_ready", "probs_ready"))
        pT_ps = [sem(f"pT_ps{c}") for c in range(2)]
        pT_done = [sem(f"pT_done{c}") for c in range(2)]
        ctx_ready, rsum_done, ctx_normed, ctxT_psd, ctxT_done, acc_ready, acc_read = (
            sem(n) for n in ("ctx_ready", "rsum_done", "ctx_normed", "ctxT_psd", "ctxT_done", "acc_ready", "acc_read"))
        dve_w, dve_ln = sem("dve_w"), sem("dve_ln")
        dve_step, var_done, rstd_done, x1_done, stored = (
            sem(n) for n in ("dve_step", "var_done", "rstd_done", "x1_done", "stored"))

        block = ctx.enter_context(nc.Block())

        zeroed, ld_router0, x1T_psd, x1T_done, logits_done, logits_read, chosen_done, place_done, place_read, send_done = (
            sem(n) for n in ("zeroed", "ld_router0", "x1T_psd", "x1T_done", "logits_done", "logits_read", "chosen_done",
                             "place_done", "place_read", "send_done"))
        sent = [sem(f"sent0_{u}") for u in range(2)]
        consts0, route_step, exp0, weight_done, fetch_ready = (
            sem(n) for n in ("consts0", "route_step", "exp0", "weight_done", "fetch_ready"))
        ld_gu = [sem(f"ld_gu{u}") for u in range(RING // 2)]
        ld_dn = [sem(f"ld_dn{u}") for u in range(RING // 2)]
        ld_xe = [sem(f"ld_xe{u}") for u in range(RING // 2)]
        st_ye = [sem(f"st_ye{u}") for u in range(RING // 2)]
        xeT_ps, xeT_done, gu_ready, silu_done, h_done, ye_ps, ye_done = (
            sem(n) for n in ("xeT_ps", "xeT_done", "gu_ready", "silu_done", "h_done", "ye_ps", "ye_done"))
        (ld_wc, gath_idx, combined, comb_step, x2_done, x2T_psd, x2T_done, fi_ready, vq_ready,
         ug_ready, gates_done, mid_step, z_done, r_done, lu_done, mix_ready, mix_read, x3_done) = (
            sem(n) for n in ("ld_wc", "gath_idx", "combined", "comb_step", "x2_done", "x2T_psd",
                             "x2T_done", "fi_ready", "vq_ready", "ug_ready", "gates_done", "mid_step", "z_done",
                             "r_done", "lu_done", "mix_ready", "mix_read", "x3_done"))
        gath = [[sem(f"gath{u}_{b}") for b in range(2)] for u in range(2)]
        (ld_w1, ld_w2, ld_sh, ld_router1, x3T_ps, x3T_done, lg1_ready, d_step, ch1_done, pl1_ready, slots1_ready,
         sent1, tanh1, consts1, gs_ready, gs_silu, hs_done, sh_ready, sh_read, last_go) = (
            sem(n) for n in ("ld_w1", "ld_w2", "ld_sh", "ld_router1", "x3T_ps", "x3T_done", "lg1_ready", "d_step",
                             "ch1_done", "pl1_ready", "slots1_ready", "sent1", "tanh1", "consts1", "gs_ready",
                             "gs_silu", "hs_done", "sh_ready", "sh_read", "last_go"))
        ld_xd = [sem(f"ld_xd{u}") for u in range(2)]
        st_yd = [sem(f"st_yd{u}") for u in range(2)]
        (xdT_ps, xdT_done, f1_ready, sgd_done, hd_done, hdT_ps, hdT_done, yd_ps, yd_done, final_step, result_done) = (
            sem(n) for n in ("xdT_ps", "xdT_done", "f1_ready", "sgd_done", "hd_done", "hdT_ps", "hdT_done", "yd_ps",
                             "yd_done", "final_step", "result_done"))
        last_in = [sem(f"last_in{t}") for t in range(TILES)]
        st_out = [sem(f"st_out{u}") for u in range(2)]
        rec_ps = [[half[0], half[1], half[2]], [half[3], pT[0], pT[1]]]
        passed = sem("passed")
        shw_half, shw_split, x3T_half, x3T_split = (sem(n) for n in ("shw_half", "shw_split", "x3T_half", "x3T_split"))
        send_idx = sem("send_idx")

        x1_flat = x1[:].rearrange("p t n -> p (t n)")

        def chain(eng, signal, base=0):
            count = [0]

            def link(ins):
                count[0] += 1
                ins.then_inc(signal, 1)
                eng.wait_ge(signal, base + count[0])
            return link

        def turn(e, u):
            return 16 // RING * (e - u) + 16

        def steps_two(eng, body):
            body(0, 0)
            body(1, 1)
            with eng.Fori(1, TILES // 2 - 1) as i:
                for u in range(2):
                    body(2 * i + u, u)
            body(TILES - 2, 0)
            body(TILES - 1, 1)

        def before(n, end):
            return not isinstance(n, int) or n < end

        def blocks_two(eng, body):
            body(0, 0)
            body(1, 1)
            with eng.Fori(1, BLOCKS // 2) as i:
                for u in range(2):
                    body(2 * i + u, u)
            body(BLOCKS - 1, 0)

        def past(n, first):
            return not isinstance(n, int) or n >= first

        def hold(eng, signal, value):
            eng.wait_ge(signal, value)
            eng.sem_inc(passed, 1)

        def rank2(t):
            return TILES + (t if isinstance(t, int) and t < 2 else 2 * t - 2)

        def rank3(t):
            return TILES + (2 * t + 3 if not isinstance(t, int) or t < TILES - 2 else TILES + t)

        def nth(qt, h):
            return qt * HEADS + h

        def chunks(qt):
            return 1 if qt < 4 else 2

        def ctxT_ps(qt):
            return pT[chunks(qt) - 1][:, 0:P]

        def route_at(qt):
            return PAIRS - 1 if qt < TILES - 1 else FREE

        def pairs_of(eng, body, qt):
            if qt == TILES - 1:
                for j in range(PAIRS):
                    body(j)
                return
            for j in range(FREE):
                body(j)
            with eng.Fori(FREE, PAIRS - 1) as j:
                body(j)
            body(PAIRS - 1)

        def ahead(qt, j, u):
            if isinstance(j, int) and j == PAIRS - 1:
                return None if qt == TILES - 1 else (qt + 1, u, nth(qt + 1, u))
            return qt, 2 * j + 2 + u, nth(qt, 2 * j + 2 + u)

        @block.sync
        def _(sp):
            sp.dma_start(xT_in[:], xT.rearrange("(c p) t -> p c t", p=P)).then_inc(ld_xT, 16)
            sp.dma_start(wkv_a[:], wkv_aT.rearrange("(c p) n -> p c n", p=P)).then_inc(ld_kv, 16)
            sp.dma_start(wkb[:], wkv_b.rearrange("(h a p) r -> a p h r", a=2, p=P)[0]).then_inc(ld_head[0], 16)
            sp.dma_start(lnw[:], bass.AP(kv_ln.tensor, 0, [[0, P], [1, RANK]])).then_inc(ld_head[1], 16)
            wq_v = wq.rearrange("(h d) n -> d h n", d=QDIM)
            wr_v = wq_ropeT.rearrange("(c p) (h r) -> p c h r", p=P, h=HEADS)
            wv_v = wkv_b.rearrange("(h a p) r -> a p h r", a=2, p=P)[1]
            wo_v = woT.rearrange("(h p) n -> p h n", p=P)

            def load_head(h, u):
                sp.dma_start(wq_h[:, u, :], wq_v[0:P, h, :]).then_inc(ld_head[u], 16)
                sp.dma_start(weff[:, u, :, RANK:], wr_v[:, :, h, :]).then_inc(ld_head[u], 16)
                sp.dma_start(wv_h[:, u, :], wv_v[:, h, :]).then_inc(ld_head[u], 16)
                sp.dma_start(wo_h[:, u, :], wo_v[:, h, :]).then_inc(ld_head[u], 16)

            load_head(0, 0)
            load_head(1, 1)
            sp.dma_start(x_in[:], x.rearrange("(t p) n -> p t n", p=P)).then_inc(ld_x, 16)
            with sp.Fori(1, PAIRS) as j:
                for u in range(2):
                    sp.wait_ge(wvo_ps, 2 * j - 1 + u)
                    sp.wait_ge(weff_split, 2 * j - 1 + u)
                    for dst, src in ((wq_h[:, u, :], wq_v[0:P, bass.ds(2 * j + u, 1), :]),
                                     (weff[:, u, :, RANK:], wr_v[:, :, bass.ds(2 * j + u, 1), :]),
                                     (wv_h[:, u, :], wv_v[:, bass.ds(2 * j + u, 1), :]),
                                     (wo_h[:, u, :], wo_v[:, bass.ds(2 * j + u, 1), :])):
                        sp.dma_start(dst, src).then_inc(ld_head[u], 16)
            sp.dma_start(router0[:], router0T.rearrange("(c p) e -> p c e", p=P)).then_inc(ld_router0, 16)
            sp.wait_ge(consts0, 1)
            for b in range(SLOTS // T):
                sp.dma_start(xe_d[b * T:(b + 1) * T, :].rearrange("(p a) n -> p (a n)", p=P),
                             zero_rows[:]).then_inc(zeroed, 16)
            for b in range(0, BLOCKS * P, T):
                n = min(T, BLOCKS * P - b)
                sp.dma_start(xd_d[b:b + n, :].rearrange("(p a) n -> p (a n)", p=P),
                             zero_rows[:, 0:n * HID // P]).then_inc(zeroed, 16)
            gu_v = gate_up0.rearrange("e (c p) f -> p e c f", p=P)
            dn_v = down0.rearrange("e i n -> i e n")
            xe_v = xe_d[0:SLOTS, :].rearrange("(e p) n -> p e n", p=P)

            def load_weights(e, u):
                if past(e, RING):
                    sp.wait_ge(ye_ps, e + 2 - RING)
                sp.dma_start(gu_w[:, u:u + 2], gu_v[:, bass.ds(e, 2)]).then_inc(ld_gu[u // 2], 16)
                sp.dma_start(dn_w[:, u:u + 2, :], dn_v[:, bass.ds(e, 2), :]).then_inc(ld_dn[u // 2], 16)

            def load_rows(e, u):
                if past(e, RING):
                    sp.wait_ge(xeT_ps, e + 2 - RING)
                sp.dma_start(xe[:, u:u + 2, :], xe_v[:, bass.ds(e, 2), :]).then_inc(ld_xe[u // 2], 16)

            sp.wait_ge(zeroed, 16 * ZEROINGS)
            for e in range(0, RING, 2):
                load_weights(e, e)
            sp.wait_ge(x1_done, TILES)
            sp.dma_start(w_c, w_in.rearrange("m (c p) n -> p m c n", p=P)).then_inc(ld_wc, 16)
            sp.dma_start(wo_c, w_mix.rearrange("m (c p) n -> p m c n", p=P)).then_inc(ld_wc, 16)
            sp.dma_start(init2[:], init_state).then_inc(ld_router1, 16)
            sp.dma_start(router1_s[:], router1.rearrange("(c p) e -> p c e", p=P)).then_inc(ld_router1, 16)

            def load_w1(e):
                sp.dma_start(w1_s[:, e * HC * 2 * I1:(e + 1) * HC * 2 * I1].rearrange("p (c f) -> p c f", c=HC),
                             w1[e].rearrange("(c p) f -> p c f", p=P)).then_inc(ld_w1, 16)

            load_w1(0)
            load_w1(1)
            for u in range(2):
                sp.wait_ge(sent[u], 16 * TILES * TOP0 // 2)
            for e in range(0, RING, 2):
                load_rows(e, e)
            with sp.Fori(1, E0 // RING) as i:
                for u in range(0, RING, 2):
                    load_rows(RING * i + u, u)
                    load_weights(RING * i + u, u)
            sp.wait_ge(ye_ps, E0)
            loads_sh = ((sh_g, sh_gate.rearrange("(c p) f -> p c f", p=P)), (sh_u, sh_up.rearrange("(c p) f -> p c f", p=P)),
                        (sh_d, sh_down.rearrange("(c p) n -> p c n", p=P)))
            for t in range(TILES):
                sp.wait_ge(combined, t + 1)
                if t + 2 < E1:
                    load_w1(t + 2)
                if t >= TILES - 3:
                    dst, src = loads_sh[t - TILES + 3]
                    sp.dma_start(dst, src).then_inc(ld_sh, 16)
            sp.wait_ge(x3_done, TILES)
            for e in range(E1):
                sp.dma_start(w2_s[:, e * I1 * HID // P:(e + 1) * I1 * HID // P].rearrange("p (c n) -> p c n", n=HID),
                             w2[e].rearrange("(c p) n -> p c n", p=P)).then_inc(ld_w2, 16)
            xd_v = xd_d.rearrange("(i p) n -> p i n", p=P)

            def load_block(i, u):
                if past(i, 2):
                    sp.wait_ge(xdT_ps, i - 1)
                sp.dma_start(xd[:, u, :], xd_v[:, bass.ds(i, 1), :]).then_inc(ld_xd[u], 16)

            sp.wait_ge(sh_ready, TILES // 2)
            sp.wait_ge(sent1, 16 * TILES * TOP1)
            blocks_two(sp, load_block)
            for t in range(TILES):
                sp.wait_ge(result_done, t + 1)
                sp.dma_start(out[t * P:(t + 1) * P, :], result[:, t, :]).then_inc(st_out[t % 2], 16)
            for u in range(2):
                sp.wait_ge(st_out[u], 16 * TILES // 2)

        @block.gpsimd
        def _(pool):
            pool.memset(ident[:], 0.0).then_inc(made, 1)
            pool.memset(causal[:], 0.0).then_inc(made, 1)
            pool.memset(minus_half[:], -0.5).then_inc(made, 1)
            pool.memset(zeros_bf[:], 0.0).then_inc(made, 1)
            pool.wait_ge(made, 4)
            pool.affine_select(out=ident[:], in_=ident[:], compare_op=ALU.not_equal, fill=1.0, base=0,
                               pattern=[[-1, P]], channel_multiplier=1).then_inc(made, 1)
            pool.affine_select(out=causal[:], in_=causal[:], compare_op=ALU.is_ge, fill=MASKED, base=0,
                               pattern=[[-1, P]], channel_multiplier=1).then_inc(made, 1)
            pool.memset(latent[:, :, RANK:], 1.0)
            pool.wait_ge(made, 6)
            pool.tensor_copy(ident_bf[:], ident[:]).then_inc(consts, 1)
            pool.memset(zero_rows[:], 0.0).then_inc(consts0, 1)
            pool.memset(ones_bf[:], 1.0).then_inc(made, 1)
            pool.memset(earlier[:], 1.0).then_inc(made, 1)
            pool.memset(chosen_before[:, 0, :], 0.0).then_inc(made, 1)
            pool.wait_ge(made, 9)
            pool.affine_select(out=earlier[:], in_=earlier[:], compare_op=ALU.is_gt, fill=0.0, base=0,
                               pattern=[[1, P]], channel_multiplier=-1).then_inc(consts0, 1)
            pool.iota(iota_e[:], pattern=[[1, E0]], base=0, channel_multiplier=0,
                      allow_small_or_imprecise_dtypes=True).then_inc(consts0, 1)
            pool.iota(spare, pattern=[[P, TILES], [T, TOP0]], base=SLOTS, channel_multiplier=1,
                      allow_small_or_imprecise_dtypes=True).then_inc(consts0, 1)
            pool.iota(iota_b[:], pattern=[[1, BLOCKS]], base=0, channel_multiplier=0,
                      allow_small_or_imprecise_dtypes=True).then_inc(consts1, 1)
            pool.iota(iota_r[:], pattern=[[P, TILES]], base=0, channel_multiplier=0,
                      allow_small_or_imprecise_dtypes=True).then_inc(consts1, 1)
            pool.memset(ones_e[:], 1.0).then_inc(consts1, 1)
            pool.memset(cb1[:, 0, :], 0.0).then_inc(consts1, 1)
            pool.wait_ge(dve_step, 2)
            pool.tensor_tensor(rms[:], ms[:], minus_half[:], ALU.pow).then_inc(dve_step, 1)

            def split_q(qt, h, u, n):
                if qt < ACT_ROUNDS:
                    if past(n, 2):
                        pool.wait_ge(scores_ready, n - 1)
                    pool.sem_inc(passed, 1)
                    pool.tensor_copy(q_hi[:, u, :], qT[:, bass.ds(h * T + qt * P, P)]).then_inc(q_half, 1)
                hold(pool, q_half, n + 1)
                pool.tensor_tensor(q_lo[:, u, :], qT[:, bass.ds(h * T + qt * P, P)], q_hi[:, u, :].bitcast(f32),
                                   ALU.subtract).then_inc(q_split, 1)

            def rstd_of(k, s=0):
                pool.wait_ge(var_done, k + 1)
                pool.tensor_tensor(rstd[:, s:s + 1], mv[:, s, 1:2], minus_half[:, 0:1], ALU.pow).then_inc(rstd_done, 1)

            pool.wait_ge(qT_done, HEADS - 1)

            def send(t, first, behind):
                pool.wait_ge(send_done, t + 1)
                for k in range(first, behind):
                    pool.indirect_dma_start(xe_d, bass.IndirectOffsetOnAxis(send_i[:, t, k:k + 1], 0),
                                            x1[:, t, :], None).then_inc(sent[k % 2], 16)

            def send_one(t, j, u):
                pool.wait_ge(send_done, t + 1)
                if not (isinstance(j, int) and 4 * t - FREE + j == 0):
                    hold(pool, sent[u], 16 * (4 * t - FREE + j))
                pool.tensor_copy(send_now[:, u:u + 1],
                                 send_flat[:, bass.ds(t * TOP0 + 2 * (j - FREE) + u, 1)]).then_inc(send_idx, 1)
                hold(pool, send_idx, t * TOP0 + 2 * (j - FREE) + u + 1)
                pool.indirect_dma_start(xe_d, bass.IndirectOffsetOnAxis(send_now[:, u:u + 1], 0),
                                        x1[:, t, :], None).then_inc(sent[u], 16)

            send_flat = send_i[:].rearrange("p t k -> p (t k)")
            split_q(0, 0, 0, 0)
            split_q(0, 1, 1, 1)
            pool.wait_ge(qT_done, HEADS)
            for qt in range(TILES):
                def pair(j):
                    for u in range(2):
                        if ahead(qt, j, u):
                            tile, head, n = ahead(qt, j, u)
                            split_q(tile, head, u, n)
                        if qt >= 2 and past(j, FREE) and before(j, PAIRS - 1):
                            send_one(qt - 2, j, u)
                    if qt and isinstance(j, int) and j == 1:
                        rstd_of(qt - 1)
                    if qt == TILES - 1 and j >= FREE + 3:
                        send(TILES - 2, 4 * (j - FREE - 3), 4 * (j - FREE - 2))
                if qt == 2:
                    pool.wait_ge(zeroed, 16 * ZEROINGS)
                pairs_of(pool, pair, qt)
            rstd_of(TILES - 1)
            send(TILES - 1, 0, TOP0)
            def fetch(t, u, first, behind):
                if first == 0:
                    if past(t, 2):
                        pool.wait_ge(combined, t - 1)
                    pool.sem_inc(passed, 1)
                    pool.tensor_copy(fetch_now[:, u, :], fetch_flat[:, bass.ds(t * TOP0, TOP0)]).then_inc(gath_idx, 1)
                    hold(pool, gath_idx, t + 1)
                for k in range(first, behind):
                    pool.indirect_dma_start(gathered[:, u, k, :], None, ye_d,
                                            bass.IndirectOffsetOnAxis(fetch_now[:, u, k:k + 1], 0)).then_inc(gath[u][2 * k // TOP0], 16)

            fetch_flat = fetch_i[:].rearrange("p t k -> p (t k)")
            pool.wait_ge(weight_done, 1)
            for u in range(RING // 2):
                pool.wait_ge(st_ye[u], 16 * E0 // RING)
            part = 6
            fetch(0, 0, 0, TOP0)
            fetch(1, 1, 0, part)
            rstd_of(rank2(0), 0)
            fetch(1, 1, part, TOP0)

            def roots_and_rows(t, u):
                if before(t, TILES - 2):
                    fetch(t + 2, u, 0, part)
                if before(t, TILES - 1):
                    rstd_of(rank2(t + 1), 0)
                if before(t, TILES - 2):
                    fetch(t + 2, u, part, TOP0)
                if past(t, 1):
                    rstd_of(rank3(t - 1), 1)
            steps_two(pool, roots_and_rows)
            rstd_of(rank3(TILES - 1), 1)
            pool.wait_ge(slots1_ready, 1)
            for t in range(TILES):
                for k in range(TOP1):
                    pool.indirect_dma_start(xd_d, bass.IndirectOffsetOnAxis(slot1[:, t, k:k + 1], 0),
                                            x1[:, t, :], None).then_inc(sent1, 16)
            pool.wait_ge(st_yd[0], 16 * (BLOCKS - BLOCKS // 2))
            pool.wait_ge(st_yd[1], 16 * (BLOCKS // 2))
            for t in range(TILES):
                for k in range(TOP1):
                    pool.indirect_dma_start(last_rows[:, t, k, :], None, yd_d,
                                            bass.IndirectOffsetOnAxis(slot1[:, t, k:k + 1], 0)).then_inc(last_in[t], 16)
            for t in range(TILES):
                rstd_of(3 * TILES + t, t % 2)

        @block.scalar
        def _(act):
            act.wait_ge(kv_ready, 1)
            act.activation(sq[:], banks[1][:].rearrange("p (t n) -> p t n", t=TILES)[:, :, 0:RANK],
                           ACT.Square).then_inc(sq_done, 1)

            def weff_copy(h, u):
                act.wait_ge(weff_ps, h + 1)
                act.copy(weff[:, u, :, 0:RANK],
                         pT[u][:, 0:HC * RANK].rearrange("p (c r) -> p c r", c=HC)).then_inc(weff_f32, 1)

            def q_copy(h, u):
                hold(act, qT_ps, h + 1)
                act.activation(qT[:, bass.ds(h * T, T)], banks[u][:], ACT.Copy,
                               scale=float(QDIM) ** -0.5).then_inc(qT_done, 1)

            weff_copy(0, 0)
            weff_copy(1, 1)
            q_copy(0, 0)
            with act.Fori(1, PAIRS) as j:
                weff_copy(2 * j, 0)
                q_copy(2 * j - 1, 1)
                weff_copy(2 * j + 1, 1)
                q_copy(2 * j, 0)
            q_copy(HEADS - 1, 1)

            def exp_probs(qt, n, u):
                L = (qt + 1) * P
                act.wait_ge(max_ready, n + 1)
                if past(n, 2):
                    act.wait_ge(pT_ps[0], n - 1)
                    if qt > 4 or qt == 4 and past(n, nth(4, 2)):
                        act.wait_ge(pT_ps[1], n - 1 - 4 * HEADS)
                act.activation(probs[:, u, 0:L], banks[u][:, 0:L], ACT.Exp,
                               bias=neg_max[:, u:u + 1]).then_inc(probs_ready, 1)

            def copy_pT(qt, n, u):
                w = min(qt + 1, 4) * P
                act.wait_ge(pT_ps[0], n + 1)
                act.copy(probsT[:, u, 0:w], pT[u if chunks(qt) == 1 else 0][:, 0:w]).then_inc(pT_done[0], 1)

            def copy_ctxT(qt, m):
                act.wait_ge(ctxT_psd, m + 1)
                act.copy(ctxT[:], ctxT_ps(qt)).then_inc(ctxT_done, 1)

            def copy_x1T(t):
                act.wait_ge(x1T_psd, t + 1)
                if t:
                    act.wait_ge(logits_done, t)
                act.copy(x1T[:], x1T_ps.rearrange("p (c n) -> p c n", c=HC)).then_inc(x1T_done, 1)

            def round_q(qt, h, u, n):
                if qt < ACT_ROUNDS:
                    return
                if isinstance(n, int) and n == nth(ACT_ROUNDS, 0):
                    act.wait_ge(q_split, n)
                hold(act, scores_ready, n - 1)
                act.activation(q_hi[:, u, :], qT[:, bass.ds(h * T + qt * P, P)], ACT.Copy).then_inc(q_half, 1)

            act.wait_ge(qT_done, HEADS)
            exp_probs(0, 0, 0)
            for qt in range(TILES):
                def pair(j):
                    if ahead(qt, j, 0):
                        tile, head, n = ahead(qt, j, 0)
                        round_q(tile, head, 0, n)
                    copy_pT(qt, nth(qt, 2 * j), 0)
                    exp_probs(qt, nth(qt, 2 * j + 1), 1)
                    if ahead(qt, j, 1):
                        tile, head, n = ahead(qt, j, 1)
                        round_q(tile, head, 1, n)
                    if past(qt * PAIRS + j, 1):
                        copy_ctxT(qt, qt * PAIRS + j - 1)
                    copy_pT(qt, nth(qt, 2 * j + 1), 1)
                    if ahead(qt, j, 0):
                        tile, head, n = ahead(qt, j, 0)
                        exp_probs(tile, n, 0)
                    if qt and isinstance(j, int) and j == FREE - 1:
                        copy_x1T(qt - 1)
                pairs_of(act, pair, qt)
            copy_ctxT(TILES - 1, TILES * PAIRS - 1)
            copy_x1T(TILES - 1)
            act.wait_ge(exp0, 1)
            act.activation(weight[:], weight[:], ACT.Exp).then_inc(exp0, 1)

            def expert_act(e, u):
                b = u % 2
                act.wait_ge(gu_ready, e + 1)
                act.activation(sg[:, b, :], half[b][0:I0, 0:P], ACT.Silu).then_inc(silu_done, 1)

            ye_v = ye_d.rearrange("(e p) n -> p e n", p=P)

            def expert_out(e, u):
                act.wait_ge(ye_ps, e + 1)
                if past(e, RING) and u % 2 == 0:
                    act.wait_ge(st_ye[u // 2], turn(e, u) - 16)
                act.copy(ye[:, u, :], half[2 + u % 2][:, 0:HID]).then_inc(ye_done, 1)
                if u % 2:
                    act.wait_ge(ye_done, e + 1)
                    act.dma_start(ye_v[:, bass.ds(e - 1, 2), :], ye[:, u - 1:u + 1, :]).then_inc(st_ye[u // 2], 16)

            expert_act(0, 0)
            for e in range(RING):
                expert_act(e + 1, (e + 1) % RING)
                expert_out(e, e)
            with act.Fori(1, E0 // RING - 1) as i:
                for u in range(RING):
                    expert_act(RING * i + u + 1, (u + 1) % RING)
                    expert_out(RING * i + u, u)
            for e in range(E0 - RING, E0):
                if e + 1 < E0:
                    expert_act(e + 1, (e + 1) % RING)
                expert_out(e, e % RING)
            def copy_x2T(t, u):
                act.wait_ge(x2T_psd, t + 1)
                act.copy(x2T[:, u], x1T_ps_c).then_inc(x2T_done, 1)
                hold(act, x2_done, t + 1)
                act.activation(x1_flat[:, bass.ds(t * HID, HID)], x2[:, u, :], ACT.Copy).then_inc(x2T_done, 1)

            def of(ap):
                return ap.rearrange("p (c n) -> p c n", c=HC)

            def gates(t, u):
                (a, b, c), n = rec_ps[u], HC * P
                act.wait_ge(fi_ready, t + 1)
                if past(t, 2):
                    act.wait_ge(lu_done, t - 1)
                act.activation(forget[:, u], of(a[:, 0:n]), ACT.Tanh).then_inc(gates_done, 1)
                act.activation(igate[:, u], of(a[:, n:]), ACT.Tanh, scale=0.5).then_inc(gates_done, 1)
                act.wait_ge(vq_ready, t + 1)
                act.activation(value[:, u], of(b[:, 0:n]), ACT.Silu).then_inc(gates_done, 1)
                if before(t, TILES - 1):
                    copy_x2T(t + 1, 1 - u)
                act.wait_ge(ug_ready, t + 1)
                act.activation(lgate[:, u], of(c[:, n:]), ACT.Silu).then_inc(gates_done, 1)
                read_out(t, u)

            def read_out(t, u):
                act.wait_ge(z_done, t + 1)
                if past(t, 2):
                    act.wait_ge(mix_ready, t - 1)
                act.activation(readout[:, u], zq[:, u], ACT.Silu, scale=0.5).then_inc(r_done, 1)

            x1T_ps_c = misc[:, 0:HID].rearrange("p (c n) -> p c n", c=HC)
            copy_x2T(0, 0)
            steps_two(act, gates)
            for b in range(2):
                act.wait_ge(x3T_ps, b + 1)
                act.copy(x3T[:, 0, b * BANK:(b + 1) * BANK], half[b]).then_inc(x3T_done, 1)

            def round_weights(n):
                k = n % SC
                if n >= 2:
                    act.wait_ge(gs_ready, n - 1)
                for m, w in enumerate((sh_g, sh_u)):
                    act.copy(shw_hi[:, n % 2, m], w[:, :, k * P:(k + 1) * P]).then_inc(shw_half, 1)

            act.wait_ge(x3T_done, 4)
            act.wait_ge(ld_sh, 48)
            round_weights(0)
            for b in range(2):
                for c in range(HC):
                    act.copy(x3T_hi[:, c, b * BANK:(b + 1) * BANK],
                             x3T[:, c, b * BANK:(b + 1) * BANK]).then_inc(x3T_half, 1)
            round_weights(1)
            act.wait_ge(tanh1, 1)
            act.activation(weight1[:, :, 1:2], weight1[:, :, 0:1], ACT.Tanh, scale=0.5).then_inc(tanh1, 1)

            def shared_act(b):
                for n in range(b * SC, (b + 1) * SC):
                    act.wait_ge(gs_ready, n + 1)
                    if n >= 2:
                        act.wait_ge(hs_done, n - 1)
                    act.activation(sgd[:, n % 2, :], half[n % 2], ACT.Silu).then_inc(gs_silu, 1)
                    if n + 2 < 2 * SC:
                        round_weights(n + 2)

            shared_act(0)

            def block_act(i, u):
                act.wait_ge(f1_ready, i + 1)
                if past(i, 2):
                    act.wait_ge(hd_done, i - 1)
                act.activation(sgd[:, u, :], half[2 * u], ACT.Silu).then_inc(sgd_done, 1)

            def block_T(i, u):
                act.wait_ge(xdT_ps, i + 1)
                if past(i, 2):
                    act.wait_ge(f1_ready, i - 1)
                act.copy(xdT[:, u], x1T_ps_c).then_inc(xdT_done, 1)

            def block_out(i, u):
                act.wait_ge(yd_ps, i + 1)
                if past(i, 2):
                    act.wait_ge(st_yd[u], 8 * (i - u))
                act.copy(yd[:, u, :], acc[:, 0:HID]).then_inc(yd_done, 1)
                act.wait_ge(yd_done, i + 1)
                act.dma_start(yd_v[:, bass.ds(i, 1), :], yd[:, u, :]).then_inc(st_yd[u], 16)

            yd_v = yd_d.rearrange("(i p) n -> p i n", p=P)
            act.wait_ge(hs_done, SC)
            block_T(0, 0)
            block_act(0, 0)
            block_T(1, 1)

            def block_steps(i, u):
                if not (isinstance(i, int) and i >= BLOCKS - 2):
                    block_T(i + 2, u)
                if not (isinstance(i, int) and i >= BLOCKS - 1):
                    block_act(i + 1, 1 - u)
                block_out(i, u)

            block_steps(0, 0)
            block_steps(1, 1)
            with act.Fori(1, BLOCKS // 2 - 1) as i:
                for u in range(2):
                    block_steps(2 * i + u, u)
            for i in range(BLOCKS - 3, BLOCKS):
                block_steps(i, i % 2)
            act.wait_ge(hd_done, BLOCKS)
            shared_act(1)

        @block.vector
        def _(dve):
            dve.wait_ge(ld_xT, 16)
            dve.tensor_copy(xT_hi[:], xT_in[:]).then_inc(x_split, 1)
            dve.wait_ge(x_split, 1)
            dve.tensor_tensor(xT_lo[:], xT_in[:], xT_hi[:].bitcast(f32), ALU.subtract).then_inc(x_split, 1)
            def split_weff(h, u, i):
                dve.wait_ge(weff_f32, h + 1)
                dve.wait_ge(ld_head[u], 16 + 64 * (i + 1))
                if not (isinstance(h, int) and h < 2):
                    dve.wait_ge(qT_ps, h - 1)
                dve.tensor_copy(weff_hi[:, u], weff[:, u]).then_inc(dve_w, 1)
                dve.wait_ge(dve_w, h + 1)
                dve.tensor_tensor(weff_lo[:, u], weff[:, u], weff_hi[:, u].bitcast(f32),
                                  ALU.subtract).then_inc(weff_split, 1)

            def wvo_copy(m):
                hold(dve, wvo_ps, 2 * m + 2)
                dve.tensor_copy(wvo[:, bass.ds(m * HID, HID)], misc[:, 0:HID]).then_inc(wvo_done, 1)

            kv_ps = banks[1][:].rearrange("p (t n) -> p t n", t=TILES)
            dve.wait_ge(sq_done, 1)
            dve.tensor_reduce(ms[:], sq[:], AX.X, ALU.add).then_inc(dve_step, 1)
            dve.wait_ge(dve_step, 1)
            dve.tensor_scalar(ms[:], ms[:], 1.0 / RANK, RMS_EPS, ALU.mult, ALU.add).then_inc(dve_step, 1)
            split_weff(0, 0, 0)
            split_weff(1, 1, 0)
            dve.tensor_copy(keys[:, :, RANK:], kv_ps[:, :, RANK:]).then_inc(keys_done, 1)
            dve.wait_ge(dve_step, 3)
            dve.wait_ge(ld_head[1], 16 + 64)
            for t in range(TILES):
                dve.scalar_tensor_tensor(keys[:, t, 0:RANK], kv_ps[:, t, 0:RANK], rms[:, t:t + 1], lnw[:],
                                         ALU.mult, ALU.mult).then_inc(keys_done, 1)
            dve.wait_ge(keys_done, TILES + 1)
            dve.tensor_copy(latent[:, :, 0:RANK], keys[:, :, 0:RANK])
            dve.wait_ge(kT_ps, 1)
            dve.tensor_copy(kT_hi[:], banks[1][:]).then_inc(k_split, 1)
            dve.wait_ge(k_split, 1)
            dve.tensor_tensor(kT_lo[:], banks[1][:], kT_hi[:].bitcast(f32), ALU.subtract).then_inc(k_split, 1)

            wvo_copy(0)
            with dve.Fori(1, PAIRS) as j:
                split_weff(2 * j, 0, j)
                split_weff(2 * j + 1, 1, j)
                wvo_copy(j)

            def row_max(qt, n, u):
                dve.wait_ge(scores_ready, n + 1)
                dve.tensor_reduce(neg_max[:, u:u + 1], banks[u][:, 0:(qt + 1) * P], AX.X, ALU.max,
                                  negate=True).then_inc(max_ready, 1)

            def copy_pT(qt, n, u):
                if chunks(qt) == 2:
                    dve.wait_ge(pT_ps[1], n + 1 - 4 * HEADS)
                    w = (qt + 1 - 4) * P
                    dve.tensor_copy(probsT[:, u, BANK:BANK + w], pT[1][:, 0:w]).then_inc(pT_done[1], 1)

            def norm_ctx(n, u, m=0):
                dve.wait_ge(ctx_ready, n + 1)
                dve.reciprocal(rsum[:, u:u + 1], ctx_ps[:, RANK:]).then_inc(rsum_done, 1)
                dve.wait_ge(rsum_done, n + 1)
                if u == 0 and not (isinstance(m, int) and m < 1):
                    dve.wait_ge(ctxT_psd, m)
                dve.tensor_scalar(ctx_n[:, u * RANK:(u + 1) * RANK], ctx_ps[:, 0:RANK],
                                  rsum[:, u:u + 1], None, ALU.mult).then_inc(ctx_normed, 1)

            def variance(k, src, eps, s=0):
                dve.bn_stats(stats[:], src).then_inc(dve_ln, 1)
                hold(dve, dve_ln, 2 * k + 1)
                dve.bn_aggr(mv[:, s, :], stats[:]).then_inc(dve_ln, 1)
                dve.wait_ge(dve_ln, 2 * k + 2)
                dve.tensor_scalar(mv[:, s, 1:2], mv[:, s, 1:2], eps, None, ALU.add).then_inc(var_done, 1)

            def normalise(k, src, dst, s=0):
                dve.wait_ge(rstd_done, k + 1)
                return dve.tensor_scalar(dst, src, mv[:, s, 0:1], rstd[:, s:s + 1], ALU.subtract, ALU.mult)

            def layernorm(k, src, dst, eps):
                variance(k, src, eps)
                return normalise(k, src, dst)

            def add_residual(qt):
                dve.wait_ge(acc_ready, (qt + 1) * PAIRS)
                dve.wait_ge(ld_x, 16)
                dve.tensor_tensor(y[:], acc[:, 0:HID], x_in[:, qt, :], ALU.add).then_inc(acc_read, 1)
                dve.wait_ge(acc_read, qt + 1)
                variance(qt, y[:], LN_EPS)

            def finish_tile(qt):
                normalise(qt, y[:], x1[:, qt, :]).then_inc(x1_done, 1)

            def read_place(t):
                dve.wait_ge(place_done, t + 1)
                dve.tensor_copy(place, place_ps).then_inc(place_read, 1)

            def read_logits(t):
                dve.wait_ge(logits_done, t + 1)
                dve.tensor_copy(logits, logits_ps).then_inc(logits_read, 1)

            def choose(t):
                link = chain(dve, route_step, 13 * t)
                dve.wait_ge(logits_read, t + 1)
                link(dve.max(top_v[:, t, :], logits))
                link(dve.max_index(top_i[:, t, :], top_v[:, t, :], logits))
                link(dve.match_replace(left, top_v[:, t, :], logits, -3e38))
                link(dve.tensor_tensor(chosen[:, t, :], logits, left, ALU.not_equal))
                if t + 1 < TILES:
                    link(dve.tensor_tensor(chosen_before[:, t + 1, :], chosen_before[:, t, :], chosen[:, t, :], ALU.add))
                else:
                    dve.sem_inc(route_step, 1)
                dve.tensor_copy(top_f[:, t, :], top_i[:, t, :]).then_inc(chosen_done, 1)

            def assign(t):
                link = chain(dve, route_step, 13 * t + 5)
                dve.wait_ge(place_read, t + 1)
                dve.wait_ge(chosen_done, t + 1)
                shape = [P, TOP0, E0]
                dve.wait_ge(consts0, 4)
                link(dve.tensor_tensor(onehot, iota_e[:].unsqueeze(1).broadcast_to(shape),
                                       top_f[:, t, :].unsqueeze(2).broadcast_to(shape), ALU.is_equal))
                link(dve.tensor_tensor(placed, onehot, place.unsqueeze(1).broadcast_to(shape), ALU.mult))
                yield
                link(dve.tensor_reduce(place8[:, t, :], placed, AX.X, ALU.add))
                dve.tensor_scalar(valid[:, t, :], place8[:, t, :], float(CAP), None, ALU.is_lt)
                link(dve.tensor_scalar(slot_t[:], place8[:, t, :], float(CAP - 1), None, ALU.min))
                link(dve.scalar_tensor_tensor(slot[:, t, :], top_f[:, t, :], float(CAP), slot_t[:], ALU.mult, ALU.add))
                link(dve.tensor_tensor(slot_t[:], slot[:, t, :], spare[:, t, :], ALU.subtract))
                link(dve.tensor_tensor(slot_t[:], slot_t[:], valid[:, t, :], ALU.mult))
                link(dve.tensor_copy(fetch_i[:, t, :], slot[:, t, :]))
                dve.tensor_tensor(send_i[:, t, :], slot_t[:], spare[:, t, :], ALU.add).then_inc(send_done, 1)
                yield

            row_max(0, 0, 0)
            row_max(0, 1, 1)
            for qt in range(TILES):
                parts = assign(qt - 2) if qt >= 2 else None

                def pair(j):
                    if past(nth(qt, 2 * j), 1):
                        norm_ctx(nth(qt, 2 * j - 1), 1)
                    copy_pT(qt, nth(qt, 2 * j), 0)
                    if ahead(qt, j, 0):
                        tile, head, n = ahead(qt, j, 0)
                        row_max(tile, n, 0)
                    if qt and isinstance(j, int) and j == 1:
                        finish_tile(qt - 1)
                    if qt >= 2 and isinstance(j, int) and j == 0:
                        choose(qt - 2)
                    if qt >= 2 and isinstance(j, int) and j == 2:
                        next(parts)
                    if qt == TILES - 1 and j == FREE + 1:
                        choose(TILES - 2)
                    if qt == TILES - 1 and j == FREE + 2:
                        parts6 = assign(TILES - 2)
                        next(parts6)
                    norm_ctx(nth(qt, 2 * j), 0, qt * PAIRS + j)
                    copy_pT(qt, nth(qt, 2 * j + 1), 1)
                    if qt >= 2 and isinstance(j, int) and j == 1:
                        read_place(qt - 2)
                    if qt and isinstance(j, int) and j == route_at(qt):
                        read_logits(qt - 1)
                    if qt == TILES - 1 and j == FREE + 1:
                        read_place(TILES - 2)
                    if qt == TILES - 1 and j == FREE + 2:
                        next(parts6)
                    if ahead(qt, j, 1):
                        tile, head, n = ahead(qt, j, 1)
                        row_max(tile, n, 1)
                    if qt and isinstance(j, int) and j == 0:
                        add_residual(qt - 1)
                    if qt >= 2 and isinstance(j, int) and j == 2:
                        next(parts)
                pairs_of(dve, pair, qt)
            norm_ctx(nth(TILES, -1), 1)
            add_residual(TILES - 1)
            finish_tile(TILES - 1)
            read_logits(TILES - 1)
            choose(TILES - 1)
            read_place(TILES - 1)
            for part in assign(TILES - 1):
                pass
            link = chain(dve, route_step, 13 * TILES)
            shape = [P, TILES, TOP0]
            dve.tensor_tensor(weight[:], top_v, top_v[:, :, 0:1].broadcast_to(shape), ALU.subtract).then_inc(exp0, 1)
            dve.wait_ge(exp0, 2)
            link(dve.tensor_reduce(wsum[:], weight[:], AX.X, ALU.add))
            link(dve.reciprocal(wsum[:], wsum[:]))
            link(dve.tensor_tensor(weight[:], weight[:], wsum[:].unsqueeze(2).broadcast_to(shape), ALU.mult))
            dve.tensor_tensor(weight[:], weight[:], valid[:], ALU.mult).then_inc(weight_done, 1)

            def copy_xeT(e, u):
                dve.wait_ge(xeT_ps, e + 1)
                if past(e, 2):
                    dve.wait_ge(gu_ready, e - 1)
                dve.tensor_copy(xeT[:, u % 2], pT[u % 2][:, 0:HID].rearrange("p (c n) -> p c n", c=HC)).then_inc(xeT_done, 1)

            def gated(e, u):
                dve.wait_ge(silu_done, e + 1)
                if past(e, 2):
                    dve.wait_ge(ye_ps, e - 1)
                dve.tensor_tensor(hT[:, u % 2, :], sg[:, u % 2, :], half[u % 2][0:I0, P:2 * P], ALU.mult).then_inc(h_done, 1)

            copy_xeT(0, 0)
            copy_xeT(1, 1)
            gated(0, 0)
            for e in range(RING):
                copy_xeT(e + 2, (e + 2) % RING)
                gated(e + 1, (e + 1) % RING)
            with dve.Fori(1, E0 // RING - 1) as i:
                for u in range(RING):
                    copy_xeT(RING * i + u + 2, (u + 2) % RING)
                    gated(RING * i + u + 1, (u + 1) % RING)
            for e in range(E0 - RING, E0):
                if e + 2 < E0:
                    copy_xeT(e + 2, (e + 2) % RING)
                if e + 1 < E0:
                    gated(e + 1, (e + 1) % RING)
            def combine(t, u):
                if past(t, 1):
                    dve.wait_ge(x2_done, t)
                for k in range(TOP0):
                    if k % (TOP0 // 2) == 0:
                        dve.wait_ge(gath[u][2 * k // TOP0], 4 * TOP0 * (t - u) + 8 * TOP0)
                    g, w = gathered[:, u, k, :], weight_flat[:, bass.ds(t * TOP0 + k, 1)]
                    total = (y_even, y_odd)[k % 2]
                    if k >= 2:
                        dve.wait_ge(comb_step, TOP0 * t + k - 1)
                    if k == 1:
                        ins = dve.tensor_scalar(total, g, w, None, ALU.mult)
                    else:
                        ins = dve.scalar_tensor_tensor(total, g, w, total if k else x1_flat[:, bass.ds(t * HID, HID)],
                                                       ALU.mult, ALU.add)
                    ins.then_inc(comb_step, 1)
                dve.wait_ge(comb_step, TOP0 * (t + 1))
                dve.tensor_tensor(y_even, y_even, y_odd, ALU.add).then_inc(combined, 1)
                dve.wait_ge(combined, t + 1)
                variance(rank2(t), y_even, LN_EPS)
                if past(t, 2):
                    dve.wait_ge(x2T_done, 2 * t - 2)
                normalise(rank2(t), y_even, x2[:, u, :]).then_inc(x2_done, 1)

            def middle(t, u):
                link = chain(dve, mid_step, 3 * t)
                dve.wait_ge(gates_done, 4 * t + 3)
                link(dve.scalar_tensor_tensor(value[:, u], igate[:, u], 1.0, value[:, u], ALU.add, ALU.mult))
                for c in range(HC):
                    init = init2[:, c:c + 1] if isinstance(t, int) and t == 0 else state[:, 1 - u, c, P - 1:P]
                    link(dve.tensor_tensor_scan(state[:, u, c, :], forget[:, u, c, :], value[:, u, c, :], init,
                                                ALU.mult, ALU.add))
                q = rec_ps[u][1][:, HC * P:].rearrange("p (c n) -> p c n", c=HC)
                dve.tensor_tensor(zq[:, u], state[:, u], q, ALU.mult).then_inc(z_done, 1)
                dve.wait_ge(gates_done, 4 * t + 4)
                if past(t, 2):
                    dve.wait_ge(mix_ready, t - 1)
                up = rec_ps[u][2][:, 0:HC * P].rearrange("p (c n) -> p c n", c=HC)
                dve.tensor_tensor(local[:, u], lgate[:, u], up, ALU.mult).then_inc(lu_done, 1)

            def add_mix(t, u):
                dve.wait_ge(mix_ready, t + 1)
                dve.wait_ge(x2T_done, 2 * t + 2)
                if past(t, 1):
                    dve.wait_ge(x3_done, t)
                dve.tensor_tensor(y[:], acc[:, 0:HID], x1_flat[:, bass.ds(t * HID, HID)], ALU.add).then_inc(mix_read, 1)
                dve.wait_ge(mix_read, t + 1)
                variance(rank3(t), y[:], LN_EPS, 1)

            def finish_mix(t, u):
                normalise(rank3(t), y[:], x1_flat[:, bass.ds(t * HID, HID)], 1).then_inc(x3_done, 1)

            weight_flat = weight[:].rearrange("p t k -> p (t k)")
            dve.wait_ge(ld_router1, 32)
            dve.tensor_scalar(init2[:], init2[:], 2.0, None, ALU.mult).then_inc(dve_step, 1)
            dve.wait_ge(weight_done, 1)
            dve.wait_ge(dve_step, 4)
            combine(0, 0)

            def step(t, u):
                if before(t, TILES - 1):
                    combine(t + 1, 1 - u)
                if past(t, 1):
                    add_mix(t - 1, 1 - u)
                middle(t, u)
                if past(t, 1):
                    finish_mix(t - 1, 1 - u)
            steps_two(dve, step)
            add_mix(TILES - 1, 1)
            finish_mix(TILES - 1, 1)
            for b in range(2):
                dve.wait_ge(x3T_ps, b + 3)
                dve.tensor_copy(x3T[:, 1, b * BANK:(b + 1) * BANK], half[2 + b]).then_inc(x3T_done, 1)

            def split_weights(n):
                k = n % SC
                dve.wait_ge(shw_half, 2 * n + 2)
                for m, w in enumerate((sh_g, sh_u)):
                    ins = dve.tensor_tensor(shw_lo[:, n % 2, m], w[:, :, k * P:(k + 1) * P],
                                            shw_hi[:, n % 2, m].bitcast(f32), ALU.subtract)
                ins.then_inc(shw_split, 1)

            def split_x3(b):
                for c in range(HC):
                    part = slice(b * BANK, (b + 1) * BANK)
                    dve.wait_ge(x3T_half, HC * b + c + 1)
                    dve.tensor_tensor(x3T_lo[:, c, part], x3T[:, c, part], x3T_hi[:, c, part].bitcast(f32),
                                      ALU.subtract).then_inc(x3T_split, 1)

            def shared_gated(b, c):
                n = b * SC + c
                dve.wait_ge(gs_silu, n + 1)
                dve.tensor_tensor(hs[:, c, :], sgd[:, n % 2, :], half[2 + n % 2], ALU.mult).then_inc(hs_done, 1)

            dve.wait_ge(ld_sh, 48)
            dve.wait_ge(x3T_done, 4)
            split_weights(0)
            split_x3(0)
            split_weights(1)

            link = chain(dve, d_step)
            dve.wait_ge(lg1_ready, 1)
            dve.wait_ge(consts1, 4)
            link(dve.tensor_copy(lg1[:], misc[:, 0:TILES * E1].rearrange("p (t e) -> p t e", t=TILES)))
            for t in range(TILES):
                ins = dve.max(tv1[:, t, :], lg1[:, t, :])
            link(ins)
            for t in range(TILES):
                ins = dve.max_index(ti1[:, t, :], tv1[:, t, :], lg1[:, t, :])
            link(ins)
            dve.tensor_tensor(weight1[:, :, 0:1], tv1[:, :, 1:2], tv1[:, :, 0:1], ALU.subtract).then_inc(tanh1, 1)
            link(dve.tensor_copy(tf1[:], ti1[:]))
            sh4 = [P, TILES, E1]
            for k in range(TOP1):
                link(dve.tensor_tensor(oh1[:, :, k, :], iota_e[:, 0:E1].unsqueeze(1).broadcast_to(sh4),
                                       tf1[:, :, k:k + 1].broadcast_to(sh4), ALU.is_equal))
            link(dve.tensor_tensor(ch1[:], oh1[:, :, 0, :], oh1[:, :, 1, :], ALU.add))
            for t in range(TILES):
                link(dve.tensor_tensor(cb1[:, t + 1, :], cb1[:, t, :], ch1[:, t, :], ALU.add))
            dve.sem_inc(ch1_done, 1)
            for c in range(2):
                shared_gated(0, c)
                split_weights(c + 2)
            dve.wait_ge(pl1_ready, 1)
            link(dve.tensor_copy(pl1[:], acc[:, 0:(TILES + 1) * E1].rearrange("p (t e) -> p t e", e=E1)))
            sh5 = [P, E1, TILES]
            link(dve.tensor_tensor(blk_cmp[:], pl1[:, TILES, :].unsqueeze(2).broadcast_to(sh5),
                                   iota_r[:].unsqueeze(1).broadcast_to(sh5), ALU.is_gt))
            link(dve.tensor_reduce(nblk[:], blk_cmp[:], AX.X, ALU.add))
            link(dve.tensor_tensor_scan(blk_end[:], ones_e[:], nblk[:], 0.0, ALU.mult, ALU.add))
            link(dve.tensor_tensor(blk_start[:], blk_end[:], nblk[:], ALU.subtract))
            link(dve.tensor_scalar(blk_start[:], blk_start[:], float(P), None, ALU.mult))
            link(dve.tensor_tensor(pl1[:, 0:TILES, :], pl1[:, 0:TILES, :],
                                   blk_start[:].unsqueeze(1).broadcast_to(sh4), ALU.add))
            for k in range(TOP1):
                link(dve.tensor_tensor(oh1[:, :, k, :], oh1[:, :, k, :], pl1[:, 0:TILES, :], ALU.mult))
            link(dve.tensor_reduce(sl1[:], oh1[:], AX.X, ALU.add))
            dve.tensor_copy(slot1[:], sl1[:]).then_inc(slots1_ready, 1)
            sh6 = [P, BLOCKS, E1]
            link(dve.tensor_tensor(own_cmp[:], blk_end[:].unsqueeze(1).broadcast_to(sh6),
                                   iota_b[:].unsqueeze(2).broadcast_to(sh6), ALU.is_le))
            link(dve.tensor_reduce(owner[:], own_cmp[:], AX.X, ALU.add))
            dve.tensor_scalar(owner_i[:], owner[:], float(E1 - 1), None, ALU.min).then_inc(slots1_ready, 1)
            dve.wait_ge(tanh1, 2)
            link(dve.tensor_scalar(weight1[:, :, 0:1], weight1[:, :, 1:2], -0.5, 0.5, ALU.mult, ALU.add))
            link(dve.tensor_scalar(weight1[:, :, 1:2], weight1[:, :, 1:2], 0.5, 0.5, ALU.mult, ALU.add))

            def add_shared(t):
                dve.wait_ge(sh_ready, t + 1)
                dve.tensor_tensor(shared[:, t, :], pT[t % 2][:, 0:HID], x1[:, t, :], ALU.add).then_inc(sh_read, 1)

            split_x3(1)
            for c in range(2, SC):
                shared_gated(0, c)
                split_weights(c + 2)
            for t in range(TILES // 2):
                add_shared(t)

            def block_gated(i, u):
                dve.wait_ge(sgd_done, i + 1)
                if past(i, 1):
                    dve.wait_ge(hdT_ps, i)
                dve.tensor_tensor(hd, sgd[:, u, :], half[2 * u + 1], ALU.mult).then_inc(hd_done, 1)

            def block_hT(i, u):
                dve.wait_ge(hdT_ps, i + 1)
                if past(i, 2):
                    dve.wait_ge(yd_ps, i - 1)
                dve.tensor_copy(hdT[:, u, :], pT[u][:]).then_inc(hdT_done, 1)

            def block_dve(i, u):
                block_gated(i, u)
                block_hT(i, u)

            def last_sum(t):
                u = t % 2
                link = chain(dve, final_step, t)
                dve.wait_ge(last_in[t], 16 * TOP1)
                dve.wait_ge(sh_read, t + 1)
                link(dve.scalar_tensor_tensor(result[:, t, :], last_rows[:, t, 0, :], weight1[:, t, 0:1],
                                              shared[:, t, :], ALU.mult, ALU.add))
                dve.scalar_tensor_tensor(result[:, t, :], last_rows[:, t, 1, :], weight1[:, t, 1:2], result[:, t, :],
                                         ALU.mult, ALU.add).then_inc(last_go, 1)
                dve.wait_ge(last_go, t + 1)
                variance(3 * TILES + t, result[:, t, :], LN_EPS, u)

            def last_norm(t):
                u = t % 2
                normalise(3 * TILES + t, result[:, t, :], result[:, t, :], u).then_inc(result_done, 1)

            blocks_two(dve, block_dve)
            dve.wait_ge(yd_ps, BLOCKS)
            for c in range(SC):
                if c == SC - 1:
                    for u in range(2):
                        dve.wait_ge(st_yd[u], 16 * (BLOCKS // 2 + (1 - u) * (BLOCKS % 2)))
                shared_gated(1, c)
                if c + 2 < SC:
                    split_weights(SC + c + 2)
                if c == SC - 3:
                    last_sum(0)
                if c == SC - 2:
                    last_sum(1)
                    last_norm(0)
            for t in range(2, TILES):
                if t + 1 in range(TILES // 2, TILES):
                    add_shared(t + 1)
                last_sum(t)
                last_norm(t - 1)
            last_norm(TILES - 1)

        @block.tensor
        def _(pe):
            def product3(out_ap, lhs, rhs, start, stop):
                (lh, ll), (rh, rl) = lhs, rhs
                pe.matmul(out_ap, lh, rh, start=start, stop=False)
                pe.matmul(out_ap, lh, rl, start=False, stop=False)
                return pe.matmul(out_ap, ll, rh, start=False, stop=stop)

            pe.wait_ge(ld_xT, 16)
            pe.wait_ge(ld_kv, 16)
            for t in range(TILES):
                for c in range(HC):
                    last = pe.matmul(banks[1][:, t * P:(t + 1) * P], xT_in[:, c, t * P:(t + 1) * P], wkv_a[:, c, :],
                                     start=c == 0, stop=c == HC - 1)
            last.then_inc(kv_ready, 1)

            def absorb(h, u, i):
                pe.wait_ge(ld_head[u], 16 + 64 * (i + 1))
                if not (isinstance(h, int) and h < 2):
                    pe.wait_ge(weff_f32, h - 1)
                for c in range(HC):
                    last = pe.matmul(pT[u][:, c * RANK:(c + 1) * RANK], wq_h[:, u, c * P:(c + 1) * P],
                                     wkb[:, bass.ds(h, 1), :], start=True, stop=True)
                last.then_inc(weff_ps, 1)
                if u == 0 and not (isinstance(i, int) and i < 1):
                    pe.wait_ge(wvo_done, i)
                pe.matmul(misc[u * RANK:(u + 1) * RANK, 0:HID], wv_h[:, u, :], wo_h[:, u, :],
                          start=True, stop=True).then_inc(wvo_ps, 1)

            def project_q(h, u):
                pe.wait_ge(weff_split, h + 1)
                if not (isinstance(h, int) and h < 2):
                    pe.wait_ge(qT_done, h - 1)
                for b in range(2):
                    for c in range(HC):
                        last = product3(banks[u][:, b * BANK:(b + 1) * BANK],
                                        (weff_hi[:, u, c, :], weff_lo[:, u, c, :]),
                                        (xT_hi[:, c, b * BANK:(b + 1) * BANK], xT_lo[:, c, b * BANK:(b + 1) * BANK]),
                                        c == 0, c == HC - 1)
                last.then_inc(qT_ps, 1)

            absorb(0, 0, 0)
            absorb(1, 1, 0)
            pe.wait_ge(x_split, 2)
            project_q(0, 0)
            pe.wait_ge(consts, 1)
            pe.wait_ge(keys_done, TILES + 1)
            for t in range(TILES):
                last = pe.transpose(banks[1][:, t * P:(t + 1) * P], keys[:, t, :], ident[:])
            last.then_inc(kT_ps, 1)
            pe.wait_ge(k_split, 2)
            with pe.Fori(1, PAIRS) as j:
                absorb(2 * j, 0, j)
                project_q(2 * j - 1, 1)
                absorb(2 * j + 1, 1, j)
                project_q(2 * j, 0)
            project_q(HEADS - 1, 1)
            pe.wait_ge(weff_f32, HEADS)
            pe.wait_ge(wvo_done, PAIRS)

            def scores(qt, n, u):
                pe.wait_ge(q_split, n + 1)
                if not (isinstance(n, int) and n < 2):
                    pe.wait_ge(probs_ready, n - 1)
                L = (qt + 1) * P
                for b in range(0, L, BANK):
                    w = min(BANK, L - b)
                    diag = b + w == L
                    last = product3(banks[u][:, b:b + w], (q_hi[:, u, :], q_lo[:, u, :]),
                                    (kT_hi[:, b:b + w], kT_lo[:, b:b + w]), True, not diag)
                    if diag:
                        last = pe.matmul(banks[u][:, L - P:L], ident_bf[:], causal[:], start=False, stop=True)
                last.then_inc(scores_ready, 1)

            def transpose_probs(qt, n, u, m=None):
                pe.wait_ge(probs_ready, n + 1)
                for c in range(chunks(qt)):
                    if m is not None and c == 1:
                        pe.wait_ge(ctxT_done, m)
                    bank = pT[u if chunks(qt) == 1 else c]
                    for k in range(4 * c, min(qt + 1, 4 * c + 4)):
                        last = pe.transpose(bank[:, (k % 4) * P:(k % 4 + 1) * P], probs[:, u, k * P:(k + 1) * P],
                                            ident[:])
                    last.then_inc(pT_ps[c], 1)

            def context(qt, n, u, between=None):
                pe.wait_ge(pT_done[0], n + 1)
                if between:
                    if chunks(qt) == 2:
                        pe.wait_ge(pT_done[1], n + 1 - 4 * HEADS)
                    between()
                if past(n, 1):
                    pe.wait_ge(ctx_normed, n)
                for k in range(qt + 1):
                    if k == 4:
                        pe.wait_ge(pT_done[1], n + 1 - 4 * HEADS)
                    last = pe.matmul(ctx_ps, probsT[:, u, k * P:(k + 1) * P], latent[:, k, :],
                                     start=k == 0, stop=k == qt)
                last.then_inc(ctx_ready, 1)

            def transpose_ctx(qt, m):
                pe.wait_ge(ctx_normed, 2 * m + 2)
                pe.transpose(ctxT_ps(qt), ctx_n[:], ident[:]).then_inc(ctxT_psd, 1)

            def output(m, j):
                pe.wait_ge(ctxT_done, m + 1)
                pe.matmul(acc[:, 0:HID], ctxT[:], wvo[:, bass.ds(j * HID, HID)], start=isinstance(j, int) and j == 0,
                          stop=isinstance(j, int) and j == PAIRS - 1).then_inc(acc_ready, 1)

            def transpose_x1(t):
                pe.wait_ge(x1_done, t + 1)
                for c in range(HC):
                    last = pe.transpose(x1T_ps[:, c * P:(c + 1) * P], x1[:, t, c * P:(c + 1) * P], ident[:])
                last.then_inc(x1T_psd, 1)

            def route(t):
                pe.wait_ge(ld_router0, 16)
                pe.wait_ge(x1T_done, t + 1)
                for c in range(HC):
                    last = pe.matmul(logits_ps, x1T[:, c, :], router0[:, c, :], start=c == 0, stop=c == HC - 1)
                last.then_inc(logits_done, 1)

            def count_places(t):
                pe.wait_ge(chosen_done, t + 1)
                pe.matmul(place_ps, ones_bf[:], chosen_before[:, t, :], start=True, stop=False)
                pe.matmul(place_ps, earlier[:], chosen[:, t, :], start=False, stop=True).then_inc(place_done, 1)

            pe.wait_ge(qT_done, HEADS - 1)
            scores(0, 0, 0)
            pe.wait_ge(qT_done, HEADS)
            scores(0, 1, 1)
            for qt in range(TILES):
                def pair(j):
                    m = qt * PAIRS + j
                    transpose_probs(qt, nth(qt, 2 * j), 0)
                    if ahead(qt, j, 0):
                        tile, head, n = ahead(qt, j, 0)
                        scores(tile, n, 0)
                    context(qt, nth(qt, 2 * j), 0)
                    if past(m, 1):
                        transpose_ctx(qt, m - 1)
                        transpose_probs(qt, nth(qt, 2 * j + 1), 1, m)
                    else:
                        transpose_probs(qt, nth(qt, 2 * j + 1), 1)
                    if ahead(qt, j, 1):
                        tile, head, n = ahead(qt, j, 1)
                        scores(tile, n, 1)
                    if qt and isinstance(j, int) and j == 1:
                        pe.wait_ge(acc_read, qt)
                    if past(m, 1):
                        output(m - 1, (j - 1) % PAIRS if isinstance(j, int) else j - 1)
                    if qt >= 2 and isinstance(j, int) and j == 1:
                        context(qt, nth(qt, 2 * j + 1), 1, lambda: count_places(qt - 2))
                        pe.wait_ge(place_read, qt - 1)
                    elif qt and isinstance(j, int) and j == FREE - 1:
                        context(qt, nth(qt, 2 * j + 1), 1, lambda: transpose_x1(qt - 1))
                        pe.wait_ge(x1T_done, qt)
                    elif qt == TILES - 1 and j == FREE + 1:
                        context(qt, nth(qt, 2 * j + 1), 1, lambda: count_places(TILES - 2))
                        pe.wait_ge(place_read, TILES - 1)
                    elif qt and isinstance(j, int) and j == route_at(qt):
                        context(qt, nth(qt, 2 * j + 1), 1, lambda: route(qt - 1))
                        pe.wait_ge(logits_read, qt)
                    else:
                        context(qt, nth(qt, 2 * j + 1), 1)
                pairs_of(pe, pair, qt)
            transpose_ctx(TILES - 1, TILES * PAIRS - 1)
            output(TILES * PAIRS - 1, PAIRS - 1)
            pe.wait_ge(acc_read, TILES)
            pe.wait_ge(ctxT_done, TILES * PAIRS)
            transpose_x1(TILES - 1)
            route(TILES - 1)
            pe.wait_ge(logits_read, TILES)
            count_places(TILES - 1)

            def transpose_rows(e, u):
                pe.wait_ge(ld_xe[u // 2], turn(e, u))
                if past(e, 2):
                    pe.wait_ge(xeT_done, e - 1)
                for c in range(HC):
                    last = pe.transpose(pT[u % 2][:, c * P:(c + 1) * P], xe[:, u, c * P:(c + 1) * P], ident[:])
                last.then_inc(xeT_ps, 1)

            def gate_up(e, u):
                b = u % 2
                pe.wait_ge(xeT_done, e + 1)
                pe.wait_ge(ld_gu[u // 2], turn(e, u))
                if past(e, 2):
                    pe.wait_ge(h_done, e - 1)
                for part in range(2):
                    for c in range(HC):
                        last = pe.matmul(half[b][0:I0, part * P:(part + 1) * P],
                                         gu_w[:, u, c, part * I0:(part + 1) * I0], xeT[:, b, c, :],
                                         start=c == 0, stop=c == HC - 1)
                last.then_inc(gu_ready, 1)

            def down(e, u):
                b = u % 2
                pe.wait_ge(h_done, e + 1)
                pe.wait_ge(ld_dn[u // 2], turn(e, u))
                if past(e, 2):
                    pe.wait_ge(ye_done, e - 1)
                pe.matmul(half[2 + b][:, 0:HID], hT[:, b, :], dn_w[:, u, :], start=True, stop=True).then_inc(ye_ps, 1)

            transpose_rows(0, 0)
            transpose_rows(1, 1)
            gate_up(0, 0)
            for e in range(RING):
                transpose_rows(e + 2, (e + 2) % RING)
                gate_up(e + 1, (e + 1) % RING)
                down(e, e)
            with pe.Fori(1, E0 // RING - 1) as i:
                for u in range(RING):
                    transpose_rows(RING * i + u + 2, (u + 2) % RING)
                    gate_up(RING * i + u + 1, (u + 1) % RING)
                    down(RING * i + u, u)
            for e in range(E0 - RING, E0):
                if e + 2 < E0:
                    transpose_rows(e + 2, (e + 2) % RING)
                if e + 1 < E0:
                    gate_up(e + 1, (e + 1) % RING)
                down(e, e % RING)
            def transpose_x2(t, u):
                pe.wait_ge(x2_done, t + 1)
                for c in range(HC):
                    last = pe.transpose(misc[:, c * P:(c + 1) * P], x2[:, u, c * P:(c + 1) * P], ident[:])
                last.then_inc(x2T_psd, 1)

            def project(t, u, part):
                bank = rec_ps[u][part]
                for m in range(2):
                    for r in range(HC):
                        o = m * HC * P + r * P
                        for c in range(HC):
                            last = pe.matmul(bank[:, o:o + P], w_c[:, 2 * part + m, c, r * P:(r + 1) * P],
                                             x2T[:, u, c, :], start=c == 0, stop=c == HC - 1)
                last.then_inc((fi_ready, vq_ready, ug_ready)[part], 1)

            def mix(t, u):
                pe.wait_ge(r_done, t + 1)
                pe.wait_ge(lu_done, t + 1)
                if past(t, 1):
                    pe.wait_ge(mix_read, t)
                for m, src in enumerate((readout, local)):
                    for c in range(HC):
                        last = pe.matmul(acc[:, 0:HID], src[:, u, c, :], wo_c[:, m, c, :], start=m + c == 0,
                                         stop=m + c == HC)
                last.then_inc(mix_ready, 1)

            pe.wait_ge(ld_wc, 32)
            pe.wait_ge(ye_done, E0)
            def step(t, u):
                pe.wait_ge(x2T_done, 2 * t + 1)
                if past(t, 2):
                    pe.wait_ge(lu_done, t - 1)
                project(t, u, 0)
                if past(t, 1):
                    mix(t - 1, 1 - u)
                project(t, u, 1)
                if before(t, TILES - 1):
                    transpose_x2(t + 1, 1 - u)
                project(t, u, 2)

            transpose_x2(0, 0)
            steps_two(pe, step)
            mix(TILES - 1, 1)

            pe.wait_ge(x3_done, TILES)
            for c in range(HC):
                for t in range(TILES):
                    last = pe.transpose(half[2 * c + t // 4][:, t % 4 * P:(t % 4 + 1) * P],
                                        x1[:, t, c * P:(c + 1) * P], ident[:])
                    if t % 4 == 3:
                        last.then_inc(x3T_ps, 1)
            pe.wait_ge(x3T_done, 4)
            pe.wait_ge(ld_router1, 32)
            for t in range(TILES):
                for c in range(HC):
                    last = pe.matmul(misc[:, t * E1:(t + 1) * E1], x3T[:, c, t * P:(t + 1) * P], router1_s[:, c, :],
                                     start=c == 0, stop=c == HC - 1)
            last.then_inc(lg1_ready, 1)
            pe.wait_ge(ld_sh, 48)

            def shared_in(b, k):
                n = b * SC + k
                pe.wait_ge(shw_split, n + 1)
                if k == 0:
                    pe.wait_ge(x3T_split, HC * (b + 1))
                if n >= 2:
                    pe.wait_ge(hs_done, n - 1)
                block = slice(b * BANK, (b + 1) * BANK)
                for m, bank in enumerate((half[n % 2], half[2 + n % 2])):
                    for c in range(HC):
                        last = product3(bank, (shw_hi[:, n % 2, m, c, :], shw_lo[:, n % 2, m, c, :]),
                                        (x3T_hi[:, c, block], x3T_lo[:, c, block]), c == 0, c == HC - 1)
                last.then_inc(gs_ready, 1)

            def shared_out(b):
                pe.wait_ge(hs_done, (b + 1) * SC)
                for q in range(4):
                    if 4 * b + q >= 2:
                        pe.wait_ge(sh_read, 4 * b + q - 1)
                    for k in range(SC):
                        last = pe.matmul(pT[q % 2][:, 0:HID], hs[:, k, q * P:(q + 1) * P], sh_d[:, k, :],
                                         start=k == 0, stop=k == SC - 1)
                    last.then_inc(sh_ready, 1)

            shared_in(0, 0)
            shared_in(0, 1)
            pe.wait_ge(ch1_done, 1)
            n = TILES * E1
            pe.matmul(acc[:, 0:n], ones_bf[:], cb1[:, 0:TILES, :].rearrange("p t e -> p (t e)"), start=True, stop=False)
            pe.matmul(acc[:, 0:n], earlier[:], ch1[:].rearrange("p t e -> p (t e)"), start=False, stop=True)
            pe.matmul(acc[:, n:n + E1], ones_bf[:], cb1[:, TILES, :], start=True, stop=True).then_inc(pl1_ready, 1)
            for k in range(2, SC):
                shared_in(0, k)
            shared_out(0)

            def block_T(i, u):
                pe.wait_ge(ld_xd[u], 8 * (i - u) + 16)
                if past(i, 1):
                    pe.wait_ge(xdT_done, i)
                for c in range(HC):
                    last = pe.transpose(misc[:, c * P:(c + 1) * P], xd[:, u, c * P:(c + 1) * P], ident[:])
                last.then_inc(xdT_ps, 1)

            def owner_of(i):
                return pe.value_load(owner_i[0:1, bass.ds(i, 1)], min_val=0, max_val=E1 - 1)

            def block_in(i, u):
                pe.wait_ge(xdT_done, i + 1)
                if past(i, 2):
                    pe.wait_ge(hd_done, i - 1)
                pe.sem_inc(passed, 1)
                e = owner_of(i)
                for part in range(2):
                    for c in range(HC):
                        last = pe.matmul(half[2 * u + part], xdT[:, u, c, :],
                                         w1_s[:, bass.ds(e * (HC * 2 * I1) + (c * 2 * I1 + part * I1), I1)],
                                         start=c == 0, stop=c == HC - 1)
                last.then_inc(f1_ready, 1)

            def block_hT(i, u):
                pe.wait_ge(hd_done, i + 1)
                if past(i, 2):
                    pe.wait_ge(hdT_done, i - 1)
                for c in range(I1 // P):
                    last = pe.transpose(pT[u][:, c * P:(c + 1) * P], hd[:, c * P:(c + 1) * P], ident[:])
                last.then_inc(hdT_ps, 1)

            def block_out(i, u):
                pe.wait_ge(hdT_done, i + 1)
                if past(i, 1):
                    pe.wait_ge(yd_done, i)
                pe.sem_inc(passed, 1)
                e = owner_of(i)
                for c in range(I1 // P):
                    last = pe.matmul(acc[:, 0:HID], hdT[:, u, c * P:(c + 1) * P],
                                     w2_s[:, bass.ds(e * (I1 * HID // P) + c * HID, HID)],
                                     start=c == 0, stop=c == I1 // P - 1)
                last.then_inc(yd_ps, 1)

            def block_pe(i, u):
                if not (isinstance(i, int) and i >= BLOCKS - 2):
                    block_T(i + 2, u)
                block_hT(i, u)
                if not (isinstance(i, int) and i >= BLOCKS - 1):
                    block_in(i + 1, 1 - u)
                block_out(i, u)

            pe.wait_ge(slots1_ready, 2)
            pe.wait_ge(sh_read, TILES // 2)
            pe.wait_ge(ld_w1, 16 * E1)
            pe.wait_ge(ld_w2, 16 * E1)
            block_T(0, 0)
            block_in(0, 0)
            block_T(1, 1)
            block_pe(0, 0)
            block_pe(1, 1)
            with pe.Fori(1, BLOCKS // 2 - 1) as i:
                for u in range(2):
                    block_pe(2 * i + u, u)
            for i in range(BLOCKS - 3, BLOCKS):
                block_pe(i, i % 2)
            pe.wait_ge(hd_done, BLOCKS)
            for k in range(SC):
                shared_in(1, k)
            shared_out(1)


def kernel(**inputs):
    import numpy as np
    import concourse.bacc as bacc
    from concourse import mybir as mb
    from concourse.bass_utils import run_bass_kernel_spmd as run

    def arr(name):
        return np.asarray(inputs[name])

    wq = arr("L0_attn_q_proj_w")
    laid_out = {
        "x": arr("L0_attn_hidden_states").reshape(T, HID),
        "xT": arr("L0_attn_hidden_states").reshape(T, HID).T,
        "wq": wq,
        "wq_ropeT": wq.reshape(HEADS, QDIM, HID)[:, NOPE:].transpose(2, 0, 1).reshape(HID, HEADS * ROPE),
        "wkv_aT": arr("L0_attn_kv_a_proj_w").T,
        "kv_ln": arr("L0_attn_kv_a_ln_w"),
        "wkv_b": arr("L0_attn_kv_b_proj_w"),
        "woT": arr("L0_attn_o_proj_w").T,
        "router0T": arr("L0_ffn_router_weight").T,
        "gate_up0": arr("L0_ffn_gate_up_proj"),
        "down0": arr("L0_ffn_down_proj"),
        "w_in": np.stack([arr(f"L1_attn_w_{n}") for n in ("f", "i", "v", "q", "up", "gate")]),
        "init_state": arr("L1_attn_init_state").reshape(HC, P).T,
        "w_mix": np.stack([arr("L1_attn_w_ro"), arr("L1_attn_w_down")]),
        "router1": arr("L1_ffn_router_w"),
        "w1": arr("L1_ffn_w1"),
        "w2": arr("L1_ffn_w2"),
        "sh_gate": arr("L1_ffn_w_gate"),
        "sh_up": arr("L1_ffn_w_up"),
        "sh_down": arr("L1_ffn_w_down"),
    }
    nc = bacc.Bacc("TRN2", target_bir_lowering=False, num_devices=1)
    arrays, args = {}, {}
    for name, a in laid_out.items():
        a = np.ascontiguousarray(a)
        arrays[name] = a
        args[name] = nc.dram_tensor(name, a.shape, mb.dt.from_np(a.dtype), kind="ExternalInput").ap()
    out = nc.dram_tensor("result", (T, HID), mb.dt.float32, kind="ExternalOutput").ap()
    build(nc, out=out, **args)
    r = run(nc, [arrays], core_ids=[0])
    return r.results[0]["result"].reshape(1, T, HID)
```
